# Optimizing a Trainium2 kernel written in Bass

```python
import numpy as np
import jax
import jax.numpy as jnp

def _softmax(x, axis=-1):
    return jax.nn.softmax(x, axis=axis)

def _gelu(x):
    return jax.nn.gelu(x, approximate=True)

def _silu(x):
    return jax.nn.silu(x)

def _sigmoid(x):
    return jax.nn.sigmoid(x)

def _layernorm(x, axis=-1, eps=1e-05):
    m = jnp.mean(x, axis=axis, keepdims=True)
    v = jnp.var(x, axis=axis, keepdims=True)
    return (x - m) / jnp.sqrt(v + eps)

def _scatter_add(tgt, idx, src, axis=0):
    return tgt.at[idx].add(src)

def _segment_sum(src, seg, n):
    return jax.ops.segment_sum(src, seg, n)
kernel_name = 'mk_gnn_resnorm_d4_gnn_r32_3f2481'

def setup_inputs(seed: int=0):
    np.random.seed(seed)
    _w = jnp.asarray

    def _rec_inputs():
        import jax
        import jax.numpy as jnp
        _gk = jax.random.key(seed)
        x = -0.0009044 + 1 * jax.random.normal(jax.random.fold_in(_gk, 1), (3125, 16), jnp.float32)
        src = jax.random.randint(jax.random.fold_in(_gk, 2), (100000,), 0, 3125, jnp.int32)
        dst = jnp.minimum((3125 * jax.random.uniform(jax.random.fold_in(_gk, 3), (100000,)) ** 2.0).astype(jnp.int32), 99999)
        _o = jnp.argsort(dst, stable=True)
        src = src[_o]
        dst = dst[_o]
        edge_attr_3 = -1.09012e-05 + 0.99985 * jax.random.normal(jax.random.fold_in(_gk, 11), (100000, 3), jnp.float32)
        edge_attr_48 = -3.69585e-06 + 0.999911 * jax.random.normal(jax.random.fold_in(_gk, 12), (100000, 48), jnp.float32)
        edge_attr_8 = -0.00010739 + 0.99994 * jax.random.normal(jax.random.fold_in(_gk, 13), (100000, 8), jnp.float32)
        edge_type_8 = jax.random.randint(jax.random.fold_in(_gk, 15), (100000,), 0, 8, jnp.int32)
        edge_weight = jax.random.uniform(jax.random.fold_in(_gk, 16), (100000,), jnp.float32, 0.0, 1)
        return (x, src, dst, edge_attr_3, edge_attr_48, edge_attr_8, edge_type_8, edge_weight)
    x, src, dst, edge_attr_3, edge_attr_48, edge_attr_8, edge_type_8, edge_weight = _rec_inputs()

    def _L0_gnn_setup():
        import jax, jax.numpy as jnp
        import numpy as np
        N_NODES = 3125
        N_EDGES = 100000
        F_IN = 16
        F_HID = 32

        def _gcn_conv(x, row, col, edge_w, W, b, num_nodes):
            loop = jnp.arange(num_nodes)
            r = jnp.concatenate([row, loop])
            c = jnp.concatenate([col, loop])
            ew = jnp.concatenate([edge_w, jnp.ones((num_nodes,), dtype=edge_w.dtype)])
            deg = jax.ops.segment_sum(ew, c, num_segments=num_nodes)
            dis = jnp.where(deg > 0, jax.lax.rsqrt(deg), 0.0)
            norm = dis[r] * ew * dis[c]
            xw = x @ W.T
            msg = xw[r] * norm[:, None]
            out = jax.ops.segment_sum(msg, c, num_segments=num_nodes)
            return out + b
        key = jax.random.key(seed)
        ks = jax.random.split(key, 8)
        x = jax.random.normal(ks[0], (N_NODES, F_IN), dtype=jnp.float32)
        edge_index = jax.random.randint(ks[1], (2, N_EDGES), 0, N_NODES, dtype=jnp.int64)
        edge_w = jax.random.uniform(ks[2], (N_EDGES,), dtype=jnp.float32)
        W1 = jax.random.normal(ks[3], (F_HID, F_IN), dtype=jnp.float32) * 0.1
        b1 = jax.random.normal(ks[4], (F_HID,), dtype=jnp.float32) * 0.1
        W2 = jax.random.normal(ks[5], (F_IN, F_HID), dtype=jnp.float32) * 0.1
        b2 = jax.random.normal(ks[6], (F_IN,), dtype=jnp.float32) * 0.1
        return {'x': x, 'edge_index': edge_index, 'edge_w': edge_w, 'W1': W1, 'b1': b1, 'W2': W2, 'b2': b2, 'num_nodes': N_NODES}
    _L0_gnn_all = _L0_gnn_setup()
    _L0_gnn_in = {k: v for k, v in _L0_gnn_all.items() if k in ('W1', 'b1', 'W2', 'b2')}
    del _L0_gnn_all

    def _L1_gnn_setup():
        import jax, jax.numpy as jnp
        import numpy as np
        NUM_ENTITIES = 3125
        NUM_RELATIONS = 8
        NUM_CLASSES = 16
        HIDDEN = 16
        NUM_EDGES = 100000

        def rgcn_conv(x, src, dst, edge_type, W, root, bias):
            num_nodes = x.shape[0]
            x_src = x[src]
            msg = jnp.zeros((src.shape[0], W.shape[2]), x.dtype)
            for r in range(NUM_RELATIONS):
                msg = msg + jnp.where((edge_type == r)[:, None], x_src @ W[r], jnp.zeros((), x.dtype))
            cnt = jnp.zeros((num_nodes, NUM_RELATIONS), x.dtype).at[dst, edge_type].add(1.0)
            norm = 1.0 / jnp.maximum(cnt[dst, edge_type], 1.0)
            agg = jax.ops.segment_sum(msg * norm[:, None], dst, num_segments=num_nodes)
            return agg + x @ root + bias
        key = jax.random.key(seed)
        ks = jax.random.split(key, 9)
        s = 1.0 / np.sqrt(HIDDEN)
        edge_index = jax.random.randint(ks[0], (2, NUM_EDGES), 0, NUM_ENTITIES, dtype=jnp.int32)
        edge_type = jax.random.randint(ks[1], (NUM_EDGES,), 0, NUM_RELATIONS, dtype=jnp.int32)
        return {'embed': jax.random.normal(ks[2], (NUM_ENTITIES, HIDDEN), jnp.float32), 'W1': jax.random.normal(ks[3], (NUM_RELATIONS, HIDDEN, HIDDEN), jnp.float32) * s, 'root1': jax.random.normal(ks[4], (HIDDEN, HIDDEN), jnp.float32) * s, 'b1': jnp.zeros((HIDDEN,), jnp.float32), 'W2': jax.random.normal(ks[5], (NUM_RELATIONS, HIDDEN, NUM_CLASSES), jnp.float32) * s, 'root2': jax.random.normal(ks[6], (HIDDEN, NUM_CLASSES), jnp.float32) * s, 'b2': jnp.zeros((NUM_CLASSES,), jnp.float32), 'edge_index': edge_index, 'edge_type': edge_type}
    _L1_gnn_all = _L1_gnn_setup()
    _L1_gnn_in = {k: v for k, v in _L1_gnn_all.items() if k in ('W1', 'root1', 'b1', 'W2', 'root2', 'b2')}
    del _L1_gnn_all

    def _L2_gnn_setup():
        import jax, jax.numpy as jnp
        import numpy as np
        NS, NV = (16, 4)
        EPS = 1e-05
        N_NODES, N_EDGES = (1250, 12500)

        def _bn_scalar(x, g, b):
            m = x.mean(0)
            v = ((x - m) ** 2).mean(0)
            return (x - m) / jnp.sqrt(v + EPS) * g + b

        def _seg_mean(x, idx, n):
            s = jax.ops.segment_sum(x, idx, num_segments=n)
            c = jax.ops.segment_sum(jnp.ones((idx.shape[0],), x.dtype), idx, num_segments=n)
            return s / jnp.maximum(c, 1.0)[:, None]

        def _edge_weights(edge_attr, w1, b1, w2, b2):
            h = jax.nn.relu(edge_attr @ w1 + b1)
            return h @ w2 + b2

        def _forward(node_attr, edge_attr, edge_vec, fc0_w1, fc0_b1, fc0_w2, fc0_b2, fc1_w1, fc1_b1, fc1_w2, fc1_b2, bn0_gs, bn0_bs, bn0_gv, bn1_gs, bn1_bs, edge_index):
            N = node_attr.shape[0]
            E = edge_attr.shape[0]
            src, dst = (edge_index[0], edge_index[1])
            rhat = edge_vec / (jnp.linalg.norm(edge_vec, axis=-1, keepdims=True) + 1e-12)
            sh1 = rhat * float(np.sqrt(3.0))
            w = _edge_weights(edge_attr, fc0_w1, fc0_b1, fc0_w2, fc0_b2)
            wa = w[:, :NS * NS].reshape(E, NS, NS)
            wb = w[:, NS * NS:].reshape(E, NS, NV)
            x = node_attr[dst]
            inv = float(1.0 / np.sqrt(NS))
            msg_s = jnp.einsum('ei,eij->ej', x, wa) * inv
            msg_v = jnp.einsum('ei,eij,ec->ejc', x, wb, sh1) * inv
            msg = jnp.concatenate([msg_s, msg_v.reshape(E, NV * 3)], axis=-1)
            out = _seg_mean(msg, src, N)
            s0 = _bn_scalar(out[:, :NS], bn0_gs, bn0_bs)
            v0 = out[:, NS:].reshape(N, NV, 3)
            vn = jnp.sqrt((v0 ** 2).mean(axis=(0, 2)) + EPS)
            v0 = v0 / vn[None, :, None] * bn0_gv[None, :, None]
            w = _edge_weights(edge_attr, fc1_w1, fc1_b1, fc1_w2, fc1_b2)
            wa = w[:, :NS * NS].reshape(E, NS, NS)
            wb = w[:, NS * NS:].reshape(E, NV, NS)
            s = s0[dst]
            v = v0[dst]
            path_a = jnp.einsum('ei,eij->ej', s, wa)
            path_b = jnp.einsum('eic,ec,eij->ej', v, sh1, wb) * float(1.0 / np.sqrt(3.0))
            msg = (path_a + path_b) * float(1.0 / np.sqrt(NS + NV))
            node1 = _seg_mean(msg, src, N)
            return _bn_scalar(node1, bn1_gs, bn1_bs)
        key = jax.random.key(seed)
        ks = jax.random.split(key, 8)
        d = 3 * NS
        wn = NS * NS + NS * NV
        g = lambda k, shape, sc: jax.random.normal(k, shape, jnp.float32) * sc
        return {'node_attr': g(ks[0], (N_NODES, NS), 1.0), 'edge_attr': g(ks[1], (N_EDGES, d), 1.0), 'edge_vec': g(ks[2], (N_EDGES, 3), 1.0), 'fc0_w1': g(ks[3], (d, d), d ** (-0.5)), 'fc0_b1': jnp.zeros((d,), jnp.float32), 'fc0_w2': g(ks[4], (d, wn), d ** (-0.5)), 'fc0_b2': jnp.zeros((wn,), jnp.float32), 'fc1_w1': g(ks[5], (d, d), d ** (-0.5)), 'fc1_b1': jnp.zeros((d,), jnp.float32), 'fc1_w2': g(ks[6], (d, wn), d ** (-0.5)), 'fc1_b2': jnp.zeros((wn,), jnp.float32), 'bn0_gs': jnp.ones((NS,), jnp.float32), 'bn0_bs': jnp.zeros((NS,), jnp.float32), 'bn0_gv': jnp.ones((NV,), jnp.float32), 'bn1_gs': jnp.ones((NS,), jnp.float32), 'bn1_bs': jnp.zeros((NS,), jnp.float32), 'edge_index': jax.random.randint(ks[7], (2, N_EDGES), 0, N_NODES)}
    _L2_gnn_all = _L2_gnn_setup()
    _L2_gnn_in = {k: v for k, v in _L2_gnn_all.items() if k in ('fc0_w1', 'fc0_b1', 'fc0_w2', 'fc0_b2', 'fc1_w1', 'fc1_b1', 'fc1_w2', 'fc1_b2', 'bn0_gs', 'bn0_bs', 'bn0_gv', 'bn1_gs', 'bn1_bs')}
    del _L2_gnn_all

    def _L3_gnn_setup():
        import jax, jax.numpy as jnp
        import numpy as np
        N_NODES = 3125
        N_EDGES = 50000
        IN_DIM = 16
        OUT_DIM = 16
        EDGE_DIM = 8
        key = jax.random.key(seed)
        ks = jax.random.split(key, 7)
        x = jax.random.normal(ks[0], (N_NODES, IN_DIM), dtype=jnp.float32)
        edge_attr = jax.random.normal(ks[1], (N_EDGES, EDGE_DIM), dtype=jnp.float32)
        root_w = jax.random.normal(ks[2], (IN_DIM, OUT_DIM), dtype=jnp.float32) * 0.1
        root_b = jax.random.normal(ks[3], (OUT_DIM,), dtype=jnp.float32) * 0.1
        edge_w = jax.random.normal(ks[4], (EDGE_DIM, OUT_DIM * IN_DIM), dtype=jnp.float32) * 0.1
        edge_b = jax.random.normal(ks[5], (OUT_DIM * IN_DIM,), dtype=jnp.float32) * 0.1
        edge_index = jax.random.randint(ks[6], (2, N_EDGES), 0, N_NODES, dtype=jnp.int64)
        return {'x': x, 'edge_attr': edge_attr, 'root_w': root_w, 'root_b': root_b, 'edge_w': edge_w, 'edge_b': edge_b, 'edge_index': edge_index}
    _L3_gnn_all = _L3_gnn_setup()
    _L3_gnn_in = {k: v for k, v in _L3_gnn_all.items() if k in ('root_w', 'root_b', 'edge_w', 'edge_b')}
    del _L3_gnn_all
    return {'x': x, 'src': src, 'dst': dst, 'edge_attr_3': edge_attr_3, 'edge_attr_48': edge_attr_48, 'edge_attr_8': edge_attr_8, 'edge_type_8': edge_type_8, 'edge_weight': edge_weight, 'L0_gnn_W1': _L0_gnn_in['W1'], 'L0_gnn_b1': _L0_gnn_in['b1'], 'L0_gnn_W2': _L0_gnn_in['W2'], 'L0_gnn_b2': _L0_gnn_in['b2'], 'L1_gnn_W1': _L1_gnn_in['W1'], 'L1_gnn_root1': _L1_gnn_in['root1'], 'L1_gnn_b1': _L1_gnn_in['b1'], 'L1_gnn_W2': _L1_gnn_in['W2'], 'L1_gnn_root2': _L1_gnn_in['root2'], 'L1_gnn_b2': _L1_gnn_in['b2'], 'L2_gnn_fc0_w1': _L2_gnn_in['fc0_w1'], 'L2_gnn_fc0_b1': _L2_gnn_in['fc0_b1'], 'L2_gnn_fc0_w2': _L2_gnn_in['fc0_w2'], 'L2_gnn_fc0_b2': _L2_gnn_in['fc0_b2'], 'L2_gnn_fc1_w1': _L2_gnn_in['fc1_w1'], 'L2_gnn_fc1_b1': _L2_gnn_in['fc1_b1'], 'L2_gnn_fc1_w2': _L2_gnn_in['fc1_w2'], 'L2_gnn_fc1_b2': _L2_gnn_in['fc1_b2'], 'L2_gnn_bn0_gs': _L2_gnn_in['bn0_gs'], 'L2_gnn_bn0_bs': _L2_gnn_in['bn0_bs'], 'L2_gnn_bn0_gv': _L2_gnn_in['bn0_gv'], 'L2_gnn_bn1_gs': _L2_gnn_in['bn1_gs'], 'L2_gnn_bn1_bs': _L2_gnn_in['bn1_bs'], 'L3_gnn_root_w': _L3_gnn_in['root_w'], 'L3_gnn_root_b': _L3_gnn_in['root_b'], 'L3_gnn_edge_w': _L3_gnn_in['edge_w'], 'L3_gnn_edge_b': _L3_gnn_in['edge_b']}

def reference(x, src, dst, edge_attr_3, edge_attr_48, edge_attr_8, edge_type_8, edge_weight, L0_gnn_W1, L0_gnn_b1, L0_gnn_W2, L0_gnn_b2, L1_gnn_W1, L1_gnn_root1, L1_gnn_b1, L1_gnn_W2, L1_gnn_root2, L1_gnn_b2, L2_gnn_fc0_w1, L2_gnn_fc0_b1, L2_gnn_fc0_w2, L2_gnn_fc0_b2, L2_gnn_fc1_w1, L2_gnn_fc1_b1, L2_gnn_fc1_w2, L2_gnn_fc1_b2, L2_gnn_bn0_gs, L2_gnn_bn0_bs, L2_gnn_bn0_gv, L2_gnn_bn1_gs, L2_gnn_bn1_bs, L3_gnn_root_w, L3_gnn_root_b, L3_gnn_edge_w, L3_gnn_edge_b):
    import jax
    import jax.numpy as jnp

    def _L0_gnn_ref(x, edge_index, edge_w, W1, b1, W2, b2, num_nodes):
        import jax, jax.numpy as jnp
        import numpy as np
        N_NODES = 3125
        N_EDGES = 100000
        F_IN = 16
        F_HID = 32

        def _gcn_conv(x, row, col, edge_w, W, b, num_nodes):
            loop = jnp.arange(num_nodes)
            r = jnp.concatenate([row, loop])
            c = jnp.concatenate([col, loop])
            ew = jnp.concatenate([edge_w, jnp.ones((num_nodes,), dtype=edge_w.dtype)])
            deg = jax.ops.segment_sum(ew, c, num_segments=num_nodes)
            dis = jnp.where(deg > 0, jax.lax.rsqrt(deg), 0.0)
            norm = dis[r] * ew * dis[c]
            xw = x @ W.T
            msg = xw[r] * norm[:, None]
            out = jax.ops.segment_sum(msg, c, num_segments=num_nodes)
            return out + b
        row, col = (edge_index[0], edge_index[1])
        h = _gcn_conv(x, row, col, edge_w, W1, b1, num_nodes)
        h = jax.nn.relu(h)
        out = _gcn_conv(h, row, col, edge_w, W2, b2, num_nodes)
        return out

    def _L1_gnn_ref(embed, W1, root1, b1, W2, root2, b2, edge_index, edge_type):
        import jax, jax.numpy as jnp
        import numpy as np
        NUM_ENTITIES = 3125
        NUM_RELATIONS = 8
        NUM_CLASSES = 16
        HIDDEN = 16
        NUM_EDGES = 100000

        def rgcn_conv(x, src, dst, edge_type, W, root, bias):
            num_nodes = x.shape[0]
            x_src = x[src]
            msg = jnp.zeros((src.shape[0], W.shape[2]), x.dtype)
            for r in range(NUM_RELATIONS):
                msg = msg + jnp.where((edge_type == r)[:, None], x_src @ W[r], jnp.zeros((), x.dtype))
            cnt = jnp.zeros((num_nodes, NUM_RELATIONS), x.dtype).at[dst, edge_type].add(1.0)
            norm = 1.0 / jnp.maximum(cnt[dst, edge_type], 1.0)
            agg = jax.ops.segment_sum(msg * norm[:, None], dst, num_segments=num_nodes)
            return agg + x @ root + bias
        src, dst = (edge_index[0], edge_index[1])
        h = rgcn_conv(embed, src, dst, edge_type, W1, root1, b1)
        h = jax.nn.relu(h)
        h = rgcn_conv(h, src, dst, edge_type, W2, root2, b2)
        return jax.nn.log_softmax(h, axis=1)

    def _L2_gnn_ref(node_attr, edge_attr, edge_vec, fc0_w1, fc0_b1, fc0_w2, fc0_b2, fc1_w1, fc1_b1, fc1_w2, fc1_b2, bn0_gs, bn0_bs, bn0_gv, bn1_gs, bn1_bs, edge_index):
        import jax, jax.numpy as jnp
        import numpy as np
        NS, NV = (16, 4)
        EPS = 1e-05
        N_NODES, N_EDGES = (1250, 12500)

        def _bn_scalar(x, g, b):
            m = x.mean(0)
            v = ((x - m) ** 2).mean(0)
            return (x - m) / jnp.sqrt(v + EPS) * g + b

        def _seg_mean(x, idx, n):
            s = jax.ops.segment_sum(x, idx, num_segments=n)
            c = jax.ops.segment_sum(jnp.ones((idx.shape[0],), x.dtype), idx, num_segments=n)
            return s / jnp.maximum(c, 1.0)[:, None]

        def _edge_weights(edge_attr, w1, b1, w2, b2):
            h = jax.nn.relu(edge_attr @ w1 + b1)
            return h @ w2 + b2

        def _forward(node_attr, edge_attr, edge_vec, fc0_w1, fc0_b1, fc0_w2, fc0_b2, fc1_w1, fc1_b1, fc1_w2, fc1_b2, bn0_gs, bn0_bs, bn0_gv, bn1_gs, bn1_bs, edge_index):
            N = node_attr.shape[0]
            E = edge_attr.shape[0]
            src, dst = (edge_index[0], edge_index[1])
            rhat = edge_vec / (jnp.linalg.norm(edge_vec, axis=-1, keepdims=True) + 1e-12)
            sh1 = rhat * float(np.sqrt(3.0))
            w = _edge_weights(edge_attr, fc0_w1, fc0_b1, fc0_w2, fc0_b2)
            wa = w[:, :NS * NS].reshape(E, NS, NS)
            wb = w[:, NS * NS:].reshape(E, NS, NV)
            x = node_attr[dst]
            inv = float(1.0 / np.sqrt(NS))
            msg_s = jnp.einsum('ei,eij->ej', x, wa) * inv
            msg_v = jnp.einsum('ei,eij,ec->ejc', x, wb, sh1) * inv
            msg = jnp.concatenate([msg_s, msg_v.reshape(E, NV * 3)], axis=-1)
            out = _seg_mean(msg, src, N)
            s0 = _bn_scalar(out[:, :NS], bn0_gs, bn0_bs)
            v0 = out[:, NS:].reshape(N, NV, 3)
            vn = jnp.sqrt((v0 ** 2).mean(axis=(0, 2)) + EPS)
            v0 = v0 / vn[None, :, None] * bn0_gv[None, :, None]
            w = _edge_weights(edge_attr, fc1_w1, fc1_b1, fc1_w2, fc1_b2)
            wa = w[:, :NS * NS].reshape(E, NS, NS)
            wb = w[:, NS * NS:].reshape(E, NV, NS)
            s = s0[dst]
            v = v0[dst]
            path_a = jnp.einsum('ei,eij->ej', s, wa)
            path_b = jnp.einsum('eic,ec,eij->ej', v, sh1, wb) * float(1.0 / np.sqrt(3.0))
            msg = (path_a + path_b) * float(1.0 / np.sqrt(NS + NV))
            node1 = _seg_mean(msg, src, N)
            return _bn_scalar(node1, bn1_gs, bn1_bs)
        return _forward(node_attr, edge_attr, edge_vec, fc0_w1, fc0_b1, fc0_w2, fc0_b2, fc1_w1, fc1_b1, fc1_w2, fc1_b2, bn0_gs, bn0_bs, bn0_gv, bn1_gs, bn1_bs, edge_index)

    def _L3_gnn_ref(x, edge_attr, root_w, root_b, edge_w, edge_b, edge_index):
        import jax, jax.numpy as jnp
        import numpy as np
        N_NODES = 3125
        N_EDGES = 50000
        IN_DIM = 16
        OUT_DIM = 16
        EDGE_DIM = 8
        src = edge_index[0]
        dst = edge_index[1]
        weights = (edge_attr @ edge_w + edge_b).reshape(-1, OUT_DIM, IN_DIM)
        msg = jnp.einsum('eoi,ei->eo', weights, x[src])
        out = x @ root_w + root_b
        out = out.at[dst].add(msg)
        return out
    edge_index = jnp.stack([src, dst])
    x = _layernorm(x + _L0_gnn_ref(x, edge_index, edge_weight, L0_gnn_W1, L0_gnn_b1, L0_gnn_W2, L0_gnn_b2, 3125), axis=-1)
    x = _layernorm(x + _L1_gnn_ref(x, L1_gnn_W1, L1_gnn_root1, L1_gnn_b1, L1_gnn_W2, L1_gnn_root2, L1_gnn_b2, edge_index, edge_type_8), axis=-1)
    x = _layernorm(x + _L2_gnn_ref(x, edge_attr_48, edge_attr_3, L2_gnn_fc0_w1, L2_gnn_fc0_b1, L2_gnn_fc0_w2, L2_gnn_fc0_b2, L2_gnn_fc1_w1, L2_gnn_fc1_b1, L2_gnn_fc1_w2, L2_gnn_fc1_b2, L2_gnn_bn0_gs, L2_gnn_bn0_bs, L2_gnn_bn0_gv, L2_gnn_bn1_gs, L2_gnn_bn1_bs, edge_index), axis=-1)
    x = _layernorm(x + _L3_gnn_ref(x, edge_attr_8, L3_gnn_root_w, L3_gnn_root_b, L3_gnn_edge_w, L3_gnn_edge_b, edge_index), axis=-1)
    return x

_drawn_inputs = setup_inputs


def setup_inputs(seed=0):
    import zlib

    import numpy as np

    out = dict(_drawn_inputs(seed))
    spreads = {'L1_gnn_b1': (0.0, 0.1),
     'L1_gnn_b2': (0.0, 0.365),
     'L2_gnn_fc0_b1': (0.0, 0.1),
     'L2_gnn_fc0_b2': (0.0, 0.1),
     'L2_gnn_fc1_b1': (0.0, 0.1),
     'L2_gnn_fc1_b2': (0.0, 0.1),
     'L2_gnn_bn0_gs': (1.0, 0.2),
     'L2_gnn_bn0_bs': (0.0, 0.1),
     'L2_gnn_bn0_gv': (1.0, 0.6),
     'L2_gnn_bn1_gs': (1.0, 0.2),
     'L2_gnn_bn1_bs': (0.0, 0.1)}
    factors = {'edge_weight': 8.0, 'L0_gnn_W1': 5.97, 'L3_gnn_root_b': 3.428}
    for name, (base, spread) in spreads.items():
        noise = np.random.default_rng([zlib.crc32(name.encode()), seed]).standard_normal(out[name].shape)
        drawn = base * np.exp(spread * noise) if base else spread * noise
        out[name] = jnp.asarray(drawn.astype(out[name].dtype))
    for name, factor in factors.items():
        out[name] = (out[name] * factor).astype(out[name].dtype)
    return out
```

```python
from contextlib import ExitStack

import numpy as np

import concourse.bass as bass
from concourse import mybir

NODES, EDGES = 3125, 100000
P = 125
HI = NODES // P
TILES = EDGES // P
G = 8
GROUPS = TILES // G
STEPS = GROUPS // 2
F = 16
HID = 32
REL = 8
D48 = 48
ND8 = 8
NV = 4
MSG2 = F + 3 * NV
W2 = 320
REL_COLS = REL * F + F
EDGE_COLS = (ND8 + 1) * F + F
T3 = (ND8 + 1) * F
KB = 4
KGROUPS = [(q * KB, min(KB, HI - q * KB)) for q in range((HI + KB - 1) // KB)]

LO_D, HI_D, LO_S, HI_S, WEIGHT, NORM, RX, RY, RZ, HITYPE = range(10)
NM = 10
IX_SRC, IX_DST, IX_SRCREL, IX_DSTREL = range(4)

PASSES = [
    ("count", "count", None, 0, 0, None),
    ("norm", "norm", IX_DSTREL, 1, 0, None),
    ("gcn1", "scale", IX_SRC, F, F, "d"),
    ("gcn2", "scale", IX_SRC, F, F, "d"),
    ("rel1", "scale", IX_SRCREL, F, F, "d"),
    ("rel2", "scale", IX_SRCREL, F, F, "d"),
    ("ten1", "tensor1", IX_DST, F, MSG2, "s"),
    ("ten2", "tensor2", IX_DST, MSG2, F, "s"),
    ("edge", "edge", IX_SRC, T3, F, "d"),
]
FUNCS = ["rnorm", "dis", "ln0", "ln1_exp", "ln1_log", "ln1", "bn0", "bnv", "bn1", "ln2", "ln3"]
MIXES = ["rel1", "rel2", "edge"]
LN_EPS = 1e-5


def gnn_kernel(nc, x, src, dst, vec3, ea48t, ea8, etype, eweight, w1t, b1, w2t, b2, relw1, relb1, relw2, relb2,
               fc0w1, fc0b1, fc0w2, fc1w1, fc1b1, fc1w2, bn0gs, bn0bs, bn0gv, bn1gs, bn1bs, edgew, edgeb, out):
    f32, i32 = mybir.dt.float32, mybir.dt.int32
    ALU, ACT, X = mybir.AluOpType, mybir.ActivationFunctionType, mybir.AxisListType.X

    ctx = ExitStack()
    with ctx:
        def sb(name, shape, dt=f32):
            return ctx.enter_context(nc.sbuf_tensor(name, shape, dt))

        def sem(name):
            return ctx.enter_context(nc.semaphore(name))

        tab = {"gcn1": (NODES, F), "gcn2": (NODES, F), "norm": (NODES * REL, 1), "rel1": (NODES * REL, F),
               "rel2": (NODES * REL, F), "ten1": (NODES, F), "ten2": (NODES, MSG2), "edge": (NODES, T3)}
        tab = {k: nc.dram_tensor(f"table_{k}", s, f32, kind="Internal").ap() for k, s in tab.items()}

        meta = sb("meta", [P, TILES, NM])
        index = sb("index", [P, 4, TILES], i32)
        ring_meta = sb("ring_meta", [P, 2, G, NM])
        ring_index = sb("ring_index", [P, 2, G], i32)
        ring_ea8 = sb("ring_ea8", [P, 2, G, ND8])
        ring_ea48 = sb("ring_ea48", [D48, 2, G * P])
        gathered = sb("gathered", [P, 2, G, T3])
        onehot = sb("onehot", [P, 2, G, P])
        spread = sb("spread", [P, 2, G, HI * MSG2])
        hidden = sb("hidden", [64, 2, G * P])
        hot_hi = sb("hot_hi", [P, 2, G, HI])
        message = sb("message", [P, 2, G, MSG2])
        prod = sb("prod", [P, 2, G, W2])
        operand = sb("operand", [P, 2, G, F + NV])
        vprod = sb("vprod", [P, 2, G, 3 * NV])
        tsum = sb("tsum", [P, 2, G, F + NV])
        xs = sb("xs", [P, HI, F])
        ya = sb("ya", [P, HI, F])
        agg = sb("agg", [P, HI, F])
        acc = sb("acc", [P, HI, MSG2])
        t1 = sb("t1", [P, HI, MSG2])
        mixed = sb("mixed", [P, HI, EDGE_COLS])
        cols = sb("cols", [P, 8, HI])
        dis = sb("dis", [P, HI])
        inv_src = sb("inv_src", [P, HI])
        inv_rel = sb("inv_rel", [P, HI * REL])
        stat = sb("stat", [P, 8, MSG2])
        xt = sb("xt", [64, 2, P])
        ht = sb("ht", [128, 2, P])
        kw1 = sb("kw1", [KB * F, KB * HID])
        kw2 = sb("kw2", [KB * HID, KB * F])
        krel = [sb(f"krel{n}", [KB * F, KB * REL_COLS]) for n in range(2)]
        kedge = sb("kedge", [KB * F, KB * EDGE_COLS])
        wfc1 = [sb(f"wfc1_{n}", [D48, D48]) for n in range(2)]
        bfc1 = [sb(f"bfc1_{n}", [D48, 1]) for n in range(2)]
        wfc2 = [sb(f"wfc2_{n}", [D48 + 1, W2]) for n in range(2)]
        b1col = sb("b1col", [KB * HID, 1])
        ident = sb("ident", [P, P])
        ones = sb("ones", [P, P])
        zeros = sb("zeros", [P, 512])
        iota_i = sb("iota_i", [P, 512], i32)
        iota = sb("iota", [P, 512])
        brow = {n: sb(f"row_{n}", [P, w]) for n, w in
                [("b2", F), ("relb1", F), ("relb2", F), ("edgeb", F), ("bn0gs", F), ("bn0bs", F), ("bn0gv", NV),
                 ("bn1gs", F), ("bn1bs", F)]}

        work = spread[:, :, :, :].rearrange("p s g c -> p (s g c)")
        wi = work.bitcast(i32)
        src_i, dst_i, type_i = (wi[:, n * TILES:(n + 1) * TILES] for n in range(3))
        f_a, f_b, f_c, f_d = (work[:, n * TILES:(n + 1) * TILES] for n in range(3, 7))
        i_a = wi[:, 7 * TILES:8 * TILES]
        v_in = work[:, 8 * TILES:11 * TILES].rearrange("p (t c) -> p t c", c=3)
        w_in = work[:, 11 * TILES:12 * TILES]

        ps_acc = ctx.enter_context(nc.psum_tensor("ps_acc", [128, 2, 512], f32))
        ps_w = ctx.enter_context(nc.psum_tensor("ps_w", [128, 2, 2, 512], f32))
        ps_h = ctx.enter_context(nc.psum_tensor("ps_h", [128, 2, 512], f32))

        loaded = sem("loaded")
        zeroed = sem("zeroed")
        iota_made = sem("iota_made")
        vchain = sem("vchain")
        node_ready = sem("node_ready")
        table_ready = sem("table_ready")
        table_stored = [sem(f"table_stored_{n}") for n in tab]
        func_asked = sem("func_asked")
        func_done = sem("func_done")
        sums_asked = sem("sums_asked")
        sums_done = sem("sums_done")
        mix_t = sem("mix_t")
        mix_ts = sem("mix_ts")
        mix_o = sem("mix_o")
        mix_os = sem("mix_os")
        gcn_h = sem("gcn_h")
        gcn_hs = sem("gcn_hs")
        acc_read = sem("acc_read")
        out_ready = sem("out_ready")
        gathers_begun = sem("gathers_begun")
        hidden_begun = sem("hidden_begun")
        out_stored = sem("out_stored")

        class PassSems:

            def __init__(self, name, kind):
                self.meta_in = [sem(f"{name}_meta_in{s}") for s in range(2)]
                if kind != "count":
                    self.index_in = [sem(f"{name}_index_in{s}") for s in range(2)]
                    self.index_used = sem(f"{name}_index_used")
                    self.gather_in = [sem(f"{name}_gather_in{s}") for s in range(2)]
                self.inputs_used = sem(f"{name}_inputs_used")
                if kind != "norm":
                    self.spread_ready = sem(f"{name}_spread_ready")
                    self.spread_used = sem(f"{name}_spread_used")
                    self.sums_ready = sem(f"{name}_sums_ready")
                if kind in ("tensor1", "tensor2"):
                    self.ea48_in = [sem(f"{name}_ea48_in{s}") for s in range(2)]
                    self.hidden_done = sem(f"{name}_hidden_done")
                    self.hidden_ready = sem(f"{name}_hidden_ready")
                    self.weights_ready = sem(f"{name}_weights_ready")
                    self.weights_used = sem(f"{name}_weights_used")

        sems = {name: PassSems(name, kind) for name, kind, *_ in PASSES}
        stored = dict(zip(tab, table_stored))
        N_LOADS = 3 + 2 + 1 + 2 * 3 + 1 + len(brow) + KB * 5
        N_TABLES = list(tab)
        TABLE_ORDER = ["norm", "gcn1", "gcn2", "rel1", "rel2", "ten1", "ten2", "edge"]

        block = ctx.enter_context(nc.Block())

        @block.sync
        def _(sp):
            def load(to, of):
                sp.dma_start(to, of).then_inc(loaded, 16)

            load(src_i, src)
            load(dst_i, dst)
            load(type_i, etype)
            load(v_in, vec3)
            load(w_in, eweight)
            load(xs[:, :, :], x)
            for n, (a, b, c) in enumerate(((fc0w1, fc0b1, fc0w2), (fc1w1, fc1b1, fc1w2))):
                load(wfc1[n][:, :], a)
                load(bfc1[n][:, :], b)
                load(wfc2[n][:, :], c)
            load(b1col[:, :], b1)
            for name, row in (("b2", b2), ("relb1", relb1), ("relb2", relb2), ("edgeb", edgeb), ("bn0gs", bn0gs),
                              ("bn0bs", bn0bs), ("bn0gv", bn0gv), ("bn1gs", bn1gs), ("bn1bs", bn1bs)):
                load(brow[name][:, :], row.partition_broadcast(P))
            sp.wait_ge(zeroed, 1)
            for k in range(KB):
                load(kw1[k * F:(k + 1) * F, k * HID:(k + 1) * HID], w1t)
                load(kw2[k * HID:(k + 1) * HID, k * F:(k + 1) * F], w2t)
                load(krel[0][k * F:(k + 1) * F, k * REL_COLS:(k + 1) * REL_COLS], relw1)
                load(krel[1][k * F:(k + 1) * F, k * REL_COLS:(k + 1) * REL_COLS], relw2)
                load(kedge[k * F:(k + 1) * F, k * EDGE_COLS:(k + 1) * EDGE_COLS], edgew)
                pass

            def store(name, of):
                sp.wait_ge(table_ready, TABLE_ORDER.index(name) + 1)
                sp.dma_start(tab[name].rearrange("(p h) c -> p h c", p=P), of).then_inc(stored[name], 16)

            for name, kind, ix, gcols, mcols, side in PASSES:
                q = sems[name]
                if name == "norm":
                    store("norm", inv_rel[:, :].unsqueeze(2))
                    store("gcn1", ya[:, :, :])
                elif name == "gcn2":
                    store("gcn2", ya[:, :, :])
                elif name in ("rel1", "rel2"):
                    sp.wait_ge(table_ready, TABLE_ORDER.index(name) + 1)
                    sp.dma_start(tab[name].rearrange("(p h r) c -> p h (r c)", p=P, r=REL),
                                 mixed[:, :, 0:REL * F]).then_inc(stored[name], 16)
                elif name == "ten1":
                    store("ten1", xs[:, :, :])
                elif name == "ten2":
                    store("ten2", acc[:, :, :])
                elif name == "edge":
                    store("edge", mixed[:, :, 0:T3])
                if name == "count":
                    sp.wait_ge(zeroed, 2)
                with sp.Fori(0, STEPS) as i:
                    for s in range(2):
                        sp.wait_ge(q.inputs_used, 2 * i + s + 1)
                        at = i * (2 * G) + s * G
                        if ix is not None:
                            sp.wait_ge(q.index_used, 2 * i + s + 1)
                            sp.dma_start(ring_index[:, s, :], index[:, ix, bass.ds(at, G)]).then_inc(q.index_in[s], 16)
                        if kind in ("tensor1", "tensor2"):
                            sp.wait_ge(q.hidden_done, 4 * i + 2 * s + 2)
                            sp.dma_start(ring_ea48[:, s, :], ea48t[:, bass.ds(at * P, G * P)]).then_inc(q.ea48_in[s], 16)
                        if kind == "edge":
                            sp.dma_start(ring_ea8[:, s, :, :], ea8[:, bass.ds(at, G), :]).then_inc(q.meta_in[s], 16)
                        sp.dma_start(ring_meta[:, s, :, :], meta[:, bass.ds(at, G), :]).then_inc(q.meta_in[s], 16)
                sp.wait_ge(q.inputs_used, GROUPS + 2)
                if ix is not None:
                    sp.wait_ge(q.index_used, GROUPS + 2)
            sp.wait_ge(out_ready, 1)
            sp.dma_start(out, xs[:, :, :]).then_inc(out_stored, 16)
            sp.wait_ge(out_stored, 16)

        @block.gpsimd
        def _(pool):
            nc.gpsimd.iota(iota_i[:, 0:256], [[1, 256]], base=0, channel_multiplier=0)
            nc.gpsimd.iota(iota_i[:, 256:257], [[1, 1]], base=0, channel_multiplier=1).then_inc(iota_made, 1)
            for name, kind, ix, gcols, mcols, side in PASSES:
                if ix is None:
                    continue
                q = sems[name]
                pool.wait_ge(stored[name], 16)
                pool.sem_inc(q.index_used, 2)
                with pool.Fori(0, STEPS) as i:
                    for s in range(2):
                        pool.wait_ge(q.index_in[s], 16 * (i + 1))
                        pool.sem_inc(gathers_begun, 1)
                        for j in range(G):
                            pool.indirect_dma_start(
                                gathered[:, s, j, 0:gcols], None, tab[name],
                                bass.IndirectOffsetOnAxis(ap=ring_index[:, s, j:j + 1], axis=0),
                                engine_sem=q.index_used if j == G - 1 else None,
                            ).then_inc(q.gather_in[s], 16)

        @block.scalar
        def _(act):
            def func(name, to, of, fn, **kw):
                n = FUNCS.index(name)
                act.wait_ge(func_asked, n + 1)
                nc.scalar.activation(to, of, fn, **kw).then_inc(func_done, 1)

            def mix(name, width):
                base = len(KGROUPS) * (1 + MIXES.index(name))
                for n, (h0, hn) in enumerate(KGROUPS):
                    act.wait_ge(mix_t, base + n + 1)
                    nc.scalar.copy(xt[0:hn * F, n % 2, :], ps_h[0:hn * F, n % 2, 0:P]).then_inc(mix_ts, 1)
                    act.wait_ge(mix_o, base + n + 1)
                    halves = 2 if hn == KB else 1
                    per = hn // halves
                    for u in range(halves):
                        last = nc.scalar.copy(mixed[:, h0 + u * per:h0 + (u + 1) * per, 0:width],
                                              ps_w[0:P, n % 2, u, 0:per * width].rearrange("p (h c) -> p h c", c=width))
                    last.then_inc(mix_os, 1)

            func("rnorm", f_b, f_a, ACT.Sqrt)
            func("dis", cols[:, 2, :], cols[:, 1, :], ACT.Sqrt)
            q = sems["norm"]
            act.sem_inc(q.inputs_used, 2)
            with act.Fori(0, STEPS) as i:
                for s in range(2):
                    act.wait_ge(q.gather_in[s], 16 * G * (i + 1))
                    act.wait_ge(q.meta_in[s], 16 * (i + 1))
                    nc.scalar.copy(meta[:, bass.ds(i * (2 * G) + s * G, G), NORM:NORM + 1],
                                   gathered[:, s, :, 0:1]).then_inc(q.inputs_used, 1)
            for n, (h0, hn) in enumerate(KGROUPS):
                act.wait_ge(mix_t, n + 1)
                nc.scalar.copy(xt[0:hn * F, n % 2, :], ps_h[0:hn * F, n % 2, 0:P]).then_inc(mix_ts, 1)
                act.wait_ge(gcn_h, n + 1)
                nc.scalar.activation(ht[0:hn * HID, n % 2, :], ps_w[0:hn * HID, n % 2, 0, 0:P], ACT.Relu,
                                     bias=b1col[0:hn * HID, 0:1]).then_inc(gcn_hs, 1)
                act.wait_ge(mix_o, n + 1)
                nc.scalar.copy(t1[:, h0:h0 + hn, 0:F],
                               ps_w[0:P, n % 2, 1, 0:hn * F].rearrange("p (h c) -> p h c", c=F)).then_inc(mix_os, 1)
            func("ln0", cols[:, 2, :], cols[:, 1, :], ACT.Sqrt)
            mix("rel1", REL_COLS)
            mix("rel2", REL_COLS)
            func("ln1_exp", t1[:, :, 0:F], acc[:, :, 0:F], ACT.Exp)
            func("ln1_log", cols[:, 2, :], cols[:, 1, :], ACT.Ln)
            func("ln1", cols[:, 2, :], cols[:, 1, :], ACT.Sqrt)
            for n, name in enumerate(("ten1", "ten2")):
                q = sems[name]
                with act.Fori(0, STEPS) as i:
                    for s in range(2):
                        for k in range(2):
                            act.wait_ge(q.hidden_done, 4 * i + 2 * s + k + 1 + 4)
                            nc.scalar.activation(hidden[0:D48, s, k * 4 * P:(k + 1) * 4 * P], ps_h[0:D48, k, 0:4 * P],
                                                 ACT.Relu, bias=bfc1[n][:, 0:1]).then_inc(q.hidden_ready, 1)
                if n == 0:
                    func("bn0", stat[:, 3, 0:F], stat[:, 2, 0:F], ACT.Sqrt)
                    func("bnv", stat[:, 3, 0:NV], stat[:, 2, 0:NV], ACT.Sqrt)
            func("bn1", stat[:, 3, 0:F], stat[:, 2, 0:F], ACT.Sqrt)
            func("ln2", cols[:, 2, :], cols[:, 1, :], ACT.Sqrt)
            mix("edge", EDGE_COLS)
            func("ln3", cols[:, 2, :], cols[:, 1, :], ACT.Sqrt)

        @block.tensor
        def _(pe):
            def scatter_part(q, s, half, per, banks, first):
                for j in range(half * (G // 2), (half + 1) * (G // 2)):
                    for b in range(banks):
                        last = nc.tensor.matmul(ps_acc[0:P, b, 0:per], onehot[:, s, j, :],
                                                spread[:, s, j, b * per:(b + 1) * per],
                                                start=False, stop=False, skip_group_check=True)
                return last

            def open_sums(per, banks):
                for b in range(banks):
                    last = nc.tensor.matmul(ps_acc[0:P, b, 0:per], zeros[:, 0:P], zeros[:, 0:per],
                                            start=True, stop=False, skip_group_check=True)
                return last

            def close_sums(per, banks):
                for b in range(banks):
                    last = nc.tensor.matmul(ps_acc[0:P, b, 0:per], zeros[:, 0:P], zeros[:, 0:per],
                                            start=False, stop=True, skip_group_check=True)
                return last

            def mix(name, weights, width):
                base = len(KGROUPS) * (1 + MIXES.index(name))
                source = {"rel1": xs, "rel2": ya, "edge": xs}[name]
                pe.wait_ge(node_ready, 2 + MIXES.index(name))
                for n, (h0, hn) in enumerate(KGROUPS):
                    nc.tensor.transpose(ps_h[0:hn * F, n % 2, 0:P], source[:, h0:h0 + hn, :].rearrange("p h c -> p (h c)"),
                                        ident[:, :]).then_inc(mix_t, 1)
                    pe.wait_ge(mix_ts, base + n + 1)
                    if n >= 2:
                        pe.wait_ge(mix_os, base + n - 1)
                    halves = 2 if hn == KB else 1
                    per = hn // halves * width
                    for u in range(halves):
                        last = nc.tensor.matmul(ps_w[0:P, n % 2, u, 0:per], xt[0:hn * F, n % 2, :],
                                                weights[0:hn * F, u * per:(u + 1) * per], start=True, stop=True)
                    last.then_inc(mix_o, 1)

            def sum_over_partitions(n, width):
                pe.wait_ge(sums_asked, n + 1)
                nc.tensor.matmul(ps_h[0:P, 0, 0:width], ones[:, :], stat[:, 0, 0:width],
                                 start=True, stop=True).then_inc(sums_done, 1)

            pe.wait_ge(zeroed, 1)
            passes = 0
            for name, kind, ix, gcols, mcols, side in PASSES:
                q = sems[name]
                if kind == "norm":
                    continue
                if passes:
                    pe.wait_ge(acc_read, passes)
                passes += 1
                banks = 2 if kind == "tensor1" else 1
                per = {"count": REL * HI + HI, "tensor1": HI * MSG2 // 2}.get(kind, HI * F)
                if name == "rel1":
                    mix("rel1", krel[0], REL_COLS)
                if name == "rel2":
                    mix("rel2", krel[1], REL_COLS)
                if name == "edge":
                    mix("edge", kedge, EDGE_COLS)
                if kind == "count":
                    open_sums(per, 1)
                    nc.tensor.matmul(ps_acc[0:P, 1, 0:HI], zeros[:, 0:P], zeros[:, 0:HI], start=True, stop=False,
                                     skip_group_check=True).then_inc(q.spread_used, 2)
                    with pe.Fori(0, STEPS) as i:
                        for s in range(2):
                            pe.wait_ge(q.spread_ready, 2 * i + s + 1)
                            for j in range(G):
                                nc.tensor.matmul(ps_acc[0:P, 0, 0:per], onehot[:, s, j, :], spread[:, s, j, 0:per],
                                                 start=False, stop=False, skip_group_check=True)
                                last = nc.tensor.matmul(ps_acc[0:P, 1, 0:HI], spread[:, s, j, 256:256 + P],
                                                        spread[:, s, j, 400:400 + HI],
                                                        start=False, stop=False, skip_group_check=True)
                            last.then_inc(q.spread_used, 1)
                    close_sums(per, 1)
                    nc.tensor.matmul(ps_acc[0:P, 1, 0:HI], zeros[:, 0:P], zeros[:, 0:HI], start=False, stop=True,
                                     skip_group_check=True).then_inc(q.sums_ready, 1)
                elif kind in ("scale", "edge"):
                    open_sums(per, 1).then_inc(q.spread_used, 2)
                    with pe.Fori(0, STEPS) as i:
                        for s in range(2):
                            for half in range(2):
                                pe.wait_ge(q.spread_ready, 4 * i + 2 * s + half + 1)
                                last = scatter_part(q, s, half, per, 1, False)
                            last.then_inc(q.spread_used, 1)
                    close_sums(per, 1).then_inc(q.sums_ready, 1)
                else:
                    n = 0 if kind == "tensor1" else 1

                    def hidden_part(i, s):
                        pe.wait_ge(q.ea48_in[s], 16 * (i + 1))
                        for k in range(2):
                            pe.wait_ge(q.hidden_ready, 4 * i + 2 * s + k + 1)
                            pe.sem_inc(hidden_begun, 1)
                            nc.tensor.matmul(ps_h[0:D48, k, 0:4 * P], wfc1[n][:, :],
                                             ring_ea48[:, s, k * 4 * P:(k + 1) * 4 * P],
                                             start=True, stop=True).then_inc(q.hidden_done, 1)

                    def weights_part(i, s, k):
                        pe.wait_ge(q.hidden_ready, 4 * i + 2 * s + k + 1 + 2)
                        for u in range(2):
                            pe.wait_ge(q.weights_used, 8 * i + 4 * s + 2 * k + u + 1)
                            for v in range(2):
                                j = 4 * k + 2 * u + v
                                last = nc.tensor.matmul(ps_w[0:P, u, v, 0:W2], hidden[0:D48 + 1, s, j * P:(j + 1) * P],
                                                        wfc2[n][:, :], start=True, stop=True)
                            last.then_inc(q.weights_ready, 1)

                    def sums_part(i, s, half):
                        pe.wait_ge(q.spread_ready, 4 * i + 2 * s + half + 1)
                        return scatter_part(q, s, half, per, banks, False)

                    pe.sem_inc(q.hidden_done, 4)
                    open_sums(per, banks).then_inc(q.spread_used, 2)
                    hidden_part(0, 0)
                    weights_part(0, 0, 0)
                    weights_part(0, 0, 1)
                    with pe.Fori(0, STEPS - 1) as i:
                        for s in range(2):
                            nxt = (i, 1) if s == 0 else (i + 1, 0)
                            hidden_part(*nxt)
                            sums_part(i, s, 0)
                            weights_part(*nxt, 0)
                            sums_part(i, s, 1).then_inc(q.spread_used, 1)
                            weights_part(*nxt, 1)
                    i = STEPS - 1
                    hidden_part(i, 1)
                    sums_part(i, 0, 0)
                    weights_part(i, 1, 0)
                    sums_part(i, 0, 1).then_inc(q.spread_used, 1)
                    weights_part(i, 1, 1)
                    sums_part(i, 1, 0)
                    sums_part(i, 1, 1).then_inc(q.spread_used, 1)
                    close_sums(per, banks).then_inc(q.sums_ready, 1)
                if name == "gcn1":
                    pe.wait_ge(node_ready, 1)
                    for n, (h0, hn) in enumerate(KGROUPS):
                        nc.tensor.transpose(ps_h[0:hn * F, n % 2, 0:P], 
                                            agg[:, h0:h0 + hn, :].rearrange("p h c -> p (h c)"),
                                            ident[:, :]).then_inc(mix_t, 1)
                        pe.wait_ge(mix_ts, n + 1)
                        if n >= 2:
                            pe.wait_ge(mix_os, n - 1)
                        nc.tensor.matmul(ps_w[0:hn * HID, n % 2, 0, 0:P], kw1[0:hn * F, 0:hn * HID],
                                         xt[0:hn * F, n % 2, :], start=True, stop=True).then_inc(gcn_h, 1)
                        pe.wait_ge(gcn_hs, n + 1)
                        nc.tensor.matmul(ps_w[0:P, n % 2, 1, 0:hn * F], ht[0:hn * HID, n % 2, :],
                                         kw2[0:hn * HID, 0:hn * F], start=True, stop=True).then_inc(mix_o, 1)
                if name == "ten1":
                    for n in range(3):
                        sum_over_partitions(n, (F, F, NV)[n])
                if name == "ten2":
                    for n in range(2):
                        sum_over_partitions(3 + n, F)

        @block.vector
        def _(dve):
            V = nc.vector
            n_chain = [0, 0]
            loop = [None, 0]

            def link(ins):
                n_chain[0] += 1
                ins.then_inc(vchain, 1)
                if loop[0] is None:
                    dve.wait_ge(vchain, n_chain[0])
                else:
                    dve.wait_ge(vchain, loop[0] * loop[1] + n_chain[0])

            def bc(ap, shape):
                return ap.broadcast_to(shape)

            def rows(name, width=F):
                return bc(brow[name][:, :].unsqueeze(1), [P, HI, width])

            def func(name):
                dve.sem_inc(func_asked, 1)
                dve.wait_ge(func_done, FUNCS.index(name) + 1)

            def tt(o, a, b, op):
                link(V.tensor_tensor(o, a, b, op))

            def ts(o, a, c1, c2, op0, op1=None):
                if op1 is None:
                    link(V.tensor_scalar(o, a, c1, None, op0))
                else:
                    link(V.tensor_scalar(o, a, c1, c2, op0, op1))

            def red(o, a, op=ALU.add):
                link(V.tensor_reduce(o, a, X, op))

            def colb(c, width=F):
                return bc(c.unsqueeze(2), [P, HI, width])

            def layer_norm(name, r):
                red(cols[:, 0, :], r)
                ts(cols[:, 0, :], cols[:, 0, :], 1.0 / F, None, ALU.mult)
                tt(r, r, colb(cols[:, 0, :]), ALU.subtract)
                tt(xs[:, :, :], r, r, ALU.mult)
                red(cols[:, 1, :], xs[:, :, :])
                ts(cols[:, 1, :], cols[:, 1, :], 1.0 / F, LN_EPS, ALU.mult, ALU.add)
                func(name)
                link(V.reciprocal(cols[:, 3, :], cols[:, 2, :]))
                tt(xs[:, :, :], r, colb(cols[:, 3, :]), ALU.mult)

            n_sums = [0]

            def total(to, of):
                w = of.shape[2]
                red(stat[:, 0, 0:w], of.rearrange("p h c -> p c h"))
                dve.sem_inc(sums_asked, 1)
                n_sums[0] += 1
                dve.wait_ge(sums_done, n_sums[0])
                link(V.tensor_copy(to, ps_h[0:P, 0, 0:w]))

            def batch_norm(name, r, scale, shift):
                sq = t1[:, :, 0:F]
                total(stat[:, 1, 0:F], r)
                ts(stat[:, 1, 0:F], stat[:, 1, 0:F], 1.0 / NODES, None, ALU.mult)
                tt(r, r, bc(stat[:, 1, 0:F].unsqueeze(1), [P, HI, F]), ALU.subtract)
                tt(sq, r, r, ALU.mult)
                total(stat[:, 2, 0:F], sq)
                ts(stat[:, 2, 0:F], stat[:, 2, 0:F], 1.0 / NODES, LN_EPS, ALU.mult, ALU.add)
                func(name)
                link(V.reciprocal(stat[:, 4, 0:F], stat[:, 3, 0:F]))
                tt(stat[:, 4, 0:F], stat[:, 4, 0:F], brow[scale][:, :], ALU.mult)
                tt(r, r, bc(stat[:, 4, 0:F].unsqueeze(1), [P, HI, F]), ALU.mult)
                tt(r, r, rows(shift), ALU.add)

            for t in (kw1, kw2, krel[0], krel[1], kedge):
                V.memset(t[:, :], 0.0)
            V.memset(zeros[:, :], 0.0)
            V.memset(ones[:, :], 1.0)
            link(V.memset(hidden[:, :, :], 1.0))
            dve.sem_inc(zeroed, 1)
            dve.wait_ge(iota_made, 1)
            link(V.tensor_copy(iota[:, 0:257], iota_i[:, 0:257]))
            row_id = iota[:, 256:257]
            ts(ident[:, :], iota[:, 0:P], row_id, None, ALU.is_equal)
            dve.wait_ge(loaded, 16 * N_LOADS)

            def split(raw, lo, hi):
                link(V.tensor_copy(f_a, raw))
                ts(i_a, f_a, 1.0 / HI, None, ALU.mult)
                link(V.tensor_copy(f_b, i_a))
                link(V.scalar_tensor_tensor(f_c, f_b, -float(HI), f_a, ALU.mult, ALU.add))
                ts(f_d, f_c, 0.0, None, ALU.is_lt)
                tt(f_b, f_b, f_d, ALU.subtract)
                link(V.scalar_tensor_tensor(f_c, f_d, float(HI), f_c, ALU.mult, ALU.add))
                ts(f_d, f_c, float(HI), None, ALU.is_ge)
                tt(meta[:, :, lo], f_b, f_d, ALU.add)
                link(V.scalar_tensor_tensor(meta[:, :, hi], f_d, -float(HI), f_c, ALU.mult, ALU.add))

            split(src_i, LO_S, HI_S)
            link(V.tensor_copy(index[:, IX_SRC, :], src_i))
            link(V.tensor_copy(f_b, type_i))
            link(V.scalar_tensor_tensor(index[:, IX_SRCREL, :], f_a, float(REL), f_b, ALU.mult, ALU.add))
            split(dst_i, LO_D, HI_D)
            link(V.tensor_copy(index[:, IX_DST, :], dst_i))
            link(V.tensor_copy(f_b, type_i))
            link(V.scalar_tensor_tensor(index[:, IX_DSTREL, :], f_a, float(REL), f_b, ALU.mult, ALU.add))
            link(V.scalar_tensor_tensor(meta[:, :, HITYPE], meta[:, :, HI_D], float(REL), f_b, ALU.mult, ALU.add))
            link(V.tensor_copy(meta[:, :, WEIGHT], w_in))
            link(V.memset(meta[:, :, NORM], 0.0))
            tt(meta[:, :, RX:RZ + 1], v_in, v_in, ALU.mult)
            red(f_a, meta[:, :, RX:RZ + 1])
            func("rnorm")
            ts(f_b, f_b, 1e-12, None, ALU.add)
            link(V.reciprocal(f_c, f_b))
            tt(meta[:, :, RX:RZ + 1], v_in, bc(f_c.unsqueeze(2), [P, TILES, 3]), ALU.mult)
            dve.sem_inc(zeroed, 1)

            def hot(o, m, width):
                n = o.shape[1]
                return V.tensor_tensor(o, bc(iota[:, 0:width].unsqueeze(1), [P, n, width]),
                                       bc(m.unsqueeze(2), [P, n, width]), ALU.is_equal)

            LINKS = {"count": 2 * 4, "scale": 2 * 2, "edge": 2 * 4, "tensor1": 2 * 3, "tensor2": 2 * 4}
            passes = 0
            for name, kind, ix, gcols, mcols, side in PASSES:
                q = sems[name]
                if kind == "norm":
                    continue
                dve.sem_inc(q.inputs_used, 2)
                if kind in ("tensor1", "tensor2"):
                    dve.sem_inc(q.weights_used, 2)
                    dve.sem_inc(q.hidden_ready, 2)
                start = n_chain[0]
                with dve.Fori(0, STEPS) as i:
                    loop[0], loop[1] = i, LINKS[kind]
                    for s in range(2):
                        m = ring_meta[:, s, :, :]
                        dve.wait_ge(q.meta_in[s], (32 if kind == "edge" else 16) * (i + 1))
                        dve.wait_ge(q.spread_used, 2 * i + s + 1)
                        lo, hi = (LO_S, HI_S) if side == "s" else (LO_D, HI_D)
                        if kind == "count":
                            hot(onehot[:, s, :, :], m[:, :, LO_D], P)
                            hot(spread[:, s, :, 0:REL * HI], m[:, :, HITYPE], REL * HI)
                            link(hot(spread[:, s, :, 256:256 + P], m[:, :, LO_S], P))
                            link(hot(spread[:, s, :, 400:400 + HI], m[:, :, HI_S], HI))
                            link(hot(hot_hi[:, s, :, :], m[:, :, HI_D], HI))
                            link(V.tensor_tensor(spread[:, s, :, REL * HI:REL * HI + HI], hot_hi[:, s, :, :],
                                                 bc(m[:, :, WEIGHT:WEIGHT + 1], [P, G, HI]), ALU.mult))
                            dve.sem_inc(q.spread_ready, 1)
                            dve.sem_inc(q.inputs_used, 1)
                            continue
                        hot(onehot[:, s, :, :], m[:, :, lo], P)
                        link(hot(hot_hi[:, s, :, :], m[:, :, hi], HI))
                        dve.wait_ge(q.gather_in[s], 16 * G * (i + 1))
                        g = gathered[:, s, :, 0:gcols]
                        if kind == "scale":
                            by = WEIGHT if name in ("gcn1", "gcn2") else NORM
                            link(V.tensor_tensor(message[:, s, :, 0:F], g, bc(m[:, :, by:by + 1], [P, G, F]), ALU.mult))
                            dve.sem_inc(q.inputs_used, 1)
                        elif kind == "edge":
                            pr = prod[:, s, :, 0:ND8 * F].rearrange("p g (k o) -> p g k o", o=F)
                            tt(pr, g[:, :, 0:ND8 * F].rearrange("p g (k o) -> p g k o", o=F),
                               bc(ring_ea8[:, s, :, :].unsqueeze(3), [P, G, ND8, F]), ALU.mult)
                            red(tsum[:, s, :, 0:F], pr.rearrange("p g k o -> p g o k"))
                            tt(message[:, s, :, 0:F], tsum[:, s, :, 0:F], g[:, :, ND8 * F:T3], ALU.add)
                            dve.sem_inc(q.inputs_used, 1)
                        else:
                            if kind == "tensor1":
                                op = g
                                nj, ni = F + NV, F
                            else:
                                nj, ni = F, F + NV
                                V.tensor_copy(operand[:, s, :, 0:F], g[:, :, 0:F])
                                tt(vprod[:, s, :, :].rearrange("p g (j c) -> p g j c", c=3),
                                   g[:, :, F:MSG2].rearrange("p g (j c) -> p g j c", c=3),
                                   bc(m[:, :, RX:RZ + 1].unsqueeze(2), [P, G, NV, 3]), ALU.mult)
                                red(operand[:, s, :, F:F + NV], vprod[:, s, :, :].rearrange("p g (j c) -> p g j c", c=3))
                                op = operand[:, s, :, :]
                            for u in range(4):
                                dve.wait_ge(q.weights_ready, 8 * i + 4 * s + u + 1)
                                V.tensor_tensor(
                                    prod[:, s, 2 * u:2 * u + 2, :].rearrange("p g (j i) -> p g j i", i=ni),
                                    ps_w[0:P, u % 2, :, 0:W2].rearrange("p g (j i) -> p g j i", i=ni),
                                    bc(op[:, 2 * u:2 * u + 2, :].unsqueeze(2), [P, 2, nj, ni]),
                                    ALU.mult).then_inc(q.weights_used, 1)
                            dve.wait_ge(q.weights_used, 8 * i + 4 * s + 4 + 2)
                            to = tsum if kind == "tensor1" else message
                            red(to[:, s, :, 0:nj], prod[:, s, :, :].rearrange("p g (j i) -> p g j i", i=ni))
                            if kind == "tensor1":
                                V.tensor_copy(message[:, s, :, 0:F], tsum[:, s, :, 0:F])
                                tt(message[:, s, :, F:MSG2].rearrange("p g (j c) -> p g j c", c=3),
                                   bc(tsum[:, s, :, F:F + NV].unsqueeze(3), [P, G, NV, 3]),
                                   bc(m[:, :, RX:RZ + 1].unsqueeze(2), [P, G, NV, 3]), ALU.mult)
                            dve.sem_inc(q.inputs_used, 1)
                        banks = 2 if kind == "tensor1" else 1
                        w = mcols // banks
                        for half in range(2):
                            t = slice(half * G // 2, (half + 1) * G // 2)
                            for b in range(banks):
                                last = V.tensor_tensor(
                                    spread[:, s, t, b * HI * w:(b + 1) * HI * w].rearrange("p g (h c) -> p g h c", c=w),
                                    bc(hot_hi[:, s, t, :].unsqueeze(3), [P, G // 2, HI, w]),
                                    bc(message[:, s, t, b * w:(b + 1) * w].unsqueeze(2), [P, G // 2, HI, w]), ALU.mult)
                            last.then_inc(q.spread_ready, 1)
                    per_turn = n_chain[0] - start
                assert per_turn == LINKS[kind], (kind, per_turn)
                n_chain[0] = start + per_turn * STEPS
                loop[0] = None
                dve.wait_ge(q.sums_ready, 1)
                if kind == "count":
                    link(V.tensor_copy(inv_rel[:, :], ps_acc[0:P, 0, 0:REL * HI]))
                    ts(cols[:, 0, :], ps_acc[0:P, 0, REL * HI:REL * HI + HI], 1.0, None, ALU.add)
                    ts(inv_src[:, :], ps_acc[0:P, 1, 0:HI], 1.0, None, ALU.max)
                    dve.sem_inc(acc_read, 1)
                    ts(inv_rel[:, :], inv_rel[:, :], 1.0, None, ALU.max)
                    link(V.reciprocal(inv_rel[:, :], inv_rel[:, :]))
                    dve.sem_inc(table_ready, 1)
                    link(V.reciprocal(inv_src[:, :], inv_src[:, :]))
                    ts(cols[:, 3, :], cols[:, 0, :], 0.0, None, ALU.is_gt)
                    ts(cols[:, 1, :], cols[:, 0, :], 1e-37, None, ALU.max)
                    func("dis")
                    link(V.reciprocal(dis[:, :], cols[:, 2, :]))
                    tt(dis[:, :], dis[:, :], cols[:, 3, :], ALU.mult)
                    tt(ya[:, :, :], xs[:, :, :], colb(dis[:, :]), ALU.mult)
                    dve.sem_inc(table_ready, 1)
                    continue
                a = acc[:, :, 0:F]
                sums = ps_acc[0:P, 0, 0:HI * F].rearrange("p (h c) -> p h c", c=F)
                if name in ("gcn1", "gcn2"):
                    tt(a, sums, ya[:, :, :], ALU.add)
                    dve.sem_inc(acc_read, 1)
                    if name == "gcn1":
                        tt(agg[:, :, :], a, colb(dis[:, :]), ALU.mult)
                        dve.sem_inc(node_ready, 1)
                        dve.wait_ge(mix_os, len(KGROUPS))
                        tt(ya[:, :, :], t1[:, :, 0:F], colb(dis[:, :]), ALU.mult)
                        dve.sem_inc(table_ready, 1)
                    else:
                        tt(a, a, colb(dis[:, :]), ALU.mult)
                        tt(a, a, rows("b2"), ALU.add)
                        tt(a, a, xs[:, :, :], ALU.add)
                        layer_norm("ln0", a)
                        dve.sem_inc(node_ready, 1)
                        dve.wait_ge(mix_os, 2 * len(KGROUPS))
                        dve.sem_inc(table_ready, 1)
                elif name in ("rel1", "rel2"):
                    tt(a, sums, mixed[:, :, REL * F:REL_COLS], ALU.add)
                    dve.sem_inc(acc_read, 1)
                    tt(a, a, rows("relb1" if name == "rel1" else "relb2"), ALU.add)
                    if name == "rel1":
                        ts(ya[:, :, :], a, 0.0, None, ALU.max)
                        dve.sem_inc(node_ready, 1)
                        dve.wait_ge(mix_os, 3 * len(KGROUPS))
                        dve.sem_inc(table_ready, 1)
                    else:
                        red(cols[:, 0, :], a, ALU.max)
                        tt(a, a, colb(cols[:, 0, :]), ALU.subtract)
                        func("ln1_exp")
                        red(cols[:, 1, :], t1[:, :, 0:F])
                        func("ln1_log")
                        tt(a, a, colb(cols[:, 2, :]), ALU.subtract)
                        tt(a, a, xs[:, :, :], ALU.add)
                        layer_norm("ln1", a)
                        dve.sem_inc(table_ready, 1)
                elif name == "ten1":
                    h = MSG2 // 2
                    for b in range(2):
                        link(V.tensor_tensor(acc[:, :, b * h:(b + 1) * h],
                                             ps_acc[0:P, b, 0:HI * h].rearrange("p (h c) -> p h c", c=h),
                                             colb(inv_src[:, :], h), ALU.mult))
                    dve.sem_inc(acc_read, 1)
                    ts(acc[:, :, 0:F], acc[:, :, 0:F], float(1.0 / np.sqrt(F)), None, ALU.mult)
                    ts(acc[:, :, F:MSG2], acc[:, :, F:MSG2], float(np.sqrt(3.0) / np.sqrt(F)), None, ALU.mult)
                    batch_norm("bn0", a, "bn0gs", "bn0bs")
                    v = acc[:, :, F:MSG2]
                    sq = t1[:, :, F:MSG2]
                    tt(sq, v, v, ALU.mult)
                    red(t1[:, :, 0:NV], sq.rearrange("p h (j c) -> p h j c", c=3))
                    total(stat[:, 2, 0:NV], t1[:, :, 0:NV])
                    ts(stat[:, 2, 0:NV], stat[:, 2, 0:NV], 1.0 / (3 * NODES), LN_EPS, ALU.mult, ALU.add)
                    func("bnv")
                    link(V.reciprocal(stat[:, 4, 0:NV], stat[:, 3, 0:NV]))
                    tt(stat[:, 4, 0:NV], stat[:, 4, 0:NV], brow["bn0gv"][:, :], ALU.mult)
                    link(V.tensor_copy(stat[:, 5, 0:3 * NV].rearrange("p (j c) -> p j c", c=3),
                                       bc(stat[:, 4, 0:NV].unsqueeze(2), [P, NV, 3])))
                    tt(v, v, bc(stat[:, 5, 0:3 * NV].unsqueeze(1), [P, HI, 3 * NV]), ALU.mult)
                    dve.sem_inc(table_ready, 1)
                elif name == "ten2":
                    tt(a, sums, colb(inv_src[:, :]), ALU.mult)
                    dve.sem_inc(acc_read, 1)
                    ts(a, a, float(1.0 / np.sqrt(F + NV)), None, ALU.mult)
                    batch_norm("bn1", a, "bn1gs", "bn1bs")
                    tt(a, a, xs[:, :, :], ALU.add)
                    layer_norm("ln2", a)
                    dve.sem_inc(node_ready, 1)
                    dve.wait_ge(mix_os, 4 * len(KGROUPS))
                    dve.sem_inc(table_ready, 1)
                else:
                    tt(a, sums, mixed[:, :, T3:EDGE_COLS], ALU.add)
                    tt(a, a, rows("edgeb"), ALU.add)
                    tt(a, a, xs[:, :, :], ALU.add)
                    layer_norm("ln3", a)
                    dve.sem_inc(out_ready, 1)
                passes += 1


def kernel(x, src, dst, edge_attr_3, edge_attr_48, edge_attr_8, edge_type_8, edge_weight, L0_gnn_W1, L0_gnn_b1,
           L0_gnn_W2, L0_gnn_b2, L1_gnn_W1, L1_gnn_root1, L1_gnn_b1, L1_gnn_W2, L1_gnn_root2, L1_gnn_b2,
           L2_gnn_fc0_w1, L2_gnn_fc0_b1, L2_gnn_fc0_w2, L2_gnn_fc0_b2, L2_gnn_fc1_w1, L2_gnn_fc1_b1, L2_gnn_fc1_w2,
           L2_gnn_fc1_b2, L2_gnn_bn0_gs, L2_gnn_bn0_bs, L2_gnn_bn0_gv, L2_gnn_bn1_gs, L2_gnn_bn1_bs, L3_gnn_root_w,
           L3_gnn_root_b, L3_gnn_edge_w, L3_gnn_edge_b):
    import concourse.bacc as bacc
    from concourse.bass_utils import run_bass_kernel_spmd

    A = np.asarray

    def per_edge(a):
        a = A(a)
        return a.reshape((P, TILES) + a.shape[1:])

    def relations(w, root):
        return np.concatenate([A(w).transpose(1, 0, 2).reshape(F, REL * F), A(root)], axis=1)

    def tensor_weights(w2, b2, i2, o1):
        w = np.concatenate([A(w2), A(b2)[None, :]], axis=0)
        a = w[:, :F * F].reshape(D48 + 1, F, F)
        b = w[:, F * F:].reshape(D48 + 1, i2, o1)
        both = np.concatenate([a, b], axis=2 if i2 == F else 1)
        return both.transpose(0, 2, 1).reshape(D48 + 1, W2)

    edge_i = np.concatenate([A(L3_gnn_edge_w), A(L3_gnn_edge_b)[None, :]], axis=0).reshape(ND8 + 1, F, F)
    edge_i = edge_i.transpose(2, 0, 1).reshape(F, T3)
    arrays = {
        "x": A(x).reshape(P, HI, F),
        "src": per_edge(src), "dst": per_edge(dst), "vec3": per_edge(edge_attr_3),
        "ea48t": per_edge(edge_attr_48).transpose(2, 1, 0).reshape(D48, TILES * P),
        "ea8": per_edge(edge_attr_8), "etype": per_edge(edge_type_8), "eweight": per_edge(edge_weight),
        "w1t": A(L0_gnn_W1).T, "b1": np.tile(A(L0_gnn_b1), KB)[:, None], "w2t": A(L0_gnn_W2).T, "b2": A(L0_gnn_b2),
        "relw1": relations(L1_gnn_W1, L1_gnn_root1), "relb1": A(L1_gnn_b1),
        "relw2": relations(L1_gnn_W2, L1_gnn_root2), "relb2": A(L1_gnn_b2),
        "fc0w1": A(L2_gnn_fc0_w1), "fc0b1": A(L2_gnn_fc0_b1)[:, None],
        "fc0w2": tensor_weights(L2_gnn_fc0_w2, L2_gnn_fc0_b2, F, NV),
        "fc1w1": A(L2_gnn_fc1_w1), "fc1b1": A(L2_gnn_fc1_b1)[:, None],
        "fc1w2": tensor_weights(L2_gnn_fc1_w2, L2_gnn_fc1_b2, NV, F),
        "bn0gs": A(L2_gnn_bn0_gs), "bn0bs": A(L2_gnn_bn0_bs), "bn0gv": A(L2_gnn_bn0_gv),
        "bn1gs": A(L2_gnn_bn1_gs), "bn1bs": A(L2_gnn_bn1_bs),
        "edgew": np.concatenate([edge_i, A(L3_gnn_root_w)], axis=1), "edgeb": A(L3_gnn_root_b),
    }
    nc = bacc.Bacc("TRN2", target_bir_lowering=False, num_devices=1)
    arrays = {k: np.ascontiguousarray(v) for k, v in arrays.items()}
    args = [nc.dram_tensor(f"in_{k}", v.shape, mybir.dt.from_np(v.dtype), kind="ExternalInput").ap()
            for k, v in arrays.items()]
    result = nc.dram_tensor("result", (P, HI, F), mybir.dt.float32, kind="ExternalOutput").ap()
    gnn_kernel(nc, *args, result)
    r = run_bass_kernel_spmd(nc, [{f"in_{k}": v for k, v in arrays.items()}], core_ids=[0])
    return r.results[0]["result"].reshape(NODES, F)
```

```python
from contextlib import ExitStack

import numpy as np

import concourse.bass as bass
from concourse import mybir

NODES, EDGES = 3125, 100000
P = 125
HI = NODES // P
TILES = EDGES // P
G = 8
GROUPS = TILES // G
HALF = G // 2 * P
STEPS = GROUPS // 2
F = 16
HID = 32
REL = 8
D48 = 48
ND8 = 8
NV = 4
MSG2 = F + 3 * NV
W2 = 320
REL_COLS = REL * F + F
EDGE_COLS = (ND8 + 1) * F + F
T3 = (ND8 + 1) * F
KB = 4
KGROUPS = [(q * KB, min(KB, HI - q * KB)) for q in range((HI + KB - 1) // KB)]

LO_D, HI_D, LO_S, HI_S, WEIGHT, NORM, RX, RY, RZ, HITYPE = range(10)
NM = 10
SRC_COLS = 4 * HI
IX_SRC, IX_DST, IX_SRCREL = range(3)

PASSES = [
    ("count", "count", None, 0, 0, "d"),
    ("gcn1", "scale_norm", IX_SRC, F, F, "d"),
    ("gcn2", "scale", IX_SRC, F, F, "d"),
    ("rel1", "scale", IX_SRCREL, F, F, "d"),
    ("rel2", "scale", IX_SRCREL, F, F, "d"),
    ("ten1", "tensor1", IX_DST, F, MSG2, "s"),
    ("ten2", "tensor2", IX_DST, MSG2, F, "s"),
    ("edge", "edge", IX_SRC, T3, F, "d"),
]
FUNCS = ["rnorm", "dis", "ln0", "ln1_exp", "ln1_log", "ln1", "bn0", "bnv", "bn1", "ln2", "ln3"]
MIXES = ["rel1", "rel2", "edge"]
LN_EPS = 1e-5


def gnn_kernel(nc, x, src, dst, vec3, ea48t, ea8, etype, eweight, w1t, b1, w2t, b2, relw1, relb1, relw2, relb2,
               fc0w1, fc0b1, fc0w2, fc1w1, fc1b1, fc1w2, bn0gs, bn0bs, bn0gv, bn1gs, bn1bs, edgew, edgeb, out):
    f32, i32 = mybir.dt.float32, mybir.dt.int32
    ALU, ACT, X = mybir.AluOpType, mybir.ActivationFunctionType, mybir.AxisListType.X

    ctx = ExitStack()
    with ctx:
        def sb(name, shape, dt=f32):
            return ctx.enter_context(nc.sbuf_tensor(name, shape, dt))

        def sem(name):
            return ctx.enter_context(nc.semaphore(name))

        tab = {"gcn1": (NODES, F), "gcn2": (NODES, F), "rel1": (NODES * REL, F),
               "rel2": (NODES * REL, F), "ten1": (NODES, F), "ten2": (NODES, MSG2), "edge": (NODES, T3)}
        tab = {k: nc.dram_tensor(f"table_{k}", s, f32, kind="Internal").ap() for k, s in tab.items()}

        meta = sb("meta", [P, TILES, NM])
        index = sb("index", [P, 3, TILES], i32)
        ring_meta = sb("ring_meta", [P, 2, G, NM])
        ring_index = sb("ring_index", [P, 2, G], i32)
        ring_ea8 = sb("ring_ea8", [P, 2, G, ND8])
        ring_ea48 = sb("ring_ea48", [2 * D48, 2, HALF])
        gathered = sb("gathered", [P, 2, G, T3])
        onehot = sb("onehot", [P, 2, G, P])
        distance = sb("distance", [P, 2, G, P])
        spread = sb("spread", [P, 2, G, HI * MSG2])
        hidden = sb("hidden", [2 * D48 + 1, 2, HALF])
        onehot_t = sb("onehot_t", [P, 2, HALF])
        ring_norm = sb("ring_norm", [P, 2, G])
        hot_hi = sb("hot_hi", [P, 2, G, HI])
        message = sb("message", [P, 2, G, MSG2])
        prod = sb("prod", [P, 2, G, W2])
        operand = sb("operand", [P, 2, G, F + NV])
        vprod = sb("vprod", [P, 2, G, 3 * NV])
        tsum = sb("tsum", [P, 2, G, F + NV])
        xs = sb("xs", [P, HI, F])
        ya = sb("ya", [P, HI, F])
        agg = sb("agg", [P, HI, F])
        acc = sb("acc", [P, HI, MSG2])
        t1 = sb("t1", [P, HI, MSG2])
        mixed = sb("mixed", [P, HI, EDGE_COLS])
        cols = sb("cols", [P, 8, HI])
        dis = sb("dis", [P, HI])
        inv_src = sb("inv_src", [P, HI])
        inv_rel = sb("inv_rel", [P, HI * REL])
        stat = sb("stat", [P, 8, MSG2])
        xt = sb("xt", [64, 2, P])
        ht = sb("ht", [128, 2, P])
        kw1 = sb("kw1", [KB * F, KB * HID])
        kw2 = sb("kw2", [KB * HID, KB * F])
        krel = [sb(f"krel{n}", [KB * F, KB * REL_COLS]) for n in range(2)]
        kedge = sb("kedge", [KB * F, KB * EDGE_COLS])
        wfc1 = [sb(f"wfc1_{n}", [2 * D48, 2 * D48]) for n in range(2)]
        bfc1 = [sb(f"bfc1_{n}", [2 * D48, 1]) for n in range(2)]
        wfc2 = [[sb(f"wfc2_{n}_{k}", [2 * D48 + 1, W2]) for k in range(2)] for n in range(2)]
        b1col = sb("b1col", [KB * HID, 1])
        ident = sb("ident", [P, P])
        ones = sb("ones", [P, P])
        zeros = sb("zeros", [P, 512])
        iota_i = sb("iota_i", [P, 512], i32)
        iota = sb("iota", [P, 512])
        brow = {n: sb(f"row_{n}", [P, w]) for n, w in
                [("b2", F), ("relb1", F), ("relb2", F), ("edgeb", F), ("bn0gs", F), ("bn0bs", F), ("bn0gv", NV),
                 ("bn1gs", F), ("bn1bs", F)]}

        work = spread[:, :, :, :].rearrange("p s g c -> p (s g c)")
        wi = work.bitcast(i32)
        src_i, dst_i, type_i = (wi[:, n * TILES:(n + 1) * TILES] for n in range(3))
        f_a, f_b, f_c, f_d = (work[:, n * TILES:(n + 1) * TILES] for n in range(3, 7))
        i_a = wi[:, 7 * TILES:8 * TILES]
        v_in = work[:, 8 * TILES:11 * TILES].rearrange("p (t c) -> p t c", c=3)
        w_in = work[:, 11 * TILES:12 * TILES]

        ps_acc = ctx.enter_context(nc.psum_tensor("ps_acc", [128, 2, 512], f32))
        ps_w = ctx.enter_context(nc.psum_tensor("ps_w", [128, 2, 2, 512], f32))
        ps_h = ctx.enter_context(nc.psum_tensor("ps_h", [128, 2, 512], f32))

        loaded = sem("loaded")
        zeroed = sem("zeroed")
        iota_made = sem("iota_made")
        vchain = sem("vchain")
        node_ready = sem("node_ready")
        table_ready = sem("table_ready")
        table_stored = [sem(f"table_stored_{n}") for n in tab]
        func_asked = sem("func_asked")
        func_done = sem("func_done")
        sums_asked = sem("sums_asked")
        sums_done = sem("sums_done")
        distance_made = sem("distance_made")
        mix_t = sem("mix_t")
        mix_ts = sem("mix_ts")
        mix_o = sem("mix_o")
        mix_os = sem("mix_os")
        gcn_h = sem("gcn_h")
        gcn_hs = sem("gcn_hs")
        acc_read = sem("acc_read")
        out_ready = sem("out_ready")
        gathers_begun = sem("gathers_begun")
        out_stored = sem("out_stored")

        class PassSems:

            def __init__(self, name, kind):
                self.meta_dmas = 2 if kind == "edge" else 1
                self.meta_in = [sem(f"{name}_meta_in{s}") for s in range(2)]
                if kind != "count":
                    self.index_in = [sem(f"{name}_index_in{s}") for s in range(2)]
                    self.index_used = sem(f"{name}_index_used")
                    self.gather_in = [sem(f"{name}_gather_in{s}") for s in range(2)]
                self.inputs_used = sem(f"{name}_inputs_used")
                self.onehot_ready = sem(f"{name}_onehot_ready")
                self.spread_ready = sem(f"{name}_spread_ready")
                self.spread_used = sem(f"{name}_spread_used")
                self.sums_ready = sem(f"{name}_sums_ready")
                if kind == "scale_norm":
                    self.turned = sem(f"{name}_turned")
                    self.turned_in = sem(f"{name}_turned_in")
                    self.norms_ready = sem(f"{name}_norms_ready")
                    self.norms_used = sem(f"{name}_norms_used")
                if kind in ("tensor1", "tensor2"):
                    self.ea48_in = [sem(f"{name}_ea48_in{s}") for s in range(2)]
                    self.hidden_done = sem(f"{name}_hidden_done")
                    self.hidden_ready = sem(f"{name}_hidden_ready")
                    self.weights_ready = sem(f"{name}_weights_ready")
                    self.weights_used = sem(f"{name}_weights_used")

        sems = {name: PassSems(name, kind) for name, kind, *_ in PASSES}
        stored = dict(zip(tab, table_stored))
        N_LOADS = 3 + 2 + 1 + 2 + 1 + len(brow) + 2 * 2 * 3 + KB * 5
        TABLE_ORDER = ["gcn1", "gcn2", "rel1", "rel2", "ten1", "ten2", "edge"]

        block = ctx.enter_context(nc.Block())

        @block.sync
        def _(sp):
            def load(to, of):
                sp.dma_start(to, of).then_inc(loaded, 16)

            load(src_i, src)
            load(dst_i, dst)
            load(type_i, etype)
            load(v_in, vec3)
            load(w_in, eweight)
            load(xs[:, :, :], x)
            for n, (a, b, c) in enumerate(((fc0w1, fc0b1, fc0w2), (fc1w1, fc1b1, fc1w2))):
                load(bfc1[n][:, :], b)
            load(b1col[:, :], b1)
            for name, row in (("b2", b2), ("relb1", relb1), ("relb2", relb2), ("edgeb", edgeb), ("bn0gs", bn0gs),
                              ("bn0bs", bn0bs), ("bn0gv", bn0gv), ("bn1gs", bn1gs), ("bn1bs", bn1bs)):
                load(brow[name][:, :], row.partition_broadcast(P))
            sp.wait_ge(zeroed, 1)
            for n, (a, c) in enumerate(((fc0w1, fc0w2), (fc1w1, fc1w2))):
                for k in range(2):
                    load(wfc1[n][k * D48:(k + 1) * D48, k * D48:(k + 1) * D48], a)
                    load(wfc2[n][k][k * D48:(k + 1) * D48, :], c[0:D48, :])
                    load(wfc2[n][k][2 * D48:2 * D48 + 1, :], c[D48:D48 + 1, :])
            for k in range(KB):
                load(kw1[k * F:(k + 1) * F, k * HID:(k + 1) * HID], w1t)
                load(kw2[k * HID:(k + 1) * HID, k * F:(k + 1) * F], w2t)
                load(krel[0][k * F:(k + 1) * F, k * REL_COLS:(k + 1) * REL_COLS], relw1)
                load(krel[1][k * F:(k + 1) * F, k * REL_COLS:(k + 1) * REL_COLS], relw2)
                load(kedge[k * F:(k + 1) * F, k * EDGE_COLS:(k + 1) * EDGE_COLS], edgew)

            def store(name, of):
                sp.wait_ge(table_ready, TABLE_ORDER.index(name) + 1)
                sp.dma_start(tab[name].rearrange("(p h) c -> p h c", p=P), of).then_inc(stored[name], 16)

            for name, kind, ix, gcols, mcols, side in PASSES:
                q = sems[name]
                if name == "gcn1":
                    store("gcn1", ya[:, :, :])
                elif name == "gcn2":
                    store("gcn2", ya[:, :, :])
                elif name in ("rel1", "rel2"):
                    sp.wait_ge(table_ready, TABLE_ORDER.index(name) + 1)
                    sp.dma_start(tab[name].rearrange("(p h r) c -> p h (r c)", p=P, r=REL),
                                 mixed[:, :, 0:REL * F]).then_inc(stored[name], 16)
                elif name == "ten1":
                    store("ten1", xs[:, :, :])
                elif name == "ten2":
                    store("ten2", acc[:, :, :])
                elif name == "edge":
                    store("edge", mixed[:, :, 0:T3])
                if name == "count":
                    sp.wait_ge(zeroed, 2)
                with sp.Fori(0, STEPS) as i:
                    for s in range(2):
                        sp.wait_ge(q.inputs_used, 2 * i + s + 1)
                        sp.wait_ge(q.onehot_ready, 2 * i + s + 1)
                        at = i * (2 * G) + s * G
                        if ix is not None:
                            sp.wait_ge(q.index_used, 2 * i + s + 1)
                            sp.dma_start(ring_index[:, s, :], index[:, ix, bass.ds(at, G)]).then_inc(q.index_in[s], 16)
                        if kind in ("tensor1", "tensor2"):
                            sp.wait_ge(q.hidden_done, 2 * i + s + 1)
                            sp.dma_start(ring_ea48[:, s, :], ea48t[:, bass.ds(i * (2 * HALF) + s * HALF, HALF)]).then_inc(q.ea48_in[s], 16)
                        if kind == "edge":
                            sp.dma_start(ring_ea8[:, s, :, :], ea8[:, bass.ds(at, G), :]).then_inc(q.meta_in[s], 16)
                        sp.dma_start(ring_meta[:, s, :, :], meta[:, bass.ds(at, G), :]).then_inc(q.meta_in[s], 16)
                sp.wait_ge(q.inputs_used, GROUPS + 2)
                sp.wait_ge(q.onehot_ready, GROUPS + 2)
                if ix is not None:
                    sp.wait_ge(q.index_used, GROUPS + 2)
            sp.wait_ge(out_ready, 1)
            sp.dma_start(out, xs[:, :, :]).then_inc(out_stored, 16)
            sp.wait_ge(out_stored, 16)

        @block.gpsimd
        def _(pool):
            nc.gpsimd.iota(iota_i[:, 0:256], [[1, 256]], base=0, channel_multiplier=0)
            nc.gpsimd.iota(iota_i[:, 256:257], [[1, 1]], base=0, channel_multiplier=1).then_inc(iota_made, 1)
            for name, kind, ix, gcols, mcols, side in PASSES:
                if ix is None:
                    continue
                q = sems[name]
                pool.wait_ge(stored[name], 16)
                pool.sem_inc(q.index_used, 2)
                with pool.Fori(0, STEPS) as i:
                    for s in range(2):
                        pool.wait_ge(q.index_in[s], 16 * (i + 1))
                        pool.sem_inc(gathers_begun, 1)
                        for j in range(G):
                            pool.indirect_dma_start(
                                gathered[:, s, j, 0:gcols], None, tab[name],
                                bass.IndirectOffsetOnAxis(ap=ring_index[:, s, j:j + 1], axis=0),
                                engine_sem=q.index_used if j == G - 1 else None,
                            ).then_inc(q.gather_in[s], 16)

        @block.scalar
        def _(act):
            def func(name, to, of, fn, **kw):
                n = FUNCS.index(name)
                act.wait_ge(func_asked, n + 1)
                nc.scalar.activation(to, of, fn, **kw).then_inc(func_done, 1)

            def mix(name, width):
                base = len(KGROUPS) * (1 + MIXES.index(name))
                for n, (h0, hn) in enumerate(KGROUPS):
                    act.wait_ge(mix_t, base + n + 1)
                    nc.scalar.copy(xt[0:hn * F, n % 2, :], ps_h[0:hn * F, n % 2, 0:P]).then_inc(mix_ts, 1)
                    act.wait_ge(mix_o, base + n + 1)
                    halves = 2 if hn == KB else 1
                    per = hn // halves
                    for u in range(halves):
                        last = nc.scalar.copy(mixed[:, h0 + u * per:h0 + (u + 1) * per, 0:width],
                                              ps_w[0:P, n % 2, u, 0:per * width].rearrange("p (h c) -> p h c", c=width))
                    last.then_inc(mix_os, 1)

            def onehot_part(q, i, s, side):
                act.wait_ge(q.meta_in[s], q.meta_dmas * 16 * (i + 1))
                act.wait_ge(q.spread_used, 2 * i + s + 1)
                lo = LO_S if side == "s" else LO_D
                for j in range(G):
                    last = nc.scalar.activation(distance[:, s, j, :], iota[:, 0:P], ACT.Abs,
                                                bias=ring_meta[:, s, j, lo:lo + 1], scale=-1.0)
                last.then_inc(distance_made, 1)

            n_groups = [0]

            def onehots(q, i, s, side):
                onehot_part(q, i, s, side)
                act.wait_ge(distance_made, 2 * i + s + 1 + n_groups[0])
                nc.scalar.activation(onehot[:, s, :, :], distance[:, s, :, :], ACT.Relu,
                                     bias=ones[:, 0:1], scale=-1.0).then_inc(q.onehot_ready, 1)

            func("rnorm", f_b, f_a, ACT.Sqrt)

            def onehot_pass(name, side):
                q = sems[name]
                act.sem_inc(q.onehot_ready, 2)
                with act.Fori(0, STEPS) as i:
                    for s in range(2):
                        onehots(q, i, s, side)
                n_groups[0] += GROUPS

            onehot_pass("count", "d")
            func("dis", cols[:, 2, :], cols[:, 1, :], ACT.Sqrt)
            q = sems["gcn1"]
            act.sem_inc(q.onehot_ready, 2)
            act.sem_inc(q.turned_in, 2)
            with act.Fori(0, STEPS) as i:
                for s in range(2):
                    onehots(q, i, s, "d")
                    for k in range(2):
                        act.wait_ge(q.turned, 4 * i + 2 * s + k + 1)
                        nc.scalar.copy(onehot_t[:, k, :], ps_h[0:P, k, 0:HALF]).then_inc(q.turned_in, 1)
            n_groups[0] += GROUPS
            for n, (h0, hn) in enumerate(KGROUPS):
                act.wait_ge(mix_t, n + 1)
                nc.scalar.copy(xt[0:hn * F, n % 2, :], ps_h[0:hn * F, n % 2, 0:P]).then_inc(mix_ts, 1)
                act.wait_ge(gcn_h, n + 1)
                nc.scalar.activation(ht[0:hn * HID, n % 2, :], ps_w[0:hn * HID, n % 2, 0, 0:P], ACT.Relu,
                                     bias=b1col[0:hn * HID, 0:1]).then_inc(gcn_hs, 1)
                act.wait_ge(mix_o, n + 1)
                nc.scalar.copy(t1[:, h0:h0 + hn, 0:F],
                               ps_w[0:P, n % 2, 1, 0:hn * F].rearrange("p (h c) -> p h c", c=F)).then_inc(mix_os, 1)
            onehot_pass("gcn2", "d")
            func("ln0", cols[:, 2, :], cols[:, 1, :], ACT.Sqrt)
            mix("rel1", REL_COLS)
            onehot_pass("rel1", "d")
            mix("rel2", REL_COLS)
            onehot_pass("rel2", "d")
            func("ln1_exp", t1[:, :, 0:F], acc[:, :, 0:F], ACT.Exp)
            func("ln1_log", cols[:, 2, :], cols[:, 1, :], ACT.Ln)
            func("ln1", cols[:, 2, :], cols[:, 1, :], ACT.Sqrt)
            for n, name in enumerate(("ten1", "ten2")):
                q = sems[name]
                def relu_part(i, s):
                    act.wait_ge(q.hidden_done, 2 * i + s + 1 + 2)
                    nc.scalar.activation(hidden[0:2 * D48, s, :], ps_h[0:2 * D48, s, 0:HALF],
                                         ACT.Relu, bias=bfc1[n][:, 0:1]).then_inc(q.hidden_ready, 1)

                act.sem_inc(q.onehot_ready, 2)
                for s in range(2):
                    relu_part(0, s)
                with act.Fori(0, STEPS - 1) as i:
                    for s in range(2):
                        onehots(q, i, s, "s")
                        relu_part(i + 1, s)
                for s in range(2):
                    onehots(q, STEPS - 1, s, "s")
                n_groups[0] += GROUPS
                if n == 0:
                    func("bn0", stat[:, 3, 0:F], stat[:, 2, 0:F], ACT.Sqrt)
                    func("bnv", stat[:, 3, 0:NV], stat[:, 2, 0:NV], ACT.Sqrt)
            func("bn1", stat[:, 3, 0:F], stat[:, 2, 0:F], ACT.Sqrt)
            func("ln2", cols[:, 2, :], cols[:, 1, :], ACT.Sqrt)
            mix("edge", EDGE_COLS)
            onehot_pass("edge", "d")
            func("ln3", cols[:, 2, :], cols[:, 1, :], ACT.Sqrt)

        @block.tensor
        def _(pe):
            def scatter_part(q, s, half, per, banks, first):
                for j in range(half * (G // 2), (half + 1) * (G // 2)):
                    for b in range(banks):
                        last = nc.tensor.matmul(ps_acc[0:P, b, 0:per], onehot[:, s, j, :],
                                                spread[:, s, j, b * per:(b + 1) * per],
                                                start=False, stop=False, skip_group_check=True)
                return last

            def open_sums(per, banks):
                for b in range(banks):
                    last = nc.tensor.matmul(ps_acc[0:P, b, 0:per], zeros[:, 0:P], zeros[:, 0:per],
                                            start=True, stop=False, skip_group_check=True)
                return last

            def close_sums(per, banks):
                for b in range(banks):
                    last = nc.tensor.matmul(ps_acc[0:P, b, 0:per], zeros[:, 0:P], zeros[:, 0:per],
                                            start=False, stop=True, skip_group_check=True)
                return last

            def mix(name, weights, width):
                base = len(KGROUPS) * (1 + MIXES.index(name))
                source = {"rel1": xs, "rel2": ya, "edge": xs}[name]
                pe.wait_ge(node_ready, 2 + MIXES.index(name))
                for n, (h0, hn) in enumerate(KGROUPS):
                    nc.tensor.transpose(ps_h[0:hn * F, n % 2, 0:P], source[:, h0:h0 + hn, :].rearrange("p h c -> p (h c)"),
                                        ident[:, :]).then_inc(mix_t, 1)
                    pe.wait_ge(mix_ts, base + n + 1)
                    if n >= 2:
                        pe.wait_ge(mix_os, base + n - 1)
                    halves = 2 if hn == KB else 1
                    per = hn // halves * width
                    for u in range(halves):
                        last = nc.tensor.matmul(ps_w[0:P, n % 2, u, 0:per], xt[0:hn * F, n % 2, :],
                                                weights[0:hn * F, u * per:(u + 1) * per], start=True, stop=True)
                    last.then_inc(mix_o, 1)

            def sum_over_partitions(n, width):
                pe.wait_ge(sums_asked, n + 1)
                nc.tensor.matmul(ps_h[0:P, 0, 0:width], ones[:, :], stat[:, 0, 0:width],
                                 start=True, stop=True).then_inc(sums_done, 1)

            pe.wait_ge(zeroed, 1)
            passes = 0
            for name, kind, ix, gcols, mcols, side in PASSES:
                q = sems[name]
                if passes:
                    pe.wait_ge(acc_read, passes)
                passes += 1
                banks = 2 if kind == "tensor1" else 1
                per = {"count": REL * HI + HI, "tensor1": HI * MSG2 // 2}.get(kind, HI * F)
                if name == "rel1":
                    mix("rel1", krel[0], REL_COLS)
                if name == "rel2":
                    mix("rel2", krel[1], REL_COLS)
                if name == "edge":
                    mix("edge", kedge, EDGE_COLS)
                if kind == "count":
                    open_sums(per, 1)
                    nc.tensor.matmul(ps_acc[0:P, 1, 0:SRC_COLS], zeros[:, 0:P], zeros[:, 0:SRC_COLS], start=True, stop=False,
                                     skip_group_check=True).then_inc(q.spread_used, 2)
                    with pe.Fori(0, STEPS) as i:
                        for s in range(2):
                            pe.wait_ge(q.onehot_ready, 2 * i + s + 1 + 2)
                            pe.wait_ge(q.spread_ready, 4 * i + 2 * s + 2 + 4)
                            for j in range(G):
                                nc.tensor.matmul(ps_acc[0:P, 0, 0:per], onehot[:, s, j, :], spread[:, s, j, 0:per],
                                                 start=False, stop=False, skip_group_check=True)
                                last = nc.tensor.matmul(ps_acc[0:P, 1, 0:SRC_COLS], spread[:, s, j, 256:256 + P],
                                                        spread[:, s, j, 400:400 + SRC_COLS],
                                                        start=False, stop=False, skip_group_check=True)
                            last.then_inc(q.spread_used, 1)
                    close_sums(per, 1)
                    nc.tensor.matmul(ps_acc[0:P, 1, 0:SRC_COLS], zeros[:, 0:P], zeros[:, 0:SRC_COLS], start=False, stop=True,
                                     skip_group_check=True).then_inc(q.sums_ready, 1)
                elif kind in ("scale", "edge", "scale_norm"):
                    open_sums(per, 1).then_inc(q.spread_used, 2)
                    with pe.Fori(0, STEPS) as i:
                        for s in range(2):
                            pe.wait_ge(q.onehot_ready, 2 * i + s + 1 + 2)
                            if kind == "scale_norm":
                                for k in range(2):
                                    pe.wait_ge(q.turned_in, 4 * i + 2 * s + k + 1)
                                    for j in range(4):
                                        last = nc.tensor.transpose(ps_h[0:P, k, j * P:(j + 1) * P],
                                                                   onehot[:, s, 4 * k + j, :], ident[:, :])
                                    last.then_inc(q.turned, 1)
                                for k in range(2):
                                    pe.wait_ge(q.turned_in, 4 * i + 2 * s + k + 1 + 2)
                                    pe.wait_ge(q.norms_used, 4 * i + 2 * s + k + 1)
                                    for j in range(4):
                                        last = nc.tensor.matmul(
                                            ps_w[0:P, k, j // 2, (j % 2) * 256:(j % 2) * 256 + REL * HI],
                                            onehot_t[:, k, j * P:(j + 1) * P], inv_rel[:, :], start=True, stop=True)
                                    last.then_inc(q.norms_ready, 1)
                            for half in range(2):
                                pe.wait_ge(q.spread_ready, 4 * i + 2 * s + half + 1 + 4)
                                last = scatter_part(q, s, half, per, 1, False)
                            last.then_inc(q.spread_used, 1)
                    close_sums(per, 1).then_inc(q.sums_ready, 1)
                else:
                    n = 0 if kind == "tensor1" else 1

                    def hidden_part(i, s):
                        pe.wait_ge(q.ea48_in[s], 16 * (i + 1))
                        pe.wait_ge(q.hidden_ready, 2 * i + s + 1)
                        nc.tensor.matmul(ps_h[0:2 * D48, s, 0:HALF], wfc1[n][:, :], ring_ea48[:, s, :],
                                         start=True, stop=True).then_inc(q.hidden_done, 1)

                    def weights_part(i, s, k):
                        pe.wait_ge(q.hidden_ready, 2 * i + s + 1 + 2)
                        for u in range(2):
                            pe.wait_ge(q.weights_used, 8 * i + 4 * s + 2 * k + u + 1)
                            for v in range(2):
                                j = 2 * u + v
                                last = nc.tensor.matmul(ps_w[0:P, u, v, 0:W2], hidden[:, s, j * P:(j + 1) * P],
                                                        wfc2[n][k][:, :], start=True, stop=True)
                            last.then_inc(q.weights_ready, 1)

                    def sums_part(i, s, half):
                        pe.wait_ge(q.onehot_ready, 2 * i + s + 1 + 2)
                        pe.wait_ge(q.spread_ready, 4 * i + 2 * s + half + 1 + 4)
                        return scatter_part(q, s, half, per, banks, False)

                    pe.sem_inc(q.hidden_done, 2)
                    open_sums(per, banks).then_inc(q.spread_used, 2)
                    hidden_part(0, 0)
                    weights_part(0, 0, 0)
                    hidden_part(0, 1)
                    weights_part(0, 0, 1)
                    weights_part(0, 1, 0)
                    with pe.Fori(0, STEPS - 1) as i:
                        for s in range(2):
                            nxt = (i, 1) if s == 0 else (i + 1, 0)
                            hidden_part(i + 1, s)
                            weights_part(*nxt, 1)
                            sums_part(i, s, 0)
                            weights_part(i + 1, s, 0)
                            sums_part(i, s, 1).then_inc(q.spread_used, 1)
                    i = STEPS - 1
                    weights_part(i, 1, 1)
                    for s in range(2):
                        sums_part(i, s, 0)
                        sums_part(i, s, 1).then_inc(q.spread_used, 1)
                    close_sums(per, banks).then_inc(q.sums_ready, 1)
                if name == "gcn1":
                    pe.wait_ge(node_ready, 1)
                    for n, (h0, hn) in enumerate(KGROUPS):
                        nc.tensor.transpose(ps_h[0:hn * F, n % 2, 0:P], 
                                            agg[:, h0:h0 + hn, :].rearrange("p h c -> p (h c)"),
                                            ident[:, :]).then_inc(mix_t, 1)
                        pe.wait_ge(mix_ts, n + 1)
                        if n >= 2:
                            pe.wait_ge(mix_os, n - 1)
                        nc.tensor.matmul(ps_w[0:hn * HID, n % 2, 0, 0:P], kw1[0:hn * F, 0:hn * HID],
                                         xt[0:hn * F, n % 2, :], start=True, stop=True).then_inc(gcn_h, 1)
                        pe.wait_ge(gcn_hs, n + 1)
                        nc.tensor.matmul(ps_w[0:P, n % 2, 1, 0:hn * F], ht[0:hn * HID, n % 2, :],
                                         kw2[0:hn * HID, 0:hn * F], start=True, stop=True).then_inc(mix_o, 1)
                if name == "ten1":
                    for n in range(3):
                        sum_over_partitions(n, (F, F, NV)[n])
                if name == "ten2":
                    for n in range(2):
                        sum_over_partitions(3 + n, F)

        @block.vector
        def _(dve):
            V = nc.vector
            n_chain = [0, 0]
            loop = [None, 0]

            def link(ins):
                n_chain[0] += 1
                ins.then_inc(vchain, 1)
                if loop[0] is None:
                    dve.wait_ge(vchain, n_chain[0])
                else:
                    dve.wait_ge(vchain, loop[0] * loop[1] + n_chain[0])

            def bc(ap, shape):
                return ap.broadcast_to(shape)

            def rows(name, width=F):
                return bc(brow[name][:, :].unsqueeze(1), [P, HI, width])

            def func(name):
                dve.sem_inc(func_asked, 1)
                dve.wait_ge(func_done, FUNCS.index(name) + 1)

            def tt(o, a, b, op):
                link(V.tensor_tensor(o, a, b, op))

            def ts(o, a, c1, c2, op0, op1=None):
                if op1 is None:
                    link(V.tensor_scalar(o, a, c1, None, op0))
                else:
                    link(V.tensor_scalar(o, a, c1, c2, op0, op1))

            def red(o, a, op=ALU.add):
                link(V.tensor_reduce(o, a, X, op))

            def colb(c, width=F):
                return bc(c.unsqueeze(2), [P, HI, width])

            def layer_norm(name, r):
                red(cols[:, 0, :], r)
                ts(cols[:, 0, :], cols[:, 0, :], 1.0 / F, None, ALU.mult)
                tt(r, r, colb(cols[:, 0, :]), ALU.subtract)
                tt(xs[:, :, :], r, r, ALU.mult)
                red(cols[:, 1, :], xs[:, :, :])
                ts(cols[:, 1, :], cols[:, 1, :], 1.0 / F, LN_EPS, ALU.mult, ALU.add)
                func(name)
                link(V.reciprocal(cols[:, 3, :], cols[:, 2, :]))
                tt(xs[:, :, :], r, colb(cols[:, 3, :]), ALU.mult)

            n_sums = [0]

            def total(to, of):
                w = of.shape[2]
                red(stat[:, 0, 0:w], of.rearrange("p h c -> p c h"))
                dve.sem_inc(sums_asked, 1)
                n_sums[0] += 1
                dve.wait_ge(sums_done, n_sums[0])
                link(V.tensor_copy(to, ps_h[0:P, 0, 0:w]))

            def batch_norm(name, r, scale, shift):
                sq = t1[:, :, 0:F]
                total(stat[:, 1, 0:F], r)
                ts(stat[:, 1, 0:F], stat[:, 1, 0:F], 1.0 / NODES, None, ALU.mult)
                tt(r, r, bc(stat[:, 1, 0:F].unsqueeze(1), [P, HI, F]), ALU.subtract)
                tt(sq, r, r, ALU.mult)
                total(stat[:, 2, 0:F], sq)
                ts(stat[:, 2, 0:F], stat[:, 2, 0:F], 1.0 / NODES, LN_EPS, ALU.mult, ALU.add)
                func(name)
                link(V.reciprocal(stat[:, 4, 0:F], stat[:, 3, 0:F]))
                tt(stat[:, 4, 0:F], stat[:, 4, 0:F], brow[scale][:, :], ALU.mult)
                tt(r, r, bc(stat[:, 4, 0:F].unsqueeze(1), [P, HI, F]), ALU.mult)
                tt(r, r, rows(shift), ALU.add)

            for t in (kw1, kw2, krel[0], krel[1], kedge, *wfc1, *wfc2[0], *wfc2[1]):
                V.memset(t[:, :], 0.0)
            V.memset(zeros[:, :], 0.0)
            V.memset(ones[:, :], 1.0)
            link(V.memset(hidden[:, :, :], 1.0))
            dve.sem_inc(zeroed, 1)
            dve.wait_ge(iota_made, 1)
            link(V.tensor_copy(iota[:, 0:257], iota_i[:, 0:257]))
            row_id = iota[:, 256:257]
            ts(ident[:, :], iota[:, 0:P], row_id, None, ALU.is_equal)
            dve.wait_ge(loaded, 16 * N_LOADS)

            def split(raw, lo, hi):
                link(V.tensor_copy(f_a, raw))
                ts(i_a, f_a, 1.0 / HI, None, ALU.mult)
                link(V.tensor_copy(f_b, i_a))
                link(V.scalar_tensor_tensor(f_c, f_b, -float(HI), f_a, ALU.mult, ALU.add))
                ts(f_d, f_c, 0.0, None, ALU.is_lt)
                tt(f_b, f_b, f_d, ALU.subtract)
                link(V.scalar_tensor_tensor(f_c, f_d, float(HI), f_c, ALU.mult, ALU.add))
                ts(f_d, f_c, float(HI), None, ALU.is_ge)
                tt(meta[:, :, lo], f_b, f_d, ALU.add)
                link(V.scalar_tensor_tensor(meta[:, :, hi], f_d, -float(HI), f_c, ALU.mult, ALU.add))

            split(src_i, LO_S, HI_S)
            link(V.tensor_copy(index[:, IX_SRC, :], src_i))
            link(V.tensor_copy(f_b, type_i))
            link(V.scalar_tensor_tensor(index[:, IX_SRCREL, :], f_a, float(REL), f_b, ALU.mult, ALU.add))
            split(dst_i, LO_D, HI_D)
            link(V.tensor_copy(index[:, IX_DST, :], dst_i))
            link(V.tensor_copy(f_b, type_i))
            link(V.scalar_tensor_tensor(meta[:, :, HITYPE], meta[:, :, HI_D], float(REL), f_b, ALU.mult, ALU.add))
            link(V.tensor_copy(meta[:, :, WEIGHT], w_in))
            link(V.memset(meta[:, :, NORM], 0.0))
            tt(meta[:, :, RX:RZ + 1], v_in, v_in, ALU.mult)
            red(f_a, meta[:, :, RX:RZ + 1])
            func("rnorm")
            ts(f_b, f_b, 1e-12, None, ALU.add)
            link(V.reciprocal(f_c, f_b))
            tt(meta[:, :, RX:RZ + 1], v_in, bc(f_c.unsqueeze(2), [P, TILES, 3]), ALU.mult)
            dve.sem_inc(zeroed, 1)

            def hot(o, m, width):
                n = o.shape[1]
                return V.tensor_tensor(o, bc(iota[:, 0:width].unsqueeze(1), [P, n, width]),
                                       bc(m.unsqueeze(2), [P, n, width]), ALU.is_equal)

            LINKS = {"count": 2 * 4, "scale_norm": 2 * 3, "scale": 2 * 2, "edge": 2 * 4, "tensor1": 2 * 3, "tensor2": 2 * 4}
            passes = 0
            for name, kind, ix, gcols, mcols, side in PASSES:
                q = sems[name]
                dve.sem_inc(q.inputs_used, 2)
                if kind == "scale_norm":
                    dve.sem_inc(q.norms_used, 2)
                if kind == "count":
                    link(V.memset(spread[:, :, :, 400:400 + SRC_COLS], 0.0))
                if kind in ("tensor1", "tensor2"):
                    dve.sem_inc(q.weights_used, 2)
                    dve.sem_inc(q.hidden_ready, 2)
                dve.sem_inc(q.spread_ready, 4)
                side_hi = HI_S if side == "s" else HI_D
                banks = 2 if kind == "tensor1" else 1
                w = mcols // banks
                tensor = kind in ("tensor1", "tensor2")
                nj, ni = (F + NV, F) if kind == "tensor1" else (F, F + NV)

                def expand(i, s, half):
                    if half == 0:
                        dve.wait_ge(q.spread_used, 2 * i + s + 1)
                    t = slice(half * G // 2, (half + 1) * G // 2)
                    for b in range(banks):
                        last = V.tensor_tensor(
                            spread[:, s, t, b * HI * w:(b + 1) * HI * w].rearrange("p g (h c) -> p g h c", c=w),
                            bc(hot_hi[:, s, t, :].unsqueeze(3), [P, G // 2, HI, w]),
                            bc(message[:, s, t, b * w:(b + 1) * w].unsqueeze(2), [P, G // 2, HI, w]), ALU.mult)
                    last.then_inc(q.spread_ready, 1)

                def prepare(i, s):
                    dve.wait_ge(q.meta_in[s], q.meta_dmas * 16 * (i + 1))
                    dve.wait_ge(q.spread_ready, 4 * i + 2 * s + 2)
                    link(hot(hot_hi[:, s, :, :], ring_meta[:, s, :, side_hi], HI))
                    if kind != "count":
                        dve.wait_ge(q.gather_in[s], 16 * G * (i + 1))
                    if kind == "tensor2":
                        g = gathered[:, s, :, 0:gcols]
                        V.tensor_copy(operand[:, s, :, 0:F], g[:, :, 0:F])
                        tt(vprod[:, s, :, :].rearrange("p g (j c) -> p g j c", c=3),
                           g[:, :, F:MSG2].rearrange("p g (j c) -> p g j c", c=3),
                           bc(ring_meta[:, s, :, RX:RZ + 1].unsqueeze(2), [P, G, NV, 3]), ALU.mult)
                        red(operand[:, s, :, F:F + NV], vprod[:, s, :, :].rearrange("p g (j c) -> p g j c", c=3))

                def multiply(i, s, k):
                    op = gathered[:, s, :, 0:F] if kind == "tensor1" else operand[:, s, :, :]
                    for u in (2 * k, 2 * k + 1):
                        dve.wait_ge(q.weights_ready, 8 * i + 4 * s + u + 1)
                        V.tensor_tensor(
                            prod[:, s, 2 * u:2 * u + 2, :].rearrange("p g (j i) -> p g j i", i=ni),
                            ps_w[0:P, u % 2, :, 0:W2].rearrange("p g (j i) -> p g j i", i=ni),
                            bc(op[:, 2 * u:2 * u + 2, :].unsqueeze(2), [P, 2, nj, ni]),
                            ALU.mult).then_inc(q.weights_used, 1)

                def finish(i, s):
                    dve.wait_ge(q.weights_used, 8 * i + 4 * s + 4 + 2)
                    to = tsum if kind == "tensor1" else message
                    red(to[:, s, :, 0:nj], prod[:, s, :, :].rearrange("p g (j i) -> p g j i", i=ni))
                    if kind == "tensor1":
                        V.tensor_copy(message[:, s, :, 0:F], tsum[:, s, :, 0:F])
                        tt(message[:, s, :, F:MSG2].rearrange("p g (j c) -> p g j c", c=3),
                           bc(tsum[:, s, :, F:F + NV].unsqueeze(3), [P, G, NV, 3]),
                           bc(ring_meta[:, s, :, RX:RZ + 1].unsqueeze(2), [P, G, NV, 3]), ALU.mult)
                    dve.sem_inc(q.inputs_used, 1)

                if tensor:
                    prepare(0, 0)
                    multiply(0, 0, 0)
                    multiply(0, 0, 1)
                    finish(0, 0)
                start = n_chain[0]
                turns = STEPS - 1 if tensor else STEPS
                with dve.Fori(0, turns) as i:
                    loop[0], loop[1] = i, LINKS[kind]
                    for s in range(2):
                        if tensor:
                            nxt = (i, 1) if s == 0 else (i + 1, 0)
                            prepare(*nxt)
                            multiply(*nxt, 0)
                            expand(i, s, 0)
                            multiply(*nxt, 1)
                            expand(i, s, 1)
                            finish(*nxt)
                            continue
                        prepare(i, s)
                        m = ring_meta[:, s, :, :]
                        g = gathered[:, s, :, 0:gcols]
                        if kind == "count":
                            dve.wait_ge(q.spread_used, 2 * i + s + 1)
                            hot(spread[:, s, :, 0:REL * HI], m[:, :, HITYPE], REL * HI)
                            link(hot(spread[:, s, :, 256:256 + P], m[:, :, LO_S], P))
                            link(hot(spread[:, s, :, 400:400 + HI], m[:, :, HI_S], HI))
                            link(V.tensor_tensor(spread[:, s, :, REL * HI:REL * HI + HI], hot_hi[:, s, :, :],
                                                 bc(m[:, :, WEIGHT:WEIGHT + 1], [P, G, HI]), ALU.mult))
                            dve.sem_inc(q.spread_ready, 2)
                            dve.sem_inc(q.inputs_used, 1)
                            continue
                        if kind == "edge":
                            pr = prod[:, s, :, 0:ND8 * F].rearrange("p g (k o) -> p g k o", o=F)
                            tt(pr, g[:, :, 0:ND8 * F].rearrange("p g (k o) -> p g k o", o=F),
                               bc(ring_ea8[:, s, :, :].unsqueeze(3), [P, G, ND8, F]), ALU.mult)
                            red(tsum[:, s, :, 0:F], pr.rearrange("p g k o -> p g o k"))
                            tt(message[:, s, :, 0:F], tsum[:, s, :, 0:F], g[:, :, ND8 * F:T3], ALU.add)
                        else:
                            by = WEIGHT if name in ("gcn1", "gcn2") else NORM
                            link(V.tensor_tensor(message[:, s, :, 0:F], g, bc(m[:, :, by:by + 1], [P, G, F]),
                                                 ALU.mult))
                        if kind != "scale_norm":
                            dve.sem_inc(q.inputs_used, 1)
                        expand(i, s, 0)
                        expand(i, s, 1)
                        if kind == "scale_norm":
                            for k in range(2):
                                dve.wait_ge(q.norms_ready, 4 * i + 2 * s + k + 1)
                                for j in range(4):
                                    last = V.scalar_tensor_tensor(
                                        prod[:, s, 4 * k + j, 0:REL * HI], iota[:, 0:REL * HI],
                                        m[:, 4 * k + j, HITYPE:HITYPE + 1],
                                        ps_w[0:P, k, j // 2, (j % 2) * 256:(j % 2) * 256 + REL * HI],
                                        ALU.is_equal, ALU.mult, accum_out=ring_norm[:, s, 4 * k + j:4 * k + j + 1])
                                last.then_inc(q.norms_used, 1)
                            dve.wait_ge(q.norms_used, 4 * i + 2 * s + 2 + 2)
                            link(V.tensor_copy(meta[:, bass.ds(i * (2 * G) + s * G, G), NORM],
                                               ring_norm[:, s, :]))
                            dve.sem_inc(q.inputs_used, 1)
                    per_turn = n_chain[0] - start
                assert per_turn == LINKS[kind], (kind, per_turn)
                n_chain[0] = start + per_turn * turns
                loop[0] = None
                if tensor:
                    i = STEPS - 1
                    prepare(i, 1)
                    multiply(i, 1, 0)
                    expand(i, 0, 0)
                    multiply(i, 1, 1)
                    expand(i, 0, 1)
                    finish(i, 1)
                    expand(i, 1, 0)
                    expand(i, 1, 1)
                dve.wait_ge(q.sums_ready, 1)
                if kind == "count":
                    link(V.tensor_copy(inv_rel[:, :], ps_acc[0:P, 0, 0:REL * HI]))
                    ts(cols[:, 0, :], ps_acc[0:P, 0, REL * HI:REL * HI + HI], 1.0, None, ALU.add)
                    ts(inv_src[:, :], ps_acc[0:P, 1, 0:HI], 1.0, None, ALU.max)
                    dve.sem_inc(acc_read, 1)
                    ts(inv_rel[:, :], inv_rel[:, :], 1.0, None, ALU.max)
                    link(V.reciprocal(inv_rel[:, :], inv_rel[:, :]))
                    link(V.reciprocal(inv_src[:, :], inv_src[:, :]))
                    ts(cols[:, 3, :], cols[:, 0, :], 0.0, None, ALU.is_gt)
                    ts(cols[:, 1, :], cols[:, 0, :], 1e-37, None, ALU.max)
                    func("dis")
                    link(V.reciprocal(dis[:, :], cols[:, 2, :]))
                    tt(dis[:, :], dis[:, :], cols[:, 3, :], ALU.mult)
                    tt(ya[:, :, :], xs[:, :, :], colb(dis[:, :]), ALU.mult)
                    dve.sem_inc(table_ready, 1)
                    continue
                a = acc[:, :, 0:F]
                sums = ps_acc[0:P, 0, 0:HI * F].rearrange("p (h c) -> p h c", c=F)
                if name in ("gcn1", "gcn2"):
                    tt(a, sums, ya[:, :, :], ALU.add)
                    dve.sem_inc(acc_read, 1)
                    if name == "gcn1":
                        tt(agg[:, :, :], a, colb(dis[:, :]), ALU.mult)
                        dve.sem_inc(node_ready, 1)
                        dve.wait_ge(mix_os, len(KGROUPS))
                        tt(ya[:, :, :], t1[:, :, 0:F], colb(dis[:, :]), ALU.mult)
                        dve.sem_inc(table_ready, 1)
                    else:
                        tt(a, a, colb(dis[:, :]), ALU.mult)
                        tt(a, a, rows("b2"), ALU.add)
                        tt(a, a, xs[:, :, :], ALU.add)
                        layer_norm("ln0", a)
                        dve.sem_inc(node_ready, 1)
                        dve.wait_ge(mix_os, 2 * len(KGROUPS))
                        dve.sem_inc(table_ready, 1)
                elif name in ("rel1", "rel2"):
                    tt(a, sums, mixed[:, :, REL * F:REL_COLS], ALU.add)
                    dve.sem_inc(acc_read, 1)
                    tt(a, a, rows("relb1" if name == "rel1" else "relb2"), ALU.add)
                    if name == "rel1":
                        ts(ya[:, :, :], a, 0.0, None, ALU.max)
                        dve.sem_inc(node_ready, 1)
                        dve.wait_ge(mix_os, 3 * len(KGROUPS))
                        dve.sem_inc(table_ready, 1)
                    else:
                        red(cols[:, 0, :], a, ALU.max)
                        tt(a, a, colb(cols[:, 0, :]), ALU.subtract)
                        func("ln1_exp")
                        red(cols[:, 1, :], t1[:, :, 0:F])
                        func("ln1_log")
                        tt(a, a, colb(cols[:, 2, :]), ALU.subtract)
                        tt(a, a, xs[:, :, :], ALU.add)
                        layer_norm("ln1", a)
                        dve.sem_inc(table_ready, 1)
                elif name == "ten1":
                    h = MSG2 // 2
                    for b in range(2):
                        link(V.tensor_tensor(acc[:, :, b * h:(b + 1) * h],
                                             ps_acc[0:P, b, 0:HI * h].rearrange("p (h c) -> p h c", c=h),
                                             colb(inv_src[:, :], h), ALU.mult))
                    dve.sem_inc(acc_read, 1)
                    ts(acc[:, :, 0:F], acc[:, :, 0:F], float(1.0 / np.sqrt(F)), None, ALU.mult)
                    ts(acc[:, :, F:MSG2], acc[:, :, F:MSG2], float(np.sqrt(3.0) / np.sqrt(F)), None, ALU.mult)
                    batch_norm("bn0", a, "bn0gs", "bn0bs")
                    v = acc[:, :, F:MSG2]
                    sq = t1[:, :, F:MSG2]
                    tt(sq, v, v, ALU.mult)
                    red(t1[:, :, 0:NV], sq.rearrange("p h (j c) -> p h j c", c=3))
                    total(stat[:, 2, 0:NV], t1[:, :, 0:NV])
                    ts(stat[:, 2, 0:NV], stat[:, 2, 0:NV], 1.0 / (3 * NODES), LN_EPS, ALU.mult, ALU.add)
                    func("bnv")
                    link(V.reciprocal(stat[:, 4, 0:NV], stat[:, 3, 0:NV]))
                    tt(stat[:, 4, 0:NV], stat[:, 4, 0:NV], brow["bn0gv"][:, :], ALU.mult)
                    link(V.tensor_copy(stat[:, 5, 0:3 * NV].rearrange("p (j c) -> p j c", c=3),
                                       bc(stat[:, 4, 0:NV].unsqueeze(2), [P, NV, 3])))
                    tt(v, v, bc(stat[:, 5, 0:3 * NV].unsqueeze(1), [P, HI, 3 * NV]), ALU.mult)
                    dve.sem_inc(table_ready, 1)
                elif name == "ten2":
                    tt(a, sums, colb(inv_src[:, :]), ALU.mult)
                    dve.sem_inc(acc_read, 1)
                    ts(a, a, float(1.0 / np.sqrt(F + NV)), None, ALU.mult)
                    batch_norm("bn1", a, "bn1gs", "bn1bs")
                    tt(a, a, xs[:, :, :], ALU.add)
                    layer_norm("ln2", a)
                    dve.sem_inc(node_ready, 1)
                    dve.wait_ge(mix_os, 4 * len(KGROUPS))
                    dve.sem_inc(table_ready, 1)
                else:
                    tt(a, sums, mixed[:, :, T3:EDGE_COLS], ALU.add)
                    tt(a, a, rows("edgeb"), ALU.add)
                    tt(a, a, xs[:, :, :], ALU.add)
                    layer_norm("ln3", a)
                    dve.sem_inc(out_ready, 1)
                passes += 1


def kernel(x, src, dst, edge_attr_3, edge_attr_48, edge_attr_8, edge_type_8, edge_weight, L0_gnn_W1, L0_gnn_b1,
           L0_gnn_W2, L0_gnn_b2, L1_gnn_W1, L1_gnn_root1, L1_gnn_b1, L1_gnn_W2, L1_gnn_root2, L1_gnn_b2,
           L2_gnn_fc0_w1, L2_gnn_fc0_b1, L2_gnn_fc0_w2, L2_gnn_fc0_b2, L2_gnn_fc1_w1, L2_gnn_fc1_b1, L2_gnn_fc1_w2,
           L2_gnn_fc1_b2, L2_gnn_bn0_gs, L2_gnn_bn0_bs, L2_gnn_bn0_gv, L2_gnn_bn1_gs, L2_gnn_bn1_bs, L3_gnn_root_w,
           L3_gnn_root_b, L3_gnn_edge_w, L3_gnn_edge_b):
    import concourse.bacc as bacc
    from concourse.bass_utils import run_bass_kernel_spmd

    A = np.asarray

    def per_edge(a):
        a = A(a)
        return a.reshape((P, TILES) + a.shape[1:])

    def relations(w, root):
        return np.concatenate([A(w).transpose(1, 0, 2).reshape(F, REL * F), A(root)], axis=1)

    def tensor_weights(w2, b2, i2, o1):
        w = np.concatenate([A(w2), A(b2)[None, :]], axis=0)
        a = w[:, :F * F].reshape(D48 + 1, F, F)
        b = w[:, F * F:].reshape(D48 + 1, i2, o1)
        both = np.concatenate([a, b], axis=2 if i2 == F else 1)
        return both.transpose(0, 2, 1).reshape(D48 + 1, W2)

    edge_i = np.concatenate([A(L3_gnn_edge_w), A(L3_gnn_edge_b)[None, :]], axis=0).reshape(ND8 + 1, F, F)
    edge_i = edge_i.transpose(2, 0, 1).reshape(F, T3)
    arrays = {
        "x": A(x).reshape(P, HI, F),
        "src": per_edge(src), "dst": per_edge(dst), "vec3": per_edge(edge_attr_3),
        "ea48t": A(edge_attr_48).reshape(P, GROUPS, 2, G // 2, D48).transpose(2, 4, 1, 3, 0).reshape(2 * D48, GROUPS * HALF),
        "ea8": per_edge(edge_attr_8), "etype": per_edge(edge_type_8), "eweight": per_edge(edge_weight),
        "w1t": A(L0_gnn_W1).T, "b1": np.tile(A(L0_gnn_b1), KB)[:, None], "w2t": A(L0_gnn_W2).T, "b2": A(L0_gnn_b2),
        "relw1": relations(L1_gnn_W1, L1_gnn_root1), "relb1": A(L1_gnn_b1),
        "relw2": relations(L1_gnn_W2, L1_gnn_root2), "relb2": A(L1_gnn_b2),
        "fc0w1": A(L2_gnn_fc0_w1), "fc0b1": np.tile(A(L2_gnn_fc0_b1), 2)[:, None],
        "fc0w2": tensor_weights(L2_gnn_fc0_w2, L2_gnn_fc0_b2, F, NV),
        "fc1w1": A(L2_gnn_fc1_w1), "fc1b1": np.tile(A(L2_gnn_fc1_b1), 2)[:, None],
        "fc1w2": tensor_weights(L2_gnn_fc1_w2, L2_gnn_fc1_b2, NV, F),
        "bn0gs": A(L2_gnn_bn0_gs), "bn0bs": A(L2_gnn_bn0_bs), "bn0gv": A(L2_gnn_bn0_gv),
        "bn1gs": A(L2_gnn_bn1_gs), "bn1bs": A(L2_gnn_bn1_bs),
        "edgew": np.concatenate([edge_i, A(L3_gnn_root_w)], axis=1), "edgeb": A(L3_gnn_root_b),
    }
    nc = bacc.Bacc("TRN2", target_bir_lowering=False, num_devices=1)
    arrays = {k: np.ascontiguousarray(v) for k, v in arrays.items()}
    args = [nc.dram_tensor(f"in_{k}", v.shape, mybir.dt.from_np(v.dtype), kind="ExternalInput").ap()
            for k, v in arrays.items()]
    result = nc.dram_tensor("result", (P, HI, F), mybir.dt.float32, kind="ExternalOutput").ap()
    gnn_kernel(nc, *args, result)
    r = run_bass_kernel_spmd(nc, [{f"in_{k}": v for k, v in arrays.items()}], core_ids=[0])
    return r.results[0]["result"].reshape(NODES, F)
```

```python
from contextlib import ExitStack

import numpy as np

import concourse.bass as bass
from concourse import mybir

NODES, EDGES = 3125, 100000
P = 125
EP = 128
HI = NODES // P
G = 8
GROUPS = 2 * -(-EDGES // (EP * 2 * G))
TILES = GROUPS * G
NO_NODE = 4 * HI
HALF = G // 2 * EP
STEPS = GROUPS // 2
F = 16
HID = 32
REL = 8
D48 = 48
ND8 = 8
NV = 4
MSG2 = F + 3 * NV
W2 = 320
REL_COLS = REL * F + F
EDGE_COLS = (ND8 + 1) * F + F
T3 = (ND8 + 1) * F
KB = 4
KGROUPS = [(q * KB, min(KB, HI - q * KB)) for q in range((HI + KB - 1) // KB)]

LO_D, HI_D, LO_S, HI_S, HITYPE, WEIGHT1, WEIGHT2, WEIGHT3, WEIGHT, NORM, RX, RY, RZ = range(13)
NM, NPAIR = 13, 8
HI2, P2 = HI + HI % 2, P + P % 2
SRC_COLS = 4 * HI
C_REL = 0
C_WEIGHT = C_REL + REL * HI
C_SRC = C_WEIGHT + 3 * HI2
C_ONEHOT_S = C_SRC + SRC_COLS
C_ONEHOT_D = C_ONEHOT_S + P2
IX_SRC, IX_DST, IX_SRCREL = range(3)

ACT_TILES = 6

LOOKUP_TILE = 0
LOOKUPS = G // 2 + 1

PASSES = [
    ("count", "count", None, 0, 0, "d"),
    ("gcn1", "scale_norm", IX_SRC, F, F, "d"),
    ("gcn2", "scale_norm", IX_SRC, F, F, "d"),
    ("rel1", "scale", IX_SRCREL, F, F, "d"),
    ("rel2", "scale", IX_SRCREL, F, F, "d"),
    ("ten1", "tensor1", IX_DST, F, MSG2, "s"),
    ("ten2", "tensor2", IX_DST, MSG2, F, "s"),
    ("edge", "edge", IX_SRC, T3, F, "d"),
]
FUNCS = ["rnorm", "dis", "ln0", "ln1_exp", "ln1_log", "ln1", "bn0", "bnv", "bn1", "ln2", "ln3"]
MIXES = ["rel1", "rel2", "edge"]
NORM_HALF = {"gcn1": 0, "gcn2": 1}
LOOKUP_PASSES = ["gcn1", "gcn2", "rel1", "rel2"]
HALVES = [range(G // 2), range(G // 2, G)]
SUM_PARTS = [range(0, 3), range(3, 4), range(4, 5), range(5, 8)]
ROW_AT = EP
TENSOR_OF = {"rel1": 0, "rel2": 1, "ten1": 0, "ten2": 1}
LN_EPS = 1e-5


def gnn_kernel(nc, x, src, dst, vec3, ea48t, ea8, etype, eweight, w1t, b1, w2t, b2, relw1, relb1, relw2, relb2,
               fc0w1, fc0b1, fc0w2, fc1w1, fc1b1, fc1w2, bn0gs, bn0bs, bn0gv, bn1gs, bn1bs, edgew, edgeb, out):
    f32, i32, bf16 = mybir.dt.float32, mybir.dt.int32, mybir.dt.bfloat16
    ALU, ACT, X = mybir.AluOpType, mybir.ActivationFunctionType, mybir.AxisListType.X

    ctx = ExitStack()
    with ctx:
        def sb(name, shape, dt=f32):
            return ctx.enter_context(nc.sbuf_tensor(name, shape, dt))

        def sem(name):
            return ctx.enter_context(nc.semaphore(name))

        tab = {"gcn1": (NODES, F), "gcn2": (NODES, F), "rel1": (NODES * REL, F),
               "rel2": (NODES * REL, F), "ten1": (NODES, F), "ten2": (NODES, MSG2), "edge": (NODES, T3)}
        tab = {k: nc.dram_tensor(f"table_{k}", s, f32, kind="Internal").ap() for k, s in tab.items()}

        hidden_of = [nc.dram_tensor(f"hidden_{n}", (2 * D48, GROUPS * HALF), f32, kind="Internal").ap()
                     for n in range(2)]

        meta = sb("meta", [EP, TILES, NM])
        index = sb("index", [EP, 3, TILES], i32)
        ring_meta = sb("ring_meta", [EP, 2, G, NM])
        ring_index = sb("ring_index", [EP, 2, G], i32)
        ring_ea8 = sb("ring_ea8", [EP, 2, G, ND8])
        shared = sb("shared", [EP, 2, max(HALF + P, LOOKUPS * P)])
        ring_ea48 = shared[0:2 * D48, :, 0:HALF]
        distance = shared[:, :, 0:LOOKUPS * P].rearrange("p s (j n) -> p s j n", n=P)
        source_distance = shared[:, :, HALF:HALF + P]
        row = sb("row", [EP, 2, F])
        row_t = sb("row_t", [F, 2, EP])
        relation = sb("relation", [EP, 2])
        gathered = sb("gathered", [EP, 2, G, T3])
        onehot = sb("onehot", [EP, 2, G, P])
        onehot_b = sb("onehot_b", [EP, 2, LOOKUPS, P], bf16)
        spread = sb("spread", [EP, 2, G, HI * MSG2])
        hidden = sb("hidden", [2 * D48 + 1, 2, HALF])
        onehot_t = sb("onehot_t", [P, 2, LOOKUPS * EP], bf16)
        ring_norm = sb("ring_norm", [EP, 2, G // 2])
        hot_hi = sb("hot_hi", [EP, 2, G, HI])
        message = sb("message", [EP, 2, G, MSG2])
        prod = sb("prod", [EP, 2, G, W2])
        operand = sb("operand", [EP, 2, G, F + NV])
        vprod = sb("vprod", [EP, 2, G, 3 * NV])
        tsum = sb("tsum", [EP, 2, G, F + NV])
        xs = sb("xs", [P, HI, F])
        ya = sb("ya", [P, HI, F])
        agg = sb("agg", [P, HI, F])
        acc = sb("acc", [P, HI, MSG2])
        t1 = sb("t1", [P, HI, MSG2])
        mixed = sb("mixed", [P, HI, EDGE_COLS])
        cols = sb("cols", [P, 4, HI])
        dis = sb("dis", [P, HI])
        inv_src = sb("inv_src", [P, HI])
        inv_rel = sb("inv_rel", [P, HI * REL])
        inv_rel_parts = sb("inv_rel_parts", [P, 3, HI * REL], bf16)
        table_parts = sb("table_parts", [P, 3, HI * F], bf16)
        stat = sb("stat", [P, 6, MSG2])
        xt = sb("xt", [64, 2, P])
        ht = sb("ht", [128, 2, P])
        kw1 = sb("kw1", [KB * F, KB * HID])
        kw2 = sb("kw2", [KB * HID, KB * F])
        krel = [sb(f"krel{n}", [KB * F, KB * REL_COLS]) for n in range(2)]
        kedge = sb("kedge", [KB * F, KB * EDGE_COLS])
        wfc1 = [sb(f"wfc1_{n}", [2 * D48, 2 * D48]) for n in range(2)]
        bfc1 = [sb(f"bfc1_{n}", [2 * D48, 1]) for n in range(2)]
        wfc2 = [[sb(f"wfc2_{n}_{k}", [2 * D48 + 1, W2]) for k in range(2)] for n in range(2)]
        b1col = sb("b1col", [KB * HID, 1])
        ident = sb("ident", [EP, EP])
        ident_b = sb("ident_b", [EP, EP], bf16)
        ones = sb("ones", [EP, P])
        zeros = sb("zeros", [EP, 512])
        iota_i = sb("iota_i", [EP, 257], i32)
        iota = sb("iota", [EP, 257])
        hot_b = sb("hot_b", [EP, 2, G, HI2], bf16)
        pairs = sb("pairs", [EP, 2, G, NPAIR, 2], bf16)
        iota_b = sb("iota_b", [EP, 256], bf16)
        brow = {n: sb(f"row_{n}", [P, w]) for n, w in
                [("b2", F), ("relb1", F), ("relb2", F), ("edgeb", F), ("bn0gs", F), ("bn0bs", F), ("bn0gv", NV),
                 ("bn1gs", F), ("bn1bs", F)]}

        work = spread[:, :, :, :].rearrange("p s g c -> p (s g c)")
        wi = work.bitcast(i32)
        counted = spread[:, :, :, :].rearrange("p s g c -> p (s g c)").bitcast(bf16).rearrange(
            "p (s g c) -> p s g c", s=2, g=G)
        src_i, dst_i = index[:, IX_SRC, :], index[:, IX_DST, :]
        w_low = wi[:, 0:TILES].bitcast(bf16)[:, 0:TILES]
        w_rest = work[:, TILES:2 * TILES]
        type_i = wi[:, 2 * TILES:3 * TILES]
        f_a, f_b, f_c, f_d = (work[:, n * TILES:(n + 1) * TILES] for n in range(3, 7))
        i_a = wi[:, 7 * TILES:8 * TILES]
        v_in = work[:, 8 * TILES:11 * TILES].rearrange("p (t c) -> p t c", c=3)
        w_in = work[:, 11 * TILES:12 * TILES]
        edge_i, no_edge = wi[:, 12 * TILES:13 * TILES], work[:, 13 * TILES:14 * TILES]

        ps_acc = ctx.enter_context(nc.psum_tensor("ps_acc", [128, 2, 512], f32))
        ps_w = ctx.enter_context(nc.psum_tensor("ps_w", [128, 2, 2, 512], f32))
        ps_h = ctx.enter_context(nc.psum_tensor("ps_h", [128, 2, 512], f32))

        edges_loaded = sem("edges_loaded")
        loaded = sem("loaded")
        weights_split = sem("weights_split")
        zeroed = sem("zeroed")
        meta_ready = sem("meta_ready")
        iota_made = sem("iota_made")
        vchain = sem("vchain")
        node_ready = sem("node_ready")
        table_ready = sem("table_ready")
        table_stored = sem("table_stored")
        func_asked = sem("func_asked")
        func_done = sem("func_done")
        sums_asked = sem("sums_asked")
        sums_done = sem("sums_done")
        distance_made = sem("distance_made")
        parts_ready = sem("parts_ready")
        lookup_rows = sem("lookup_rows")
        turned = sem("turned")
        turned_in = sem("turned_in")
        row_found = sem("row_found")
        row_turned = sem("row_turned")
        row_in = sem("row_in")
        projected = sem("projected")
        norms_ready = sem("norms_ready")
        norms_used = sem("norms_used")
        sums_ready = sem("sums_ready")
        block_made = sem("block_made")
        block_read = sem("block_read")
        mix_t = sem("mix_t")
        mix_ts = sem("mix_ts")
        mix_o = sem("mix_o")
        mix_os = sem("mix_os")
        gcn_h = sem("gcn_h")
        gcn_hs = sem("gcn_hs")
        acc_read = sem("acc_read")
        out_ready = sem("out_ready")
        pool_begun = sem("pool_begun")
        out_stored = sem("out_stored")

        class PassSems:

            def __init__(self, name, kind):
                self.meta_dmas = 2 if kind == "edge" else 1
                self.meta_in = [sem(f"{name}_meta_in{s}") for s in range(2)]
                if kind != "count":
                    self.index_in = [sem(f"{name}_index_in{s}") for s in range(2)]
                    self.index_used = sem(f"{name}_index_used")
                    self.gather_in = [sem(f"{name}_gather_in{s}") for s in range(2)]
                    self.rows_used = sem(f"{name}_rows_used")
                self.inputs_used = sem(f"{name}_inputs_used")
                self.onehot_ready = sem(f"{name}_onehot_ready")
                self.spread_ready = sem(f"{name}_spread_ready")
                self.spread_used = sem(f"{name}_spread_used")
                if kind == "scale":
                    self.ea48_in = [sem(f"{name}_ea48_in{s}") for s in range(2)]
                    self.hidden_done = sem(f"{name}_hidden_done")
                    self.hidden_ready = sem(f"{name}_hidden_ready")
                    self.hidden_stored = [sem(f"{name}_hidden_stored{s}") for s in range(2)]
                if kind in ("tensor1", "tensor2"):
                    self.hidden_in = [sem(f"{name}_hidden_in{s}") for s in range(2)]
                    self.hidden_used = sem(f"{name}_hidden_used")
                    self.weights_ready = sem(f"{name}_weights_ready")
                    self.weights_used = sem(f"{name}_weights_used")

        sems = {name: PassSems(name, kind) for name, kind, *_ in PASSES}
        N_LOADS = 1 + 2 + 1 + len(brow) + 2 * 2 * 3 + KB * 5
        EDGE_LOADS = ((src_i, src), (dst_i, dst), (w_in, eweight), (type_i, etype), (v_in, vec3))
        WEIGHT_STEPS = 10
        VECTOR_TABLES = ["gcn1", "gcn2", "ten1", "ten2"]

        block = ctx.enter_context(nc.Block())

        @block.sync
        def _(sp):
            def load(to, of):
                sp.dma_start(to, of).then_inc(loaded, 16)

            for to, of in EDGE_LOADS:
                sp.dma_start(to, of).then_inc(edges_loaded, 16)
            load(xs[:, :, :], x)
            load(bfc1[0][:, :], fc0b1)
            load(bfc1[1][:, :], fc1b1)
            load(b1col[:, :], b1)
            for name, row in (("b2", b2), ("relb1", relb1), ("relb2", relb2), ("edgeb", edgeb), ("bn0gs", bn0gs),
                              ("bn0bs", bn0bs), ("bn0gv", bn0gv), ("bn1gs", bn1gs), ("bn1bs", bn1bs)):
                load(brow[name][:, :], row.partition_broadcast(P))
            sp.wait_ge(zeroed, 1)
            for n, (a, c) in enumerate(((fc0w1, fc0w2), (fc1w1, fc1w2))):
                for k in range(2):
                    load(wfc1[n][k * D48:(k + 1) * D48, k * D48:(k + 1) * D48], a)
                    load(wfc2[n][k][k * D48:(k + 1) * D48, :], c[0:D48, :])
                    load(wfc2[n][k][2 * D48:2 * D48 + 1, :], c[D48:D48 + 1, :])
            for k in range(KB):
                load(kw1[k * F:(k + 1) * F, k * HID:(k + 1) * HID], w1t)
                load(kw2[k * HID:(k + 1) * HID, k * F:(k + 1) * F], w2t)
                load(krel[0][k * F:(k + 1) * F, k * REL_COLS:(k + 1) * REL_COLS], relw1)
                load(krel[1][k * F:(k + 1) * F, k * REL_COLS:(k + 1) * REL_COLS], relw2)
                load(kedge[k * F:(k + 1) * F, k * EDGE_COLS:(k + 1) * EDGE_COLS], edgew)

            def store(name, of):
                sp.wait_ge(table_ready, VECTOR_TABLES.index(name) + 1)
                sp.dma_start(tab[name].rearrange("(p h) c -> p h c", p=P), of).then_inc(table_stored, 16)

            def store_blocks(name, rows_per_node):
                to = tab[name].rearrange("(p h r) c -> p h (r c)", p=P, r=rows_per_node)
                for n, (h0, hn) in enumerate(KGROUPS):
                    sp.wait_ge(mix_os, len(KGROUPS) * (1 + MIXES.index(name)) + n + 1)
                    sp.dma_start(to[:, h0:h0 + hn, :], mixed[:, h0:h0 + hn, 0:to.shape[2]]).then_inc(table_stored, 16)

            for name, kind, ix, gcols, mcols, side in PASSES:
                q = sems[name]
                if name == "gcn1":
                    store("gcn1", ya[:, :, :])
                elif name == "gcn2":
                    store("gcn2", ya[:, :, :])
                elif name in ("rel1", "rel2"):
                    store_blocks(name, REL)
                elif name == "ten1":
                    store("ten1", xs[:, :, :])
                elif name == "ten2":
                    store("ten2", acc[:, :, :])
                elif name == "edge":
                    store_blocks("edge", 1)
                if name == "count":
                    sp.wait_ge(meta_ready, 1)
                if name == "ten1":
                    for before in ("rel1", "rel2"):
                        for s in range(2):
                            sp.wait_ge(sems[before].hidden_stored[s], 16 * (STEPS + 1))
                with sp.Fori(0, STEPS) as i:
                    for s in range(2):
                        at = i * (2 * G) + s * G
                        if ix is not None:
                            sp.wait_ge(q.rows_used, 2 * i + s + 1)
                            sp.wait_ge(q.index_used, 2 * i + s + 1)
                            sp.dma_start(ring_index[:, s, :], index[:, ix, bass.ds(at, G)]).then_inc(q.index_in[s], 16)
                        wide = bass.ds(i * (2 * HALF) + s * HALF, HALF)
                        if kind == "scale":
                            sp.wait_ge(q.hidden_done, 2 * i + s + 1)
                            sp.dma_start(ring_ea48[:, s, :], ea48t[:, wide]).then_inc(q.ea48_in[s], 16)
                        if kind in ("tensor1", "tensor2"):
                            sp.wait_ge(q.hidden_used, 2 * i + s + 1)
                            sp.dma_start(hidden[0:2 * D48, s, :],
                                         hidden_of[TENSOR_OF[name]][:, wide]).then_inc(q.hidden_in[s], 16)
                        sp.wait_ge(q.inputs_used, 2 * i + s + 1)
                        sp.wait_ge(q.onehot_ready, 2 * i + s + 1)
                        if kind == "edge":
                            sp.dma_start(ring_ea8[:, s, :, :], ea8[:, bass.ds(at, G), :]).then_inc(q.meta_in[s], 16)
                        sp.dma_start(ring_meta[:, s, :, :], meta[:, bass.ds(at, G), :]).then_inc(q.meta_in[s], 16)
                sp.wait_ge(q.inputs_used, GROUPS + 2)
                sp.wait_ge(q.onehot_ready, GROUPS + 2)
                if ix is not None:
                    sp.wait_ge(q.rows_used, GROUPS + 2)
                    sp.wait_ge(q.index_used, GROUPS + 2)
            sp.wait_ge(out_ready, 1)
            sp.dma_start(out, xs[:, :, :]).then_inc(out_stored, 16)
            sp.wait_ge(out_stored, 16)

        @block.gpsimd
        def _(pool):
            nc.gpsimd.iota(iota_i[:, 0:256], [[1, 256]], base=0, channel_multiplier=0)
            nc.gpsimd.iota(iota_i[:, 256:257], [[1, 1]], base=0, channel_multiplier=1)
            nc.gpsimd.iota(edge_i, [[1, TILES]], base=0, channel_multiplier=TILES).then_inc(iota_made, 1)
            pool.wait_ge(edges_loaded, 16 * len(EDGE_LOADS))
            n = [0]

            def step(ins):
                n[0] += 1
                ins.then_inc(weights_split, 1)
                pool.wait_ge(weights_split, n[0])

            rest = w_in
            for part in (WEIGHT1, WEIGHT2, WEIGHT3):
                step(nc.gpsimd.tensor_copy(w_low, rest))
                step(nc.gpsimd.tensor_copy(meta[:, :, part], w_low))
                if part != WEIGHT3:
                    step(nc.gpsimd.tensor_tensor(w_rest, rest, meta[:, :, part], ALU.subtract))
                    rest = w_rest
            step(nc.gpsimd.tensor_copy(meta[:, :, WEIGHT], w_in))
            step(nc.gpsimd.memset(meta[:, :, NORM], 0.0))
            assert n[0] == WEIGHT_STEPS
            n_stores = 0
            for name, kind, ix, gcols, mcols, side in PASSES:
                if ix is None:
                    continue
                q = sems[name]
                pool.sem_inc(q.index_used, 2)
                n_stores += 1 if name in VECTOR_TABLES else len(KGROUPS)
                pool.wait_ge(table_stored, 16 * n_stores)
                with pool.Fori(0, STEPS) as i:
                    for s in range(2):
                        pool.wait_ge(q.index_in[s], 16 * (i + 1))
                        pool.sem_inc(pool_begun, 1)
                        for j in range(LOOKUP_TILE + 1 if name in LOOKUP_PASSES else 0, G):
                            pool.indirect_dma_start(
                                gathered[:, s, j, 0:gcols], None, tab[name],
                                bass.IndirectOffsetOnAxis(ap=ring_index[:, s, j:j + 1], axis=0),
                                engine_sem=q.index_used if j == G - 1 else None,
                            ).then_inc(q.gather_in[s], 16)

        @block.scalar
        def _(act):
            def func(name, to, of, fn, **kw):
                n = FUNCS.index(name)
                act.wait_ge(func_asked, n + 1)
                nc.scalar.activation(to, of, fn, **kw).then_inc(func_done, 1)

            def transposed_block(base, n):
                act.wait_ge(mix_t, base + n + 1)
                rows = KGROUPS[n][1] * F
                nc.scalar.copy(xt[0:rows, n % 2, :], ps_h[0:rows, n % 2, 0:P]).then_inc(mix_ts, 1)

            def mix(name, width):
                base = len(KGROUPS) * (1 + MIXES.index(name))
                for step in range(len(KGROUPS) + 1):
                    if step < len(KGROUPS):
                        transposed_block(base, step)
                    if step:
                        n = step - 1
                        h0, hn = KGROUPS[n]
                        act.wait_ge(mix_o, base + n + 1)
                        halves = 2 if hn == KB else 1
                        per = hn // halves
                        for u in range(halves):
                            last = nc.scalar.copy(
                                mixed[:, h0 + u * per:h0 + (u + 1) * per, 0:width],
                                ps_w[0:P, n % 2, u, 0:per * width].rearrange("p (h c) -> p h c", c=width))
                        last.then_inc(mix_os, 1)

            n_distances = [0]

            def onehots(name, i, s, side, between=None):
                q = sems[name]
                tiles = ACT_TILES if name == "count" else G
                lo = LO_S if side == "s" else LO_D
                act.wait_ge(q.meta_in[s], q.meta_dmas * 16 * (i + 1))
                act.wait_ge(q.spread_used, 2 * i + s + 1)
                for j in range(tiles):
                    last = nc.scalar.activation(onehot[:, s, j, :], iota[:, 0:P], ACT.Abs,
                                                bias=ring_meta[:, s, j, lo:lo + 1], scale=-1.0)
                last.then_inc(distance_made, 1)
                if between:
                    between()
                if name in LOOKUP_PASSES:
                    act.wait_ge(distance_made, 4 * i + 2 * s + 2 + n_distances[0])
                else:
                    act.wait_ge(distance_made, 2 * i + s + 1 + n_distances[0])
                to = counted[:, s, 0:tiles, C_ONEHOT_D:C_ONEHOT_D + P] if name == "count" else onehot[:, s, :, :]
                nc.scalar.activation(to, onehot[:, s, 0:tiles, :], ACT.Relu,
                                     bias=ones[:, 0:1], scale=-1.0).then_inc(q.onehot_ready, 1)

            func("rnorm", f_b, f_a, ACT.Sqrt)

            def onehot_pass(name, side):
                q = sems[name]
                act.sem_inc(q.onehot_ready, 2)
                with act.Fori(0, STEPS) as i:
                    for s in range(2):
                        onehots(name, i, s, side)
                n_distances[0] += GROUPS

            onehot_pass("count", "d")
            func("dis", cols[:, 2, :], cols[:, 1, :], ACT.Sqrt)

            def norm_pass(name):
                q = sems[name]
                act.sem_inc(q.onehot_ready, 2)
                k = NORM_HALF[name]
                base = GROUPS * LOOKUP_PASSES.index(name)
                with act.Fori(0, STEPS) as i:
                    for s in range(2):
                        act.wait_ge(q.meta_in[s], 16 * (i + 1))
                        for j in range(LOOKUPS):
                            lo, tile = (LO_D, k * G // 2 + j) if j < G // 2 else (LO_S, LOOKUP_TILE)
                            last = nc.scalar.activation(distance[:, s, j, :], iota[:, 0:P], ACT.Abs,
                                                        bias=ring_meta[:, s, tile, lo:lo + 1], scale=-1.0)
                        last.then_inc(distance_made, 1)
                        act.wait_ge(distance_made, 4 * i + 2 * s + 1 + n_distances[0])
                        nc.scalar.activation(onehot_b[:, s, :, :], distance[:, s, :, :], ACT.Relu,
                                             bias=ones[:, 0:1], scale=-1.0).then_inc(lookup_rows, 1)
                        act.wait_ge(turned, 2 * i + s + 1 + base)
                        nc.scalar.copy(onehot_t[:, s, :],
                                       ps_h[0:P, s, :].bitcast(bf16)[:, 0:LOOKUPS * EP]).then_inc(turned_in, 1)
                        onehots(name, i, s, "d")
                n_distances[0] += 2 * GROUPS

            act.sem_inc(turned_in, 2)
            norm_pass("gcn1")
            for step in range(len(KGROUPS) + 2):
                if step < len(KGROUPS):
                    transposed_block(0, step)
                if 1 <= step <= len(KGROUPS):
                    n = step - 1
                    rows = KGROUPS[n][1] * HID
                    act.wait_ge(gcn_h, n + 1)
                    nc.scalar.activation(ht[0:rows, n % 2, :], ps_w[0:rows, n % 2, 0, 0:P], ACT.Relu,
                                         bias=b1col[0:rows, 0:1]).then_inc(gcn_hs, 1)
                if step >= 2:
                    n = step - 2
                    h0, hn = KGROUPS[n]
                    act.wait_ge(mix_o, n + 1)
                    nc.scalar.copy(t1[:, h0:h0 + hn, 0:F],
                                   ps_w[0:P, n % 2, 1, 0:hn * F].rearrange("p (h c) -> p h c", c=F)).then_inc(mix_os, 1)
            norm_pass("gcn2")
            func("ln0", cols[:, 2, :], cols[:, 1, :], ACT.Sqrt)

            def relational_pass(name):
                q, n = sems[name], TENSOR_OF[name]
                base = GROUPS * LOOKUP_PASSES.index(name)
                first = GROUPS * TENSOR_OF[name]
                act.sem_inc(q.onehot_ready, 2)
                act.sem_inc(q.hidden_ready, 2)
                for s in range(2):
                    act.sem_inc(q.hidden_stored[s], 16)
                with act.Fori(0, STEPS) as i:
                    for s in range(2):
                        act.wait_ge(q.meta_in[s], q.meta_dmas * 16 * (i + 1))
                        nc.scalar.activation(source_distance[:, s, :], iota[:, 0:P], ACT.Abs,
                                             bias=ring_meta[:, s, LOOKUP_TILE, LO_S:LO_S + 1],
                                             scale=-1.0).then_inc(distance_made, 1)
                        act.wait_ge(distance_made, 4 * i + 2 * s + 1 + n_distances[0])
                        nc.scalar.activation(onehot_b[:, s, G // 2, :], source_distance[:, s, :], ACT.Relu,
                                             bias=ones[:, 0:1], scale=-1.0).then_inc(lookup_rows, 1)
                        act.wait_ge(turned, 2 * i + s + 1 + base)
                        nc.scalar.copy(onehot_t[:, s, G // 2 * EP:LOOKUPS * EP],
                                       ps_w[0:P, s, 0, :].bitcast(bf16)[:, 0:EP]).then_inc(turned_in, 1)
                        act.wait_ge(q.hidden_done, 2 * i + s + 1 + 2)
                        act.wait_ge(q.hidden_stored[s], 16 * (i + 1))
                        nc.scalar.activation(hidden[0:2 * D48, s, :], ps_h[0:2 * D48, s, 0:HALF],
                                             ACT.Relu, bias=bfc1[n][:, 0:1]).then_inc(q.hidden_ready, 1)

                        def row_copy():
                            act.wait_ge(row_turned, 2 * i + s + 1 + first)
                            nc.scalar.copy(row_t[:, s, :], ps_w[0:F, s, 0, ROW_AT:ROW_AT + EP]).then_inc(row_in, 1)

                        onehots(name, i, s, "d", row_copy)
                        act.wait_ge(q.hidden_ready, 2 * i + s + 1 + 2)
                        act.dma_start(hidden_of[n][:, bass.ds(i * (2 * HALF) + s * HALF, HALF)],
                                      hidden[0:2 * D48, s, :]).then_inc(q.hidden_stored[s], 16)
                n_distances[0] += 2 * GROUPS
                for s in range(2):
                    act.wait_ge(q.hidden_stored[s], 16 * (STEPS + 1))

            mix("rel1", REL_COLS)
            relational_pass("rel1")
            mix("rel2", REL_COLS)
            relational_pass("rel2")
            func("ln1_exp", t1[:, :, 0:F], acc[:, :, 0:F], ACT.Exp)
            func("ln1_log", cols[:, 2, :], cols[:, 1, :], ACT.Ln)
            func("ln1", cols[:, 2, :], cols[:, 1, :], ACT.Sqrt)
            onehot_pass("ten1", "s")
            func("bn0", stat[:, 3, 0:F], stat[:, 2, 0:F], ACT.Sqrt)
            func("bnv", stat[:, 3, 0:NV], stat[:, 2, 0:NV], ACT.Sqrt)
            onehot_pass("ten2", "s")
            func("bn1", stat[:, 3, 0:F], stat[:, 2, 0:F], ACT.Sqrt)
            func("ln2", cols[:, 2, :], cols[:, 1, :], ACT.Sqrt)
            mix("edge", EDGE_COLS)
            onehot_pass("edge", "d")
            func("ln3", cols[:, 2, :], cols[:, 1, :], ACT.Sqrt)

        @block.tensor
        def _(pe):
            def scatter_part(s, tiles, per, banks):
                for j in tiles:
                    for b in range(banks):
                        last = nc.tensor.matmul(ps_acc[0:P, b, 0:per], onehot[:, s, j, :],
                                                spread[:, s, j, b * per:(b + 1) * per],
                                                start=False, stop=False, skip_group_check=True)
                return last

            def open_sums(per, banks):
                for b in range(banks):
                    last = nc.tensor.matmul(ps_acc[0:P, b, 0:per], zeros[:, 0:P], zeros[:, 0:per],
                                            start=True, stop=False, skip_group_check=True)
                return last

            def close_sums(per, banks):
                for b in range(banks):
                    last = nc.tensor.matmul(ps_acc[0:P, b, 0:per], zeros[:, 0:P], zeros[:, 0:per],
                                            start=False, stop=True, skip_group_check=True)
                return last

            def transpose_block(source, n):
                h0, hn = KGROUPS[n]
                nc.tensor.transpose(ps_h[0:hn * F, n % 2, 0:P], source[:, h0:h0 + hn, :].rearrange("p h c -> p (h c)"),
                                    ident[0:P, 0:P]).then_inc(mix_t, 1)

            def mix(name, weights, width):
                base = len(KGROUPS) * (1 + MIXES.index(name))
                source = {"rel1": xs, "rel2": ya, "edge": xs}[name]
                pe.wait_ge(node_ready, 2 + MIXES.index(name))
                transpose_block(source, 0)
                for n, (h0, hn) in enumerate(KGROUPS):
                    if n + 1 < len(KGROUPS):
                        transpose_block(source, n + 1)
                    pe.wait_ge(mix_ts, base + n + 1)
                    if n >= 2:
                        pe.wait_ge(mix_os, base + n - 1)
                    halves = 2 if hn == KB else 1
                    per = hn // halves * width
                    for u in range(halves):
                        last = nc.tensor.matmul(ps_w[0:P, n % 2, u, 0:per], xt[0:hn * F, n % 2, :],
                                                weights[0:hn * F, u * per:(u + 1) * per], start=True, stop=True)
                    last.then_inc(mix_o, 1)

            def sum_over_partitions(n, width):
                pe.wait_ge(sums_asked, n + 1)
                nc.tensor.matmul(ps_h[0:P, 0, 0:width], ones[0:P, :], stat[:, 0, 0:width],
                                 start=True, stop=True).then_inc(sums_done, 1)

            pe.wait_ge(zeroed, 1)
            passes = 0
            for name, kind, ix, gcols, mcols, side in PASSES:
                q = sems[name]
                if passes:
                    pe.wait_ge(acc_read, passes)
                passes += 1
                banks = 2 if kind == "tensor1" else 1
                per = {"count": REL * HI + 3 * HI2, "tensor1": HI * MSG2 // 2}.get(kind, HI * F)
                if name == "rel1":
                    mix("rel1", krel[0], REL_COLS)
                if name == "rel2":
                    mix("rel2", krel[1], REL_COLS)
                if name == "edge":
                    mix("edge", kedge, EDGE_COLS)
                if kind == "count":
                    zb = zeros[:, :].bitcast(bf16)

                    def count_edge(start):
                        nc.tensor.matmul(ps_acc[0:P, 0, 0:per], zb[:, 0:P], zb[:, 0:per], start=start,
                                         stop=not start, skip_group_check=True)
                        return nc.tensor.matmul(ps_acc[0:P, 1, 0:SRC_COLS], zb[:, 0:P], zb[:, 0:SRC_COLS],
                                                start=start, stop=not start, skip_group_check=True)

                    count_edge(True).then_inc(q.spread_used, 2)
                    with pe.Fori(0, STEPS) as i:
                        for s in range(2):
                            pe.wait_ge(q.onehot_ready, 2 * i + s + 1 + 2)
                            pe.wait_ge(q.spread_ready, 4 * i + 2 * s + 2 + 4)
                            for j in range(G):
                                t = counted[:, s, j, :]
                                nc.tensor.matmul(ps_acc[0:P, 0, 0:per], t[:, C_ONEHOT_D:C_ONEHOT_D + P],
                                                 t[:, C_REL:C_REL + per], start=False, stop=False,
                                                 skip_group_check=True)
                                last = nc.tensor.matmul(ps_acc[0:P, 1, 0:SRC_COLS], t[:, C_ONEHOT_S:C_ONEHOT_S + P],
                                                        t[:, C_SRC:C_SRC + SRC_COLS], start=False, stop=False,
                                                        skip_group_check=True)
                            last.then_inc(q.spread_used, 1)
                    count_edge(False).then_inc(sums_ready, 1)
                elif kind in ("scale", "edge", "scale_norm"):
                    norms = kind == "scale_norm"
                    looked = name in LOOKUP_PASSES
                    base = GROUPS * LOOKUP_PASSES.index(name) if looked else None
                    first = GROUPS * TENSOR_OF[name] if kind == "scale" else None

                    def turn_part(i, s):
                        pe.wait_ge(lookup_rows, 2 * i + s + 1 + base)
                        pe.wait_ge(turned_in, 2 * i + s + 1 + base)
                        to = (ps_h[0:P, s, :] if norms else ps_w[0:P, s, 0, :]).bitcast(bf16)
                        for j in range(LOOKUPS if norms else 1):
                            rows = onehot_b[:, s, j if norms else G // 2, :]
                            last = nc.tensor.transpose(to[:, j * EP:(j + 1) * EP], rows, ident_b[:, :])
                        last.then_inc(turned, 1)

                    def row_part(i, s):
                        pe.wait_ge(row_found, 2 * i + s + 1 + first)
                        nc.tensor.transpose(ps_w[0:F, s, 0, ROW_AT:ROW_AT + EP], row[:, s, :],
                                            ident[:, :]).then_inc(row_turned, 1)

                    def project_part(i, s):
                        pe.wait_ge(row_in, 2 * i + s + 1 + first)
                        nc.tensor.matmul(ps_w[0:EP, s, 1, 0:REL * F], row_t[:, s, :],
                                         krel[TENSOR_OF[name]][0:F, 0:REL * F],
                                         start=True, stop=True).then_inc(projected, 1)

                    def lookup_part(i, s):
                        pe.wait_ge(turned_in, 2 * i + s + 1 + 2 + base)
                        pe.wait_ge(block_read, 2 * i + s + 1 + base)
                        for part in range(3):
                            last = nc.tensor.matmul(ps_acc[0:EP, 1, 0:HI * F], onehot_t[:, s, G // 2 * EP:LOOKUPS * EP],
                                                    table_parts[:, part, :], start=part == 0, stop=part == 2)
                        last.then_inc(block_made, 1)

                    def norm_part(i, s):
                        pe.wait_ge(norms_used, 2 * i + s + 1 + base)
                        for j in range(G // 2):
                            for part in range(3):
                                last = nc.tensor.matmul(
                                    ps_w[0:EP, s, j // 2, (j % 2) * 256:(j % 2) * 256 + REL * HI],
                                    onehot_t[:, s, j * EP:(j + 1) * EP], inv_rel_parts[:, part, :],
                                    start=part == 0, stop=part == 2)
                        last.then_inc(norms_ready, 1)

                    def hidden_part(i, s):
                        pe.wait_ge(q.ea48_in[s], 16 * (i + 1))
                        pe.wait_ge(q.hidden_ready, 2 * i + s + 1)
                        nc.tensor.matmul(ps_h[0:2 * D48, s, 0:HALF], wfc1[TENSOR_OF[name]][:, :], ring_ea48[:, s, :],
                                         start=True, stop=True).then_inc(q.hidden_done, 1)

                    def sums_part(i, s, tiles):
                        half = tiles[0] // (G // 2)
                        pe.wait_ge(q.onehot_ready, 2 * i + s + 1 + 2)
                        pe.wait_ge(q.spread_ready, 4 * i + 2 * s + half + 1 + 4)
                        last = scatter_part(s, tiles, per, 1)
                        if tiles[-1] == G - 1:
                            last.then_inc(q.spread_used, 1)

                    open_sums(per, 1).then_inc(q.spread_used, 2)
                    if kind == "scale":
                        pe.sem_inc(q.hidden_done, 2)
                        pe.wait_ge(mix_os, len(KGROUPS) * (2 + MIXES.index(name)))
                    if looked:
                        pe.wait_ge(parts_ready, 1 + LOOKUP_PASSES.index(name))

                    def ahead(i, s, part):
                        if part == 0:
                            turn_part(i, s)
                            if not norms:
                                hidden_part(i, s)
                                lookup_part(i, s)
                        elif part == 1 and not norms:
                            row_part(i, s)
                        elif part == 2 and norms:
                            lookup_part(i, s)
                        elif part == 3 and not norms:
                            project_part(i, s)
                        elif part == 4 and norms:
                            norm_part(i, s)

                    def group(i, s, nxt):
                        for part, tiles in enumerate(SUM_PARTS):
                            if nxt and looked:
                                ahead(*nxt, part)
                            sums_part(i, s, tiles)
                        if nxt and looked:
                            ahead(*nxt, len(SUM_PARTS))

                    if looked:
                        for part in range(len(SUM_PARTS) + 1):
                            ahead(0, 0, part)
                    with pe.Fori(0, STEPS - 1) as i:
                        group(i, 0, (i, 1))
                        group(i, 1, (i + 1, 0))
                    group(STEPS - 1, 0, (STEPS - 1, 1))
                    group(STEPS - 1, 1, None)
                    close_sums(per, 1).then_inc(sums_ready, 1)
                    if kind == "scale":
                        pe.wait_ge(q.hidden_ready, GROUPS + 2)
                else:
                    n = TENSOR_OF[name]

                    def weights_part(i, s, k):
                        pe.wait_ge(q.hidden_in[s], 16 * (i + 1))
                        for u in range(2):
                            pe.wait_ge(q.weights_used, 8 * i + 4 * s + 2 * k + u + 1)
                            for v in range(2):
                                j = 2 * u + v
                                last = nc.tensor.matmul(ps_w[0:EP, u, v, 0:W2], hidden[:, s, j * EP:(j + 1) * EP],
                                                        wfc2[n][k][:, :], start=True, stop=True)
                            last.then_inc(q.weights_ready, 1)

                    def hidden_released(i, s):
                        pe.wait_ge(q.weights_ready, 8 * i + 4 * s + 4)
                        pe.sem_inc(q.hidden_used, 1)

                    def sums_part(i, s, half):
                        pe.wait_ge(q.onehot_ready, 2 * i + s + 1 + 2)
                        pe.wait_ge(q.spread_ready, 4 * i + 2 * s + half + 1 + 4)
                        return scatter_part(s, HALVES[half], per, banks)

                    pe.sem_inc(q.hidden_used, 2)
                    open_sums(per, banks).then_inc(q.spread_used, 2)
                    weights_part(0, 0, 0)
                    weights_part(0, 0, 1)
                    weights_part(0, 1, 0)
                    hidden_released(0, 0)
                    with pe.Fori(0, STEPS - 1) as i:
                        for s in range(2):
                            nxt = (i, 1) if s == 0 else (i + 1, 0)
                            weights_part(*nxt, 1)
                            sums_part(i, s, 0)
                            weights_part(i + 1, s, 0)
                            hidden_released(*nxt)
                            sums_part(i, s, 1).then_inc(q.spread_used, 1)
                    i = STEPS - 1
                    weights_part(i, 1, 1)
                    hidden_released(i, 1)
                    for s in range(2):
                        sums_part(i, s, 0)
                        sums_part(i, s, 1).then_inc(q.spread_used, 1)
                    close_sums(per, banks).then_inc(sums_ready, 1)
                if name == "gcn1":
                    pe.wait_ge(node_ready, 1)
                    for step in range(len(KGROUPS) + 2):
                        if step < len(KGROUPS):
                            transpose_block(agg, step)
                        if 1 <= step <= len(KGROUPS):
                            n = step - 1
                            hn = KGROUPS[n][1]
                            pe.wait_ge(mix_ts, n + 1)
                            nc.tensor.matmul(ps_w[0:hn * HID, n % 2, 0, 0:P], kw1[0:hn * F, 0:hn * HID],
                                             xt[0:hn * F, n % 2, :], start=True, stop=True).then_inc(gcn_h, 1)
                        if step >= 2:
                            n = step - 2
                            hn = KGROUPS[n][1]
                            pe.wait_ge(gcn_hs, n + 1)
                            if n >= 2:
                                pe.wait_ge(mix_os, n - 1)
                            nc.tensor.matmul(ps_w[0:P, n % 2, 1, 0:hn * F], ht[0:hn * HID, n % 2, :],
                                             kw2[0:hn * HID, 0:hn * F], start=True, stop=True).then_inc(mix_o, 1)
                if name == "ten1":
                    for n in range(3):
                        sum_over_partitions(n, (F, F, NV)[n])
                if name == "ten2":
                    for n in range(2):
                        sum_over_partitions(3 + n, F)

        @block.vector
        def _(dve):
            V = nc.vector
            n_chain = [0, 0]
            loop = [None, 0]

            def mark(ins):
                n_chain[0] += 1
                ins.then_inc(vchain, 1)

            def settle(but=0):
                if loop[0] is None:
                    dve.wait_ge(vchain, n_chain[0] - but)
                else:
                    dve.wait_ge(vchain, loop[0] * loop[1] + (n_chain[0] - but))

            def link(ins):
                mark(ins)
                settle()

            def bc(ap, shape):
                return ap.broadcast_to(shape)

            def rows(name, width=F):
                return bc(brow[name][:, :].unsqueeze(1), [P, HI, width])

            def func(name):
                dve.sem_inc(func_asked, 1)
                dve.wait_ge(func_done, FUNCS.index(name) + 1)

            def tt(o, a, b, op):
                link(V.tensor_tensor(o, a, b, op))

            def ts(o, a, c1, c2, op0, op1=None):
                if op1 is None:
                    link(V.tensor_scalar(o, a, c1, None, op0))
                else:
                    link(V.tensor_scalar(o, a, c1, c2, op0, op1))

            def red(o, a, op=ALU.add):
                link(V.tensor_reduce(o, a, X, op))

            def mixed_ready(name):
                dve.wait_ge(mix_os, len(KGROUPS) * (2 + MIXES.index(name)))

            def colb(c, width=F):
                return bc(c.unsqueeze(2), [P, HI, width])

            def layer_norm(name, r):
                red(cols[:, 0, :], r)
                ts(cols[:, 0, :], cols[:, 0, :], 1.0 / F, None, ALU.mult)
                tt(r, r, colb(cols[:, 0, :]), ALU.subtract)
                tt(xs[:, :, :], r, r, ALU.mult)
                red(cols[:, 1, :], xs[:, :, :])
                ts(cols[:, 1, :], cols[:, 1, :], 1.0 / F, LN_EPS, ALU.mult, ALU.add)
                func(name)
                link(V.reciprocal(cols[:, 3, :], cols[:, 2, :]))
                tt(xs[:, :, :], r, colb(cols[:, 3, :]), ALU.mult)

            n_sums = [0]

            def total(to, of):
                w = of.shape[2]
                red(stat[:, 0, 0:w], of.rearrange("p h c -> p c h"))
                dve.sem_inc(sums_asked, 1)
                n_sums[0] += 1
                dve.wait_ge(sums_done, n_sums[0])
                link(V.tensor_copy(to, ps_h[0:P, 0, 0:w]))

            def batch_norm(name, r, scale, shift):
                sq = t1[:, :, 0:F]
                total(stat[:, 1, 0:F], r)
                ts(stat[:, 1, 0:F], stat[:, 1, 0:F], 1.0 / NODES, None, ALU.mult)
                tt(r, r, bc(stat[:, 1, 0:F].unsqueeze(1), [P, HI, F]), ALU.subtract)
                tt(sq, r, r, ALU.mult)
                total(stat[:, 2, 0:F], sq)
                ts(stat[:, 2, 0:F], stat[:, 2, 0:F], 1.0 / NODES, LN_EPS, ALU.mult, ALU.add)
                func(name)
                link(V.reciprocal(stat[:, 4, 0:F], stat[:, 3, 0:F]))
                tt(stat[:, 4, 0:F], stat[:, 4, 0:F], brow[scale][:, :], ALU.mult)
                tt(r, r, bc(stat[:, 4, 0:F].unsqueeze(1), [P, HI, F]), ALU.mult)
                tt(r, r, rows(shift), ALU.add)

            for t in (kw1, kw2, krel[0], krel[1], kedge, *wfc1, *wfc2[0], *wfc2[1]):
                V.memset(t[:, :], 0.0)
            V.memset(zeros[:, :], 0.0)
            V.memset(ones[:, :], 1.0)
            link(V.memset(hidden[:, :, :], 1.0))
            dve.sem_inc(zeroed, 1)
            dve.wait_ge(iota_made, 1)
            link(V.tensor_copy(iota[:, 0:257], iota_i[:, 0:257]))
            link(V.tensor_copy(iota_b[:, :], iota[:, 0:256]))
            row_id = iota[:, 256:257]
            ts(ident[:, :], iota[:, 0:EP], row_id, None, ALU.is_equal)
            link(V.tensor_copy(ident_b[:, :], ident[:, :]))
            link(V.tensor_copy(no_edge, edge_i))
            ts(no_edge, no_edge, float(EDGES), float(NO_NODE), ALU.is_ge, ALU.mult)
            dve.wait_ge(edges_loaded, 16 * len(EDGE_LOADS))

            def split(raw, lo, hi):
                link(V.tensor_copy(f_a, raw))
                ts(i_a, f_a, 1.0 / HI, None, ALU.mult)
                link(V.tensor_copy(f_b, i_a))
                link(V.scalar_tensor_tensor(f_c, f_b, -float(HI), f_a, ALU.mult, ALU.add))
                ts(f_d, f_c, 0.0, None, ALU.is_lt)
                tt(f_b, f_b, f_d, ALU.subtract)
                link(V.scalar_tensor_tensor(f_c, f_d, float(HI), f_c, ALU.mult, ALU.add))
                ts(f_d, f_c, float(HI), None, ALU.is_ge)
                tt(meta[:, :, lo], f_b, f_d, ALU.add)
                link(V.scalar_tensor_tensor(f_c, f_d, -float(HI), f_c, ALU.mult, ALU.add))
                tt(meta[:, :, hi], f_c, no_edge, ALU.add)

            split(src_i, LO_S, HI_S)
            link(V.tensor_copy(f_b, type_i))
            link(V.scalar_tensor_tensor(index[:, IX_SRCREL, :], f_a, float(REL), f_b, ALU.mult, ALU.add))
            split(dst_i, LO_D, HI_D)
            link(V.tensor_copy(f_b, type_i))
            link(V.scalar_tensor_tensor(meta[:, :, HITYPE], meta[:, :, HI_D], float(REL), f_b, ALU.mult, ALU.add))
            tt(meta[:, :, RX:RZ + 1], v_in, v_in, ALU.mult)
            red(f_a, meta[:, :, RX:RZ + 1])
            func("rnorm")
            ts(f_b, f_b, 1e-12, None, ALU.add)
            link(V.reciprocal(f_c, f_b))
            tt(meta[:, :, RX:RZ + 1], v_in, bc(f_c.unsqueeze(2), [EP, TILES, 3]), ALU.mult)
            dve.wait_ge(weights_split, WEIGHT_STEPS)
            dve.wait_ge(loaded, 16 * N_LOADS)
            dve.sem_inc(meta_ready, 1)

            def hot(o, m, width):
                n = o.shape[1]
                return V.tensor_tensor(o, bc(iota[:, 0:width].unsqueeze(1), [EP, n, width]),
                                       bc(m.unsqueeze(2), [EP, n, width]), ALU.is_equal)

            def by_pairs(o, a, b, op):
                shape = [EP, o.shape[1], o.shape[2] // 2, 2]
                return V.tensor_tensor(o.rearrange("p g (n two) -> p g n two", two=2),
                                       a.rearrange("p g (n two) -> p g n two", two=2).broadcast_to(shape),
                                       bc(b.unsqueeze(2), shape), op)

            def flat(a):
                return a[:, :, :].rearrange("p h c -> p (h c)")

            def three_parts(parts, of, rest):
                link(V.tensor_copy(parts[:, 0, :], of))
                tt(rest, of, parts[:, 0, :], ALU.subtract)
                link(V.tensor_copy(parts[:, 1, :], rest))
                tt(rest, rest, parts[:, 1, :], ALU.subtract)
                link(V.tensor_copy(parts[:, 2, :], rest))

            LINKS = {"count": 2 * 2, "scale_norm": 2 * 4, "scale": 2 * 5, "edge": 2 * 4, "tensor1": 4 * 3,
                     "tensor2": 4 * 4}
            for passes, (name, kind, ix, gcols, mcols, side) in enumerate(PASSES, 1):
                q = sems[name]
                if kind != "count":
                    dve.sem_inc(q.rows_used, 2)
                dve.sem_inc(q.inputs_used, 2)
                if name == "gcn1":
                    dve.sem_inc(block_read, 1)
                    dve.sem_inc(norms_used, 2)
                if kind == "count":
                    link(V.memset(counted[:, :, :, C_SRC:C_SRC + SRC_COLS], 0.0))
                if kind in ("tensor1", "tensor2"):
                    dve.sem_inc(q.weights_used, 2)
                dve.sem_inc(q.spread_ready, 4)
                side_hi = HI_S if side == "s" else HI_D
                banks = 2 if kind == "tensor1" else 1
                w = mcols // banks
                tensor = kind in ("tensor1", "tensor2")
                nj, ni = (F + NV, F) if kind == "tensor1" else (F, F + NV)

                def expand(i, s, half):
                    if half == 0:
                        dve.wait_ge(q.spread_used, 2 * i + s + 1)
                    t = slice(half * G // 2, (half + 1) * G // 2)
                    for b in range(banks):
                        last = V.tensor_tensor(
                            spread[:, s, t, b * HI * w:(b + 1) * HI * w].rearrange("p g (h c) -> p g h c", c=w),
                            bc(hot_hi[:, s, t, :].unsqueeze(3), [EP, G // 2, HI, w]),
                            bc(message[:, s, t, b * w:(b + 1) * w].unsqueeze(2), [EP, G // 2, HI, w]), ALU.mult)
                    last.then_inc(q.spread_ready, 1)

                def hi_parts(i, s):
                    dve.wait_ge(q.meta_in[s], q.meta_dmas * 16 * (i + 1))
                    dve.wait_ge(q.spread_ready, 4 * i + 2 * s + 2)
                    mark(hot(hot_hi[:, s, :, :], ring_meta[:, s, :, side_hi], HI))

                def operands(i, s):
                    dve.wait_ge(q.meta_in[s], 16 * (i + 1))
                    dve.wait_ge(q.gather_in[s], 16 * G * (i + 1))
                    g = gathered[:, s, :, 0:gcols]
                    V.tensor_copy(operand[:, s, :, 0:F], g[:, :, 0:F])
                    mark(V.tensor_tensor(vprod[:, s, :, :].rearrange("p g (j c) -> p g j c", c=3),
                                         g[:, :, F:MSG2].rearrange("p g (j c) -> p g j c", c=3),
                                         bc(ring_meta[:, s, :, RX:RZ + 1].unsqueeze(2), [EP, G, NV, 3]), ALU.mult))

                def add_operands(i, s):
                    dve.sem_inc(q.rows_used, 1)
                    mark(V.tensor_reduce(operand[:, s, :, F:F + NV],
                                         vprod[:, s, :, :].rearrange("p g (j c) -> p g j c", c=3), X, ALU.add))

                def multiply(i, s, k):
                    if kind == "tensor1":
                        op = gathered[:, s, :, 0:F]
                        dve.wait_ge(q.gather_in[s], 16 * G * (i + 1))
                    else:
                        op = operand[:, s, :, :]
                    for u in (2 * k, 2 * k + 1):
                        dve.wait_ge(q.weights_ready, 8 * i + 4 * s + u + 1)
                        V.tensor_tensor(
                            prod[:, s, 2 * u:2 * u + 2, :].rearrange("p g (j i) -> p g j i", i=ni),
                            ps_w[0:EP, u % 2, :, 0:W2].rearrange("p g (j i) -> p g j i", i=ni),
                            bc(op[:, 2 * u:2 * u + 2, :].unsqueeze(2), [EP, 2, nj, ni]),
                            ALU.mult).then_inc(q.weights_used, 1)

                def add_products(i, s):
                    dve.wait_ge(q.weights_used, 8 * i + 4 * s + 4 + 2)
                    if kind == "tensor1":
                        dve.sem_inc(q.rows_used, 1)
                    to = tsum if kind == "tensor1" else message
                    mark(V.tensor_reduce(to[:, s, :, 0:nj], prod[:, s, :, :].rearrange("p g (j i) -> p g j i", i=ni),
                                         X, ALU.add))

                def vectors(i, s):
                    V.tensor_copy(message[:, s, :, 0:F], tsum[:, s, :, 0:F])
                    mark(V.tensor_tensor(message[:, s, :, F:MSG2].rearrange("p g (j c) -> p g j c", c=3),
                                         bc(tsum[:, s, :, F:F + NV].unsqueeze(3), [EP, G, NV, 3]),
                                         bc(ring_meta[:, s, :, RX:RZ + 1].unsqueeze(2), [EP, G, NV, 3]), ALU.mult))

                def finish(group, behind):
                    if kind == "tensor1":
                        if group:
                            add_products(*group)
                        if behind:
                            hi_parts(*behind)
                        if group:
                            settle(1 if behind else 0)
                            vectors(*group)
                        return
                    if behind:
                        operands(*behind)
                    if group:
                        add_products(*group)
                    if behind:
                        settle(1 if group else 0)
                        add_operands(*behind)
                        hi_parts(*behind)
                        settle(1)

                def expand_half(i, s, half):
                    if half == 0:
                        settle()
                        dve.sem_inc(q.inputs_used, 1)
                    expand(i, s, half)

                base = GROUPS * LOOKUP_PASSES.index(name) if name in LOOKUP_PASSES else None
                first = GROUPS * TENSOR_OF[name] if kind == "scale" else None

                def find_row(i, s):
                    dve.wait_ge(q.meta_in[s], q.meta_dmas * 16 * (i + 1))
                    dve.wait_ge(block_made, 2 * i + s + 1 + base)
                    block = prod[:, s, G // 2:G, :].rearrange("p g c -> p (g c)")[:, 0:HI * F]
                    block = block.rearrange("p (h c) -> p h c", c=F)
                    V.scalar_tensor_tensor(
                        block, bc(iota[:, 0:HI].unsqueeze(2), [EP, HI, F]), ring_meta[:, s, LOOKUP_TILE, HI_S:HI_S + 1],
                        ps_acc[0:EP, 1, 0:HI * F].rearrange("p (h c) -> p h c", c=F), ALU.is_equal,
                        ALU.mult).then_inc(block_read, 1)
                    dve.wait_ge(block_read, 2 * i + s + 1 + base + 1)
                    V.tensor_reduce(row[:, s, :], block.rearrange("p h c -> p c h"), X,
                                    ALU.add).then_inc(row_found, 1)

                def relational(i, s, nxt):
                    m = ring_meta[:, s, :, :]
                    mark(V.scalar_tensor_tensor(relation[:, s:s + 1], m[:, LOOKUP_TILE, HI_D:HI_D + 1], -float(REL),
                                                m[:, LOOKUP_TILE, HITYPE:HITYPE + 1], ALU.mult, ALU.add))
                    hi_parts(i, s)
                    dve.wait_ge(projected, 2 * i + s + 1 + first)
                    settle(1)
                    chosen = prod[:, s, 0, 0:REL * F].rearrange("p (r c) -> p r c", c=F)
                    mark(V.scalar_tensor_tensor(
                        chosen, bc(iota[:, 0:REL].unsqueeze(2), [EP, REL, F]), relation[:, s:s + 1],
                        ps_w[0:EP, s, 1, 0:REL * F].rearrange("p (r c) -> p r c", c=F), ALU.is_equal, ALU.mult))
                    settle()
                    mark(V.tensor_reduce(gathered[:, s, LOOKUP_TILE, 0:F], chosen.rearrange("p r c -> p c r"),
                                         X, ALU.add))
                    settle()
                    dve.wait_ge(q.gather_in[s], 16 * (G - 1) * (i + 1))
                    link(V.tensor_tensor(message[:, s, :, 0:F], gathered[:, s, :, 0:F],
                                         bc(m[:, :, NORM:NORM + 1], [EP, G, F]), ALU.mult))
                    dve.sem_inc(q.rows_used, 1)
                    dve.sem_inc(q.inputs_used, 1)
                    expand(i, s, 0)
                    if nxt:
                        find_row(*nxt)
                    expand(i, s, 1)

                if kind == "scale":
                    find_row(0, 0)
                if tensor:
                    finish(None, (0, 0))
                    multiply(0, 0, 0)
                    multiply(0, 0, 1)
                    finish((0, 0), (0, 1))
                start = n_chain[0]
                steps_per_turn = 2 if tensor else 1
                turns = (STEPS - 1 if tensor or kind == "scale" else STEPS) // steps_per_turn
                assert not tensor or turns * steps_per_turn == STEPS - 1
                with dve.Fori(0, turns) as turn:
                    loop[0], loop[1] = turn, LINKS[kind]
                    groups = [(turn * 2 + step, s) for step in range(2) for s in range(2)] if tensor else [
                        (turn, s) for s in range(2)]
                    for i, s in groups:
                        if tensor:
                            nxt = (i, 1) if s == 0 else (i + 1, 0)
                            multiply(*nxt, 0)
                            expand_half(i, s, 0)
                            multiply(*nxt, 1)
                            expand_half(i, s, 1)
                            finish(nxt, (i + 1, s))
                            continue
                        m = ring_meta[:, s, :, :]
                        if kind == "count":
                            dve.wait_ge(q.meta_in[s], 16 * (i + 1))
                            dve.wait_ge(q.spread_used, 2 * i + s + 1)
                            dve.wait_ge(q.spread_ready, 4 * i + 2 * s + 2)
                            two = pairs[:, s, :, :, :]
                            link(V.tensor_copy(two, bc(m[:, :, 0:NPAIR].unsqueeze(3), [EP, G, NPAIR, 2])))
                            dve.sem_inc(q.inputs_used, 1)
                            t = counted[:, s, :, :]
                            ids = iota_b[:, :].unsqueeze(1)
                            mark(by_pairs(hot_b[:, s, :, :], ids[:, :, 0:HI2], two[:, :, HI_D, :], ALU.is_equal))
                            by_pairs(t[:, :, C_REL:C_REL + REL * HI], ids[:, :, 0:REL * HI], two[:, :, HITYPE, :],
                                     ALU.is_equal)
                            by_pairs(t[:, :, C_ONEHOT_S:C_ONEHOT_S + P2], ids[:, :, 0:P2], two[:, :, LO_S, :],
                                     ALU.is_equal)
                            by_pairs(t[:, ACT_TILES:G, C_ONEHOT_D:C_ONEHOT_D + P2], ids[:, :, 0:P2],
                                     two[:, ACT_TILES:G, LO_D, :], ALU.is_equal)
                            by_pairs(t[:, :, C_SRC:C_SRC + HI2], ids[:, :, 0:HI2], two[:, :, HI_S, :], ALU.is_equal)
                            settle()
                            for part in range(3):
                                last = by_pairs(t[:, :, C_WEIGHT + part * HI2:C_WEIGHT + (part + 1) * HI2],
                                                hot_b[:, s, :, :], two[:, :, WEIGHT1 + part, :], ALU.mult)
                            last.then_inc(q.spread_ready, 2)
                            continue
                        if kind == "scale_norm":
                            k = NORM_HALF[name]
                            dve.wait_ge(q.meta_in[s], 16 * (i + 1))
                            dve.wait_ge(block_made, 2 * i + s + 1 + k * GROUPS)
                            block = prod[:, s, G // 2:G, :].rearrange("p g c -> p (g c)")[:, 0:HI * F]
                            block = block.rearrange("p (h c) -> p h c", c=F)
                            V.scalar_tensor_tensor(
                                block, bc(iota[:, 0:HI].unsqueeze(2), [EP, HI, F]), m[:, LOOKUP_TILE, HI_S:HI_S + 1],
                                ps_acc[0:EP, 1, 0:HI * F].rearrange("p (h c) -> p h c", c=F), ALU.is_equal,
                                ALU.mult).then_inc(block_read, 1)
                            hi_parts(i, s)
                            dve.wait_ge(block_read, 2 * i + s + 1 + k * GROUPS + 1)
                            mark(V.tensor_reduce(gathered[:, s, LOOKUP_TILE, 0:F], block.rearrange("p h c -> p c h"),
                                                 X, ALU.add))
                            settle()
                            dve.wait_ge(q.gather_in[s], 16 * (G - 1) * (i + 1))
                            link(V.tensor_tensor(message[:, s, :, 0:F], gathered[:, s, :, 0:F],
                                                 bc(m[:, :, WEIGHT:WEIGHT + 1], [EP, G, F]), ALU.mult))
                            dve.sem_inc(q.rows_used, 1)
                            expand(i, s, 0)
                            dve.wait_ge(norms_ready, 2 * i + s + 1 + k * GROUPS)
                            for j in range(G // 2):
                                last = V.scalar_tensor_tensor(
                                    prod[:, s, j, 0:REL * HI], iota[:, 0:REL * HI],
                                    m[:, k * G // 2 + j, HITYPE:HITYPE + 1],
                                    ps_w[0:EP, s, j // 2, (j % 2) * 256:(j % 2) * 256 + REL * HI],
                                    ALU.is_equal, ALU.mult, accum_out=ring_norm[:, s, j:j + 1])
                            last.then_inc(norms_used, 1)
                            expand(i, s, 1)
                            dve.wait_ge(norms_used, 2 * i + s + 1 + 2 + k * GROUPS)
                            dve.sem_inc(q.inputs_used, 1)
                            mark(V.tensor_copy(meta[:, bass.ds(i * (2 * G) + s * G + k * G // 2, G // 2), NORM],
                                               ring_norm[:, s, :]))
                            continue
                        if kind == "scale":
                            relational(i, s, (i, 1) if s == 0 else (i + 1, 0))
                            continue
                        hi_parts(i, s)
                        dve.wait_ge(q.gather_in[s], 16 * G * (i + 1))
                        g = gathered[:, s, :, 0:gcols]
                        pr = prod[:, s, :, 0:ND8 * F].rearrange("p g (k o) -> p g k o", o=F)
                        tt(pr, g[:, :, 0:ND8 * F].rearrange("p g (k o) -> p g k o", o=F),
                           bc(ring_ea8[:, s, :, :].unsqueeze(3), [EP, G, ND8, F]), ALU.mult)
                        red(tsum[:, s, :, 0:F], pr.rearrange("p g k o -> p g o k"))
                        tt(message[:, s, :, 0:F], tsum[:, s, :, 0:F], g[:, :, ND8 * F:T3], ALU.add)
                        dve.sem_inc(q.rows_used, 1)
                        dve.sem_inc(q.inputs_used, 1)
                        expand(i, s, 0)
                        expand(i, s, 1)
                    per_turn = n_chain[0] - start
                assert per_turn == LINKS[kind], (kind, per_turn)
                n_chain[0] = start + per_turn * turns
                loop[0] = None
                if tensor:
                    i = STEPS - 1
                    multiply(i, 1, 0)
                    expand_half(i, 0, 0)
                    multiply(i, 1, 1)
                    expand_half(i, 0, 1)
                    finish((i, 1), None)
                    expand_half(i, 1, 0)
                    expand_half(i, 1, 1)
                if kind == "scale":
                    relational(STEPS - 1, 0, (STEPS - 1, 1))
                    relational(STEPS - 1, 1, None)
                dve.wait_ge(sums_ready, passes)
                if kind == "count":
                    link(V.tensor_copy(inv_rel[:, :], ps_acc[0:P, 0, 0:REL * HI]))
                    weights = ps_acc[0:P, 0, C_WEIGHT:C_WEIGHT + 3 * HI2].rearrange("p (w h) -> p h w", h=HI2)
                    red(cols[:, 0, :], weights[:, 0:HI, :])
                    ts(cols[:, 0, :], cols[:, 0, :], 1.0, None, ALU.add)
                    ts(inv_src[:, :], ps_acc[0:P, 1, 0:HI], 1.0, None, ALU.max)
                    dve.sem_inc(acc_read, 1)
                    ts(inv_rel[:, :], inv_rel[:, :], 1.0, None, ALU.max)
                    link(V.reciprocal(inv_rel[:, :], inv_rel[:, :]))
                    link(V.reciprocal(inv_src[:, :], inv_src[:, :]))
                    ts(cols[:, 3, :], cols[:, 0, :], 0.0, None, ALU.is_gt)
                    ts(cols[:, 1, :], cols[:, 0, :], 1e-37, None, ALU.max)
                    func("dis")
                    link(V.reciprocal(dis[:, :], cols[:, 2, :]))
                    tt(dis[:, :], dis[:, :], cols[:, 3, :], ALU.mult)
                    tt(ya[:, :, :], xs[:, :, :], colb(dis[:, :]), ALU.mult)
                    dve.sem_inc(table_ready, 1)
                    three_parts(table_parts, flat(ya), flat(agg))
                    three_parts(inv_rel_parts, inv_rel[:, :], flat(agg)[:, 0:HI * REL])
                    dve.sem_inc(parts_ready, 1)
                    continue
                a = acc[:, :, 0:F]
                sums = ps_acc[0:P, 0, 0:HI * F].rearrange("p (h c) -> p h c", c=F)
                if name in ("gcn1", "gcn2"):
                    tt(a, sums, ya[:, :, :], ALU.add)
                    dve.sem_inc(acc_read, 1)
                    if name == "gcn1":
                        tt(agg[:, :, :], a, colb(dis[:, :]), ALU.mult)
                        dve.sem_inc(node_ready, 1)
                        dve.wait_ge(mix_os, len(KGROUPS))
                        tt(ya[:, :, :], t1[:, :, 0:F], colb(dis[:, :]), ALU.mult)
                        dve.sem_inc(table_ready, 1)
                        three_parts(table_parts, flat(ya), flat(agg))
                        dve.sem_inc(parts_ready, 1)
                    else:
                        tt(a, a, colb(dis[:, :]), ALU.mult)
                        tt(a, a, rows("b2"), ALU.add)
                        tt(a, a, xs[:, :, :], ALU.add)
                        layer_norm("ln0", a)
                        dve.sem_inc(node_ready, 1)
                        three_parts(table_parts, flat(xs), flat(agg))
                        dve.sem_inc(parts_ready, 1)
                        mixed_ready("rel1")
                elif name in ("rel1", "rel2"):
                    tt(a, sums, mixed[:, :, REL * F:REL_COLS], ALU.add)
                    dve.sem_inc(acc_read, 1)
                    tt(a, a, rows("relb1" if name == "rel1" else "relb2"), ALU.add)
                    if name == "rel1":
                        ts(ya[:, :, :], a, 0.0, None, ALU.max)
                        dve.sem_inc(node_ready, 1)
                        three_parts(table_parts, flat(ya), flat(agg))
                        dve.sem_inc(parts_ready, 1)
                        mixed_ready("rel2")
                    else:
                        red(cols[:, 0, :], a, ALU.max)
                        tt(a, a, colb(cols[:, 0, :]), ALU.subtract)
                        func("ln1_exp")
                        red(cols[:, 1, :], t1[:, :, 0:F])
                        func("ln1_log")
                        tt(a, a, colb(cols[:, 2, :]), ALU.subtract)
                        tt(a, a, xs[:, :, :], ALU.add)
                        layer_norm("ln1", a)
                        dve.sem_inc(table_ready, 1)
                elif name == "ten1":
                    h = MSG2 // 2
                    for b in range(2):
                        link(V.tensor_tensor(acc[:, :, b * h:(b + 1) * h],
                                             ps_acc[0:P, b, 0:HI * h].rearrange("p (h c) -> p h c", c=h),
                                             colb(inv_src[:, :], h), ALU.mult))
                    dve.sem_inc(acc_read, 1)
                    ts(acc[:, :, 0:F], acc[:, :, 0:F], float(1.0 / np.sqrt(F)), None, ALU.mult)
                    ts(acc[:, :, F:MSG2], acc[:, :, F:MSG2], float(np.sqrt(3.0) / np.sqrt(F)), None, ALU.mult)
                    batch_norm("bn0", a, "bn0gs", "bn0bs")
                    v = acc[:, :, F:MSG2]
                    sq = t1[:, :, F:MSG2]
                    tt(sq, v, v, ALU.mult)
                    red(t1[:, :, 0:NV], sq.rearrange("p h (j c) -> p h j c", c=3))
                    total(stat[:, 2, 0:NV], t1[:, :, 0:NV])
                    ts(stat[:, 2, 0:NV], stat[:, 2, 0:NV], 1.0 / (3 * NODES), LN_EPS, ALU.mult, ALU.add)
                    func("bnv")
                    link(V.reciprocal(stat[:, 4, 0:NV], stat[:, 3, 0:NV]))
                    tt(stat[:, 4, 0:NV], stat[:, 4, 0:NV], brow["bn0gv"][:, :], ALU.mult)
                    link(V.tensor_copy(stat[:, 5, 0:3 * NV].rearrange("p (j c) -> p j c", c=3),
                                       bc(stat[:, 4, 0:NV].unsqueeze(2), [P, NV, 3])))
                    tt(v, v, bc(stat[:, 5, 0:3 * NV].unsqueeze(1), [P, HI, 3 * NV]), ALU.mult)
                    dve.sem_inc(table_ready, 1)
                elif name == "ten2":
                    tt(a, sums, colb(inv_src[:, :]), ALU.mult)
                    dve.sem_inc(acc_read, 1)
                    ts(a, a, float(1.0 / np.sqrt(F + NV)), None, ALU.mult)
                    batch_norm("bn1", a, "bn1gs", "bn1bs")
                    tt(a, a, xs[:, :, :], ALU.add)
                    layer_norm("ln2", a)
                    dve.sem_inc(node_ready, 1)
                    mixed_ready("edge")
                else:
                    tt(a, sums, mixed[:, :, T3:EDGE_COLS], ALU.add)
                    tt(a, a, rows("edgeb"), ALU.add)
                    tt(a, a, xs[:, :, :], ALU.add)
                    layer_norm("ln3", a)
                    dve.sem_inc(out_ready, 1)


def kernel(x, src, dst, edge_attr_3, edge_attr_48, edge_attr_8, edge_type_8, edge_weight, L0_gnn_W1, L0_gnn_b1,
           L0_gnn_W2, L0_gnn_b2, L1_gnn_W1, L1_gnn_root1, L1_gnn_b1, L1_gnn_W2, L1_gnn_root2, L1_gnn_b2,
           L2_gnn_fc0_w1, L2_gnn_fc0_b1, L2_gnn_fc0_w2, L2_gnn_fc0_b2, L2_gnn_fc1_w1, L2_gnn_fc1_b1, L2_gnn_fc1_w2,
           L2_gnn_fc1_b2, L2_gnn_bn0_gs, L2_gnn_bn0_bs, L2_gnn_bn0_gv, L2_gnn_bn1_gs, L2_gnn_bn1_bs, L3_gnn_root_w,
           L3_gnn_root_b, L3_gnn_edge_w, L3_gnn_edge_b):
    import concourse.bacc as bacc
    from concourse.bass_utils import run_bass_kernel_spmd

    A = np.asarray

    def per_edge(a):
        a = A(a)
        whole = np.zeros((EP * TILES,) + a.shape[1:], a.dtype)
        whole[:EDGES] = a
        return whole.reshape((EP, TILES) + a.shape[1:])

    def relations(w, root):
        return np.concatenate([A(w).transpose(1, 0, 2).reshape(F, REL * F), A(root)], axis=1)

    def tensor_weights(w2, b2, i2, o1):
        w = np.concatenate([A(w2), A(b2)[None, :]], axis=0)
        a = w[:, :F * F].reshape(D48 + 1, F, F)
        b = w[:, F * F:].reshape(D48 + 1, i2, o1)
        both = np.concatenate([a, b], axis=2 if i2 == F else 1)
        return both.transpose(0, 2, 1).reshape(D48 + 1, W2)

    edge_i = np.concatenate([A(L3_gnn_edge_w), A(L3_gnn_edge_b)[None, :]], axis=0).reshape(ND8 + 1, F, F)
    edge_i = edge_i.transpose(2, 0, 1).reshape(F, T3)
    arrays = {
        "x": A(x).reshape(P, HI, F),
        "src": per_edge(src), "dst": per_edge(dst), "vec3": per_edge(edge_attr_3),
        "ea48t": per_edge(edge_attr_48).reshape(EP, GROUPS, 2, G // 2, D48).transpose(2, 4, 1, 3, 0).reshape(
            2 * D48, GROUPS * HALF),
        "ea8": per_edge(edge_attr_8), "etype": per_edge(edge_type_8), "eweight": per_edge(edge_weight),
        "w1t": A(L0_gnn_W1).T, "b1": np.tile(A(L0_gnn_b1), KB)[:, None], "w2t": A(L0_gnn_W2).T, "b2": A(L0_gnn_b2),
        "relw1": relations(L1_gnn_W1, L1_gnn_root1), "relb1": A(L1_gnn_b1),
        "relw2": relations(L1_gnn_W2, L1_gnn_root2), "relb2": A(L1_gnn_b2),
        "fc0w1": A(L2_gnn_fc0_w1), "fc0b1": np.tile(A(L2_gnn_fc0_b1), 2)[:, None],
        "fc0w2": tensor_weights(L2_gnn_fc0_w2, L2_gnn_fc0_b2, F, NV),
        "fc1w1": A(L2_gnn_fc1_w1), "fc1b1": np.tile(A(L2_gnn_fc1_b1), 2)[:, None],
        "fc1w2": tensor_weights(L2_gnn_fc1_w2, L2_gnn_fc1_b2, NV, F),
        "bn0gs": A(L2_gnn_bn0_gs), "bn0bs": A(L2_gnn_bn0_bs), "bn0gv": A(L2_gnn_bn0_gv),
        "bn1gs": A(L2_gnn_bn1_gs), "bn1bs": A(L2_gnn_bn1_bs),
        "edgew": np.concatenate([edge_i, A(L3_gnn_root_w)], axis=1), "edgeb": A(L3_gnn_root_b),
    }
    nc = bacc.Bacc("TRN2", target_bir_lowering=False, num_devices=1)
    arrays = {k: np.ascontiguousarray(v) for k, v in arrays.items()}
    args = [nc.dram_tensor(f"in_{k}", v.shape, mybir.dt.from_np(v.dtype), kind="ExternalInput").ap()
            for k, v in arrays.items()]
    result = nc.dram_tensor("result", (P, HI, F), mybir.dt.float32, kind="ExternalOutput").ap()
    gnn_kernel(nc, *args, result)
    r = run_bass_kernel_spmd(nc, [{f"in_{k}": v for k, v in arrays.items()}], core_ids=[0])
    return r.results[0]["result"].reshape(NODES, F)
```
